# Optimizing a Trainium2 kernel written in Bass

```python
import numpy as np
import jax
import jax.numpy as jnp

def _softmax(x, axis=-1):
    return jax.nn.softmax(x, axis=axis)

def _gelu(x):
    return jax.nn.gelu(x, approximate=True)

def _silu(x):
    return jax.nn.silu(x)

def _sigmoid(x):
    return jax.nn.sigmoid(x)

def _layernorm(x, axis=-1, eps=1e-05):
    m = jnp.mean(x, axis=axis, keepdims=True)
    v = jnp.var(x, axis=axis, keepdims=True)
    return (x - m) / jnp.sqrt(v + eps)

def _scatter_add(tgt, idx, src, axis=0):
    return tgt.at[idx].add(src)

def _segment_sum(src, seg, n):
    return jax.ops.segment_sum(src, seg, n)
kernel_name = 'mk_seq_postln_d2_jaxref_r8_a69676'

def setup_inputs(seed: int=0):
    np.random.seed(seed)
    _w = jnp.asarray

    def _L0_attn_setup():
        import jax, jax.numpy as jnp
        import numpy as np
        BATCH, SEQ, D_MODEL = (2, 512, 128)
        D_STATE, EXPAND = (64, 2)
        D_INNER = D_MODEL * EXPAND

        def _silu(v):
            return v * jax.nn.sigmoid(v)
        key = jax.random.key(seed)
        ks = jax.random.split(key, 12)
        s = 0.02
        return {'x': jax.random.normal(ks[0], (BATCH, SEQ, D_MODEL), dtype=jnp.float32), 'W_in': jax.random.normal(ks[1], (D_MODEL, 2 * D_INNER), dtype=jnp.float32) * s, 'b_in': jnp.zeros((2 * D_INNER,), dtype=jnp.float32), 'W_xp': jax.random.normal(ks[2], (D_INNER, D_STATE), dtype=jnp.float32) * s, 'b_xp': jnp.zeros((D_STATE,), dtype=jnp.float32), 'W_dt': jax.random.normal(ks[3], (D_INNER, D_MODEL), dtype=jnp.float32) * s, 'b_dt': jnp.zeros((D_MODEL,), dtype=jnp.float32), 'W_out': jax.random.normal(ks[4], (D_INNER, D_MODEL), dtype=jnp.float32) * s, 'b_out': jnp.zeros((D_MODEL,), dtype=jnp.float32), 'A_log': jax.random.normal(ks[5], (D_STATE,), dtype=jnp.float32), 'D': jax.random.normal(ks[6], (D_MODEL,), dtype=jnp.float32)}
    _L0_attn_in = _L0_attn_setup()

    def _L0_ffn_setup():
        import jax, jax.numpy as jnp
        import numpy as np
        D = 128
        H = 16
        DH = D // H
        DC = D // 4
        HID = 256
        G = 2
        EPG = 4
        E = G * EPG
        TOPK = 2
        EPS = 1e-06
        B, T = (2, 256)

        def _rope_sincos(t, dh):
            inv_freq = 1.0 / 10000.0 ** (jnp.arange(0, dh, 2, dtype=jnp.float32) / dh)
            ang = jnp.arange(t, dtype=jnp.float32)[:, None] * inv_freq[None, :]
            return (jnp.sin(ang), jnp.cos(ang))

        def _apply_rope(x, sin, cos):
            x1 = x[..., ::2]
            x2 = x[..., 1::2]
            r = jnp.stack([x1 * cos - x2 * sin, x1 * sin + x2 * cos], axis=-1)
            return r.reshape(x.shape)

        def _swiglu(x):
            a, b = jnp.split(x, 2, axis=-1)
            return jax.nn.silu(a) * b

        def _rmsnorm(x, w):
            return x * jax.lax.rsqrt(jnp.mean(x * x, axis=-1, keepdims=True) + EPS) * w
        key = jax.random.key(seed)
        ks = jax.random.split(key, 14)
        s = 0.02
        return {'src': jax.random.normal(ks[0], (B, T, D), jnp.float32), 'Wq': jax.random.normal(ks[1], (D, D), jnp.float32) * s, 'Wk_c': jax.random.normal(ks[2], (D, DC), jnp.float32) * s, 'Wv_c': jax.random.normal(ks[3], (D, DC), jnp.float32) * s, 'Wk': jax.random.normal(ks[4], (DC, D), jnp.float32) * s, 'Wv': jax.random.normal(ks[5], (DC, D), jnp.float32) * s, 'Wo': jax.random.normal(ks[6], (D, D), jnp.float32) * s, 'W_shared_in': jax.random.normal(ks[7], (D, 2 * HID), jnp.float32) * s, 'W_shared_out': jax.random.normal(ks[8], (HID, D), jnp.float32) * s, 'W1_shared': jax.random.normal(ks[9], (D, 2 * HID), jnp.float32) * s, 'W2_experts': jax.random.normal(ks[10], (E, HID, D), jnp.float32) * s, 'Wg_gate': jax.random.normal(ks[11], (D, G), jnp.float32) * s, 'We_gate': jax.random.normal(ks[12], (D, E), jnp.float32) * s, 'group_bias': jnp.zeros((G,), jnp.float32), 'expert_bias': jnp.zeros((E,), jnp.float32), 'norm1_w': jnp.ones((D,), jnp.float32), 'norm2_w': jnp.ones((D,), jnp.float32)}
    _L0_ffn_in = _L0_ffn_setup()

    def _L1_attn_setup():
        import jax, jax.numpy as jnp
        import numpy as np
        B, S, D = (2, 512, 128)
        EPS = 1e-05

        def _rmsnorm(x, gamma):
            ss = jnp.sum(jnp.square(x), axis=-1, keepdims=True)
            inv = jax.lax.rsqrt(ss + EPS)
            return inv * x * gamma * x.shape[-1] ** 0.5

        def _gate_loop_operator(kv, q, a):

            def binop(e_i, e_j):
                a_i, kv_i = e_i
                a_j, kv_j = e_j
                return (a_j * a_i, a_j * kv_i + kv_j)
            _, y = jax.lax.associative_scan(binop, (a, kv), axis=1)
            return q * y
        key = jax.random.key(seed)
        ks = jax.random.split(key, 7)
        x = jax.random.normal(ks[0], (B, S, D), dtype=jnp.float32)
        gamma = jnp.ones((D,), dtype=jnp.float32)
        wq, wk, wv, wa, wg, wo = (jax.random.normal(k, (D, D), dtype=jnp.float32) for k in ks[1:7])
        return {'x': x, 'gamma': gamma, 'wq': wq, 'wk': wk, 'wv': wv, 'wa': wa, 'wg': wg, 'wo': wo}
    _L1_attn_in = _L1_attn_setup()

    def _L1_ffn_setup():
        import jax, jax.numpy as jnp
        import numpy as np
        N_EXPERTS = 8
        CAP_FACTOR = 1.25
        BATCH, SEQ, DMODEL, DFF = (4, 256, 128, 512)
        key = jax.random.key(seed)
        k0, k1, k2, k3 = jax.random.split(key, 4)
        x = jax.random.normal(k0, (BATCH, SEQ, DMODEL), dtype=jnp.float32)
        Wr = jax.random.normal(k1, (DMODEL, N_EXPERTS), dtype=jnp.float32) * 0.02
        W1 = jax.random.normal(k2, (N_EXPERTS, DMODEL, DFF), dtype=jnp.float32) * 0.02
        W2 = jax.random.normal(k3, (N_EXPERTS, DFF, DMODEL), dtype=jnp.float32) * 0.02
        return {'x': x, 'Wr': Wr, 'W1': W1, 'W2': W2}
    _L1_ffn_in = _L1_ffn_setup()
    _d = {'L0_attn_x': _L0_attn_in['x'], 'L0_attn_W_in': _L0_attn_in['W_in'], 'L0_attn_b_in': _L0_attn_in['b_in'], 'L0_attn_W_xp': _L0_attn_in['W_xp'], 'L0_attn_b_xp': _L0_attn_in['b_xp'], 'L0_attn_W_dt': _L0_attn_in['W_dt'], 'L0_attn_b_dt': _L0_attn_in['b_dt'], 'L0_attn_W_out': _L0_attn_in['W_out'], 'L0_attn_b_out': _L0_attn_in['b_out'], 'L0_attn_A_log': _L0_attn_in['A_log'], 'L0_attn_D': _L0_attn_in['D'], 'L0_ffn_Wq': _L0_ffn_in['Wq'], 'L0_ffn_Wk_c': _L0_ffn_in['Wk_c'], 'L0_ffn_Wv_c': _L0_ffn_in['Wv_c'], 'L0_ffn_Wk': _L0_ffn_in['Wk'], 'L0_ffn_Wv': _L0_ffn_in['Wv'], 'L0_ffn_Wo': _L0_ffn_in['Wo'], 'L0_ffn_W_shared_in': _L0_ffn_in['W_shared_in'], 'L0_ffn_W_shared_out': _L0_ffn_in['W_shared_out'], 'L0_ffn_W1_shared': _L0_ffn_in['W1_shared'], 'L0_ffn_W2_experts': _L0_ffn_in['W2_experts'], 'L0_ffn_Wg_gate': _L0_ffn_in['Wg_gate'], 'L0_ffn_We_gate': _L0_ffn_in['We_gate'], 'L0_ffn_group_bias': _L0_ffn_in['group_bias'], 'L0_ffn_expert_bias': _L0_ffn_in['expert_bias'], 'L0_ffn_norm1_w': _L0_ffn_in['norm1_w'], 'L0_ffn_norm2_w': _L0_ffn_in['norm2_w'], 'L1_attn_gamma': _L1_attn_in['gamma'], 'L1_attn_wq': _L1_attn_in['wq'], 'L1_attn_wk': _L1_attn_in['wk'], 'L1_attn_wv': _L1_attn_in['wv'], 'L1_attn_wa': _L1_attn_in['wa'], 'L1_attn_wg': _L1_attn_in['wg'], 'L1_attn_wo': _L1_attn_in['wo'], 'L1_ffn_Wr': _L1_ffn_in['Wr'], 'L1_ffn_W1': _L1_ffn_in['W1'], 'L1_ffn_W2': _L1_ffn_in['W2']}
    _x0 = _d['L0_attn_x']
    _d['L0_attn_x'] = jax.random.normal(jax.random.fold_in(jax.random.key(seed), 1), (1, 2048, 128), dtype=_x0.dtype)
    del _x0
    return _d

def reference(L0_attn_x, L0_attn_W_in, L0_attn_b_in, L0_attn_W_xp, L0_attn_b_xp, L0_attn_W_dt, L0_attn_b_dt, L0_attn_W_out, L0_attn_b_out, L0_attn_A_log, L0_attn_D, L0_ffn_Wq, L0_ffn_Wk_c, L0_ffn_Wv_c, L0_ffn_Wk, L0_ffn_Wv, L0_ffn_Wo, L0_ffn_W_shared_in, L0_ffn_W_shared_out, L0_ffn_W1_shared, L0_ffn_W2_experts, L0_ffn_Wg_gate, L0_ffn_We_gate, L0_ffn_group_bias, L0_ffn_expert_bias, L0_ffn_norm1_w, L0_ffn_norm2_w, L1_attn_gamma, L1_attn_wq, L1_attn_wk, L1_attn_wv, L1_attn_wa, L1_attn_wg, L1_attn_wo, L1_ffn_Wr, L1_ffn_W1, L1_ffn_W2):

    def _L0_attn_ref(x, W_in, b_in, W_xp, b_xp, W_dt, b_dt, W_out, b_out, A_log, D):
        import jax, jax.numpy as jnp
        import numpy as np
        BATCH, SEQ, D_MODEL = (2, 512, 128)
        D_STATE, EXPAND = (64, 2)
        D_INNER = D_MODEL * EXPAND

        def _silu(v):
            return v * jax.nn.sigmoid(v)
        xr = x @ W_in + b_in
        x_inner, res = jnp.split(xr, 2, axis=-1)
        x_inner = _silu(x_inner)
        A = -jnp.exp(A_log)
        delta = jax.nn.softplus(x_inner @ W_dt + b_dt)
        mean_delta = delta.mean(axis=-1)
        a = jnp.exp(A[None, None, :] * mean_delta[..., None])
        bx = x_inner @ W_xp + b_xp

        def step(state, inp):
            a_t, bx_t = inp
            state = a_t * state + bx_t
            return (state, state.sum(axis=-1))
        init = jnp.zeros((x.shape[0], D_STATE), dtype=x.dtype)
        _, s_sum = jax.lax.scan(step, init, (a.transpose(1, 0, 2), bx.transpose(1, 0, 2)))
        s_sum = s_sum.T
        y = s_sum[..., None] * x_inner
        y = y * _silu(res)
        out = y @ W_out + b_out + x * D
        return out

    def _L0_ffn_ref(src, Wq, Wk_c, Wv_c, Wk, Wv, Wo, W_shared_in, W_shared_out, W1_shared, W2_experts, Wg_gate, We_gate, group_bias, expert_bias, norm1_w, norm2_w):
        import jax, jax.numpy as jnp
        import numpy as np
        D = 128
        H = 16
        DH = D // H
        DC = D // 4
        HID = 256
        G = 2
        EPG = 4
        E = G * EPG
        TOPK = 2
        EPS = 1e-06
        B, T = (2, 256)

        def _rope_sincos(t, dh):
            inv_freq = 1.0 / 10000.0 ** (jnp.arange(0, dh, 2, dtype=jnp.float32) / dh)
            ang = jnp.arange(t, dtype=jnp.float32)[:, None] * inv_freq[None, :]
            return (jnp.sin(ang), jnp.cos(ang))

        def _apply_rope(x, sin, cos):
            x1 = x[..., ::2]
            x2 = x[..., 1::2]
            r = jnp.stack([x1 * cos - x2 * sin, x1 * sin + x2 * cos], axis=-1)
            return r.reshape(x.shape)

        def _swiglu(x):
            a, b = jnp.split(x, 2, axis=-1)
            return jax.nn.silu(a) * b

        def _rmsnorm(x, w):
            return x * jax.lax.rsqrt(jnp.mean(x * x, axis=-1, keepdims=True) + EPS) * w
        Bb, Tt, C = src.shape
        q = (src @ Wq).reshape(Bb, Tt, H, DH).transpose(0, 2, 1, 3)
        k = (src @ Wk_c @ Wk).reshape(Bb, Tt, H, DH).transpose(0, 2, 1, 3)
        v = (src @ Wv_c @ Wv).reshape(Bb, Tt, H, DH).transpose(0, 2, 1, 3)
        sin, cos = _rope_sincos(Tt, DH)
        q = _apply_rope(q, sin, cos)
        k = _apply_rope(k, sin, cos)
        attn = jnp.einsum('bhqd,bhkd->bhqk', q, k) / np.sqrt(DH).astype(np.float32)
        attn = jax.nn.softmax(attn, axis=-1)
        sa = jnp.einsum('bhqk,bhkd->bhqd', attn, v)
        sa = sa.transpose(0, 2, 1, 3).reshape(Bb, Tt, C) @ Wo
        x = _rmsnorm(src + sa, norm1_w)
        S = Bb * Tt
        flat = x.reshape(S, C)
        shared = _swiglu(flat @ W_shared_in) @ W_shared_out
        g_probs = jax.nn.softmax(flat @ Wg_gate + group_bias, -1)
        g_idx = jnp.argmax(g_probs, axis=-1)
        e_logits = flat @ We_gate + expert_bias
        e_group = jnp.arange(E) // EPG
        in_group = e_group[None, :] == g_idx[:, None]
        e_probs = jax.nn.softmax(jnp.where(in_group, e_logits, -jnp.inf), -1)
        g_prob = jnp.take_along_axis(g_probs, g_idx[:, None], axis=1)
        p_expert = e_probs * g_prob
        topv, topi = jax.lax.top_k(p_expert, TOPK)
        w = jnp.zeros((S, E), flat.dtype).at[jnp.arange(S)[:, None], topi].set(topv)
        h = _swiglu(flat @ W1_shared)
        routed = jnp.zeros_like(shared)
        for e in range(E):
            routed = routed + h @ W2_experts[e] * w[:, e:e + 1]
        out = x + (shared + routed).reshape(Bb, Tt, C)
        return _rmsnorm(out, norm2_w)

    def _L1_attn_ref(x, gamma, wq, wk, wv, wa, wg, wo):
        import jax, jax.numpy as jnp
        import numpy as np
        B, S, D = (2, 512, 128)
        EPS = 1e-05

        def _rmsnorm(x, gamma):
            ss = jnp.sum(jnp.square(x), axis=-1, keepdims=True)
            inv = jax.lax.rsqrt(ss + EPS)
            return inv * x * gamma * x.shape[-1] ** 0.5

        def _gate_loop_operator(kv, q, a):

            def binop(e_i, e_j):
                a_i, kv_i = e_i
                a_j, kv_j = e_j
                return (a_j * a_i, a_j * kv_i + kv_j)
            _, y = jax.lax.associative_scan(binop, (a, kv), axis=1)
            return q * y
        x = _rmsnorm(x, gamma)
        q = x @ wq
        k = x @ wk
        v = x @ wv
        a = jax.nn.sigmoid(x @ wa)
        g = x @ wg
        kv = k * v
        y = _gate_loop_operator(kv, q, a)
        y = y * jax.nn.silu(g)
        return y @ wo

    def _L1_ffn_ref(x, Wr, W1, W2):
        import jax, jax.numpy as jnp
        import numpy as np
        N_EXPERTS = 8
        CAP_FACTOR = 1.25
        BATCH, SEQ, DMODEL, DFF = (4, 256, 128, 512)
        B, S, D = x.shape
        E = W1.shape[0]
        cap = int(CAP_FACTOR * B * S / E)
        t = x.reshape(-1, D)
        probs = jax.nn.softmax(t @ Wr, axis=-1)
        idx = jnp.argmax(probs, axis=-1)
        pmax = jnp.max(probs, axis=-1)
        onehot = jax.nn.one_hot(idx, E, dtype=jnp.int32)
        pos = jnp.sum(jnp.cumsum(onehot, axis=0) * onehot, axis=-1) - 1
        kept = pos < cap
        flat = idx * cap + jnp.minimum(pos, cap - 1)
        disp = jnp.zeros((E * cap, D), t.dtype).at[flat].add(t * kept[:, None].astype(t.dtype))
        ein = disp.reshape(E, cap, D)
        h = jax.nn.relu(jnp.einsum('ecd,edf->ecf', ein, W1))
        eout = jnp.einsum('ecf,efd->ecd', h, W2).reshape(E * cap, D)
        comb = jnp.where(kept[:, None], eout[flat], t)
        factor = jnp.where(kept, pmax, jnp.ones_like(pmax))
        out = (comb * factor[:, None]).reshape(B, S, D)
        return out
    x = L0_attn_x
    x = _layernorm(x + _L0_attn_ref(x, L0_attn_W_in, L0_attn_b_in, L0_attn_W_xp, L0_attn_b_xp, L0_attn_W_dt, L0_attn_b_dt, L0_attn_W_out, L0_attn_b_out, L0_attn_A_log, L0_attn_D), axis=-1)
    x = _layernorm(x + _L0_ffn_ref(x, L0_ffn_Wq, L0_ffn_Wk_c, L0_ffn_Wv_c, L0_ffn_Wk, L0_ffn_Wv, L0_ffn_Wo, L0_ffn_W_shared_in, L0_ffn_W_shared_out, L0_ffn_W1_shared, L0_ffn_W2_experts, L0_ffn_Wg_gate, L0_ffn_We_gate, L0_ffn_group_bias, L0_ffn_expert_bias, L0_ffn_norm1_w, L0_ffn_norm2_w), axis=-1)
    x = _layernorm(x + _L1_attn_ref(x, L1_attn_gamma, L1_attn_wq, L1_attn_wk, L1_attn_wv, L1_attn_wa, L1_attn_wg, L1_attn_wo), axis=-1)
    x = _layernorm(x + _L1_ffn_ref(x, L1_ffn_Wr, L1_ffn_W1, L1_ffn_W2), axis=-1)
    return x

_drawn_inputs = setup_inputs


def setup_inputs(seed=0):
    import zlib

    import numpy as np

    out = dict(_drawn_inputs(seed))
    spreads = {'L0_attn_b_in': (0.0, 0.8),
     'L0_attn_b_xp': (0.0, 0.8),
     'L0_attn_b_dt': (0.0, 0.8),
     'L0_attn_b_out': (0.0, 0.1),
     'L0_ffn_group_bias': (0.0, 0.8),
     'L0_ffn_expert_bias': (0.0, 0.8),
     'L0_ffn_norm1_w': (1.0, 0.2),
     'L0_ffn_norm2_w': (1.0, 0.2),
     'L1_attn_gamma': (1.0, 0.2)}
    factors = {'L0_attn_W_in': 8.0,
     'L0_attn_W_xp': 4.887,
     'L0_attn_W_dt': 8.0,
     'L0_attn_W_out': 8.0,
     'L0_attn_A_log': 8.0,
     'L0_ffn_Wq': 8.0,
     'L0_ffn_Wk_c': 8.0,
     'L0_ffn_Wv_c': 8.0,
     'L0_ffn_Wk': 8.0,
     'L0_ffn_Wv': 8.0,
     'L0_ffn_Wo': 8.0,
     'L0_ffn_W_shared_in': 5.238,
     'L0_ffn_W_shared_out': 5.294,
     'L0_ffn_W1_shared': 8.0,
     'L0_ffn_W2_experts': 8.0,
     'L0_ffn_Wg_gate': 8.0,
     'L0_ffn_We_gate': 8.0,
     'L1_ffn_Wr': 4.718,
     'L1_ffn_W1': 5.441,
     'L1_ffn_W2': 4.557}
    for name, (base, spread) in spreads.items():
        noise = np.random.default_rng([zlib.crc32(name.encode()), seed]).standard_normal(out[name].shape)
        drawn = base * np.exp(spread * noise) if base else spread * noise
        out[name] = jnp.asarray(drawn.astype(out[name].dtype))
    for name, factor in factors.items():
        out[name] = (out[name] * factor).astype(out[name].dtype)
    return out
```

```python
import math
import struct
from contextlib import ExitStack

import concourse.bass as bass
from concourse import mybir

F32 = mybir.dt.float32
BF16 = mybir.dt.bfloat16
I32 = mybir.dt.int32
ACT = mybir.ActivationFunctionType
ALU = mybir.AluOpType
AX = mybir.AxisListType

P = 128
D = 128
S = 2048
NT = S // P
CH = 512
NC = S // CH
TC = CH // P
NSTATE = 64
H, DH = 16, 8
HID = 256
E0, EPG = 8, 4
E1, CAP, DFF = 8, 320, 512
SLOTS = E1 * CAP
NST = SLOTS // P
FM = DFF // P
LN_EPS, RMS0_EPS, RMS1_EPS = 1e-5, 1e-6, 1e-5
BIG = 1e30
RSQRT_MAGIC = float(0x5F3759DF)
ONE_PAIR = struct.unpack("<f", struct.pack("<I", 0x3F803F80))[0]

TERMS = 72
ROWS = TERMS + 2
HB = 4
AHEAD = 3
PR = 2
STB = 3
LOOPED = 12

N_LN1, N_RMSX, N_RMSO, N_LN2, N_RMS1, N_LN3, N_LN4 = range(7)


def psum_plan():
    first, rest = [], []
    for i in range(12):
        if i < NC:
            first.append((("xT", i), i % 2))
        if 1 <= i <= NC:
            first += [(("xr", i - 1, m), 2 + m) for m in range(4)]
        if 2 <= i <= NC + 1:
            first.append((("dt", i - 2), 6))
        if 5 <= i <= NC + 4:
            first += [(("bx", i - 5), 0), (("mean", i - 5), 7)]
        if 6 <= i <= NC + 5:
            first.append((("ssum", i - 6), 1))
        if 7 <= i <= NC + 6:
            first.append((("outA", i - 7), 2 + i - 7))
        if i >= 8:
            first.append((("x1T", i - 8), 6 + i % 2))
    for c in range(NC):
        first += [(("q", c), 0), (("qr", c), 1), (("kvc", c), 2)]
        first += [(("k", c), 3), (("kr", c), 4), (("v", c), 5)]
    rest += [(("wo", c), c) for c in range(NC)]
    rest += [(("xnT", c), 4 + c % 2) for c in range(NC)]
    rest.append((("gate",), 6))
    rest += [(("ffn", c, m), m) for c in range(NC) for m in range(8)]
    for t in range(NT):
        if t % TC == 0:
            rest.append((("sh", t // TC), (t // TC) % 2))
        rest += [(("rt", t, f), 2 + f + 2 * (t % 2)) for f in range(2)]
    rest += [(("xrT", c), 6 + c % 2) for c in range(NC)]
    for c in range(NC + 1):
        if c < NC:
            rest += [(("pk", c), 0), (("pv", c), 1), (("pq", c), 2), (("pa", c), 3), (("pg", c), 4)]
        if c >= 1:
            rest.append((("wo1", c - 1), 5))
    rest += [(("x3T", c), 6 + c % 2) for c in range(NC)]
    rest += [(("route",), 0), (("cum",), 1)]
    rest += [(("einT", n), 2 + n % 2) for n in range(NST // TC)]
    for e in range(E1):
        rest += [(("h1", e, m), 4 + m) for m in range(FM)]
        rest.append((("eo", e), e % 2))
    plan, fills = {}, [0] * 8
    for order in (first, rest):
        tenant = [None] * 8
        for key, b in order:
            fills[b] += 1
            plan[key] = (b, fills[b], tenant[b])
            tenant[b] = key
        if order is first:
            last = list(tenant)
    return plan, last


def norm_order():
    order = [(k, c) for k in (N_LN1, N_RMSX) for c in range(NC)]
    for j in range(NC + 2):
        order += [(k, j - i) for i, k in enumerate((N_RMSO, N_LN2, N_RMS1)) if 0 <= j - i < NC]
    return order + [(k, c) for k in (N_LN3, N_LN4) for c in range(NC)]


def build(nc, a, scratch, out):
    plan, before_attention = psum_plan()
    norms = norm_order()
    with ExitStack() as ctx:
        def sb(name, shape, dt=F32):
            return ctx.enter_context(nc.sbuf_tensor(name, shape, dt))

        def sem(name):
            return ctx.enter_context(nc.semaphore(name))

        bank = [ctx.enter_context(nc.psum_tensor(f"bank{i}", [P, CH], F32)) for i in range(3)]
        maxps = [ctx.enter_context(nc.psum_tensor(f"maxps{i}", [P, 2 * CH], F32)) for i in range(2)]
        pvps = ctx.enter_context(nc.psum_tensor("pvps", [P, CH], F32))
        bank_ap = [bank[0][:, :], bank[1][:, :], bank[2][:, :], maxps[0][:, 0:CH], maxps[0][:, CH:],
                   maxps[1][:, 0:CH], maxps[1][:, CH:], pvps[:, :]]

        slot = [sb(f"slot{i}", [P, S]) for i in range(18)]

        def two(i):
            return [slot[i], slot[i + 1]]

        x0T, x0F = slot[0], slot[1]
        xin, gated = two(2), two(4)
        sp_abs, sp_relu = slot[6], slot[7]
        aF, bxF, stF = slot[8], slot[9], slot[10]
        pre, x1T, x1F = slot[11], slot[12], slot[1]
        cosF, sinF = slot[13], slot[14]
        vT = slot[15]
        kvcF = two(8)
        rope_t = [slot[6], slot[7]]
        rope_s = slot[10]
        heads_q = [slot[2 + i // 2][:, (i % 2) * 1024:(i % 2) * 1024 + 1024].bitcast(BF16) for i in range(HB)]
        heads_k = [slot[4 + i // 2][:, (i % 2) * 1024:(i % 2) * 1024 + 1024].bitcast(BF16) for i in range(HB)]
        prob = [slot[16], slot[17]]
        pv_sb = slot[0]
        numF, denF = slot[6], slot[7]
        xnT, xnF = slot[8], slot[1]
        act_ff = slot[9]
        hid = [two(2), two(4)]
        oT = slot[10]
        x2T, xrT, xrF = slot[0], slot[11], slot[1]
        qF, kvF, decF, gsF, kF, hsF, yF = slot[13], slot[6], slot[7], slot[2], slot[3], slot[4], slot[5]
        x3T, x3F = slot[12], slot[1]
        w1 = [slot[14], slot[15]]
        w2 = [slot[16], slot[17]]
        einT = [slot[2], slot[3]]
        einF = [slot[4], slot[5]]
        hE = [slot[6], slot[7]]
        eoT = slot[8]
        combT, finT, yT = slot[9], slot[10], slot[11]

        w_in = sb("w_in", [P, 512])
        w_xp = sb("w_xp", [P, 2, NSTATE])
        w_dt = sb("w_dt", [P, 2, D])
        w_out = sb("w_out", [P, 2, D])
        b_in = sb("b_in", [P, 4])
        b_xp = sb("b_xp", [NSTATE, 1])
        b_dt = sb("b_dt", [P, 1])
        a_log = sb("a_log", [P, 1])
        a_exp = sb("a_exp", [P, 1])
        a_neg = sb("a_neg", [P, 1])
        bc = {n: sb(f"bc_{n}", [P, D]) for n in ("d", "bo", "n1", "n2")}
        wq = sb("wq", [P, D])
        wqr = sb("wqr", [P, D])
        wkvc = sb("wkvc", [P, 64])
        wk = sb("wk", [32, D])
        wkr = sb("wkr", [32, D])
        wv = sb("wv", [32, D])
        wo = sb("wo", [P, D])
        w_ff = sb("w_ff", [P, 2, 512])
        w_so = sb("w_so", [P, 2, D])
        w2e = sb("w2e", [P, 2, E0 * D])
        w_gate = sb("w_gate", [P, 2 + E0])
        b_gate = sb("b_gate", [P, 2 + E0])
        w_l1 = {n: sb(f"l1_{n}", [P, D]) for n in ("q", "k", "v", "a", "g", "o")}
        gamma = sb("gamma", [P, 1])
        w_r = sb("w_r", [P, E1])

        ident = sb("ident", [P, P])
        identb = sb("identb", [P, P], BF16)
        ones = sb("ones", [P, P])
        mean_w = sb("mean_w", [P, NSTATE])
        triu = sb("triu", [P, P], BF16)
        onesb = sb("onesb", [P, P], BF16)
        rev4 = sb("rev4", [P, EPG])
        rev8 = sb("rev8", [P, E1])
        base8 = sb("base8", [P, E1])
        keep_scan = sb("keep_scan", [P, E1 * NT])
        token_i = sb("token_i", [P, NT], I32)
        spare = sb("spare", [P, NT])
        zeros = sb("zeros", [P, 512])

        bn = sb("bn", [P, 2, TC, 6])
        mv = sb("mv", [P, 7 * NC, TC, 2])
        msq = sb("msq", [P, 7 * NC, TC])
        var = sb("var", [P, 7 * NC, TC])
        rs = sb("rs", [P, 7 * NC, TC])
        nw = sb("nw", [P, 2, TC])
        maxes = sb("maxes", [P, 2, NT, 2])
        mneg = sb("mneg", [P, NT])
        mparts = sb("mparts", [P, 2 * NT], BF16)
        mrows = sb("mrows", [2 * NT, P], BF16)
        vh = sb("vh", [P, 2, NT, 32])
        gl = sb("gl", [P, NT, 2 + E0])
        g_s = sb("g_s", [P, 12, NT])
        g4 = sb("g4", [P, 12, NT, EPG])
        wtop = sb("wtop", [P, NT, E0])
        r8 = sb("r8", [P, 6, NT, E1])
        onehot = sb("onehot", [P, E1, NT], BF16)
        et = sb("et", [P, 4, E1, NT])
        r_s = sb("r_s", [P, 12, NT])
        dest = sb("dest", [P, NT], I32)

        ld_x = [sem(f"ld_x{c}") for c in range(NC)]
        ld_a, ld_a1, ld_a2, ld_b, ld_c, ld_d, ld_e = (sem(f"ld_{n}") for n in ("w_in", "w_dt", "layer0", "attn", "ffn", "layer1", "experts"))
        const_pool, const_dve, zeroed = sem("const_pool"), sem("const_dve"), sem("zeroed")
        bank_full = [sem(f"bank_full{i}") for i in range(8)]
        resid_ready, acc_ready, l1_ps = sem("resid_ready"), sem("acc_ready"), sem("l1_ps")
        relu_act, relu_dve, comb_ready = sem("relu_act"), sem("relu_dve"), sem("comb_ready")
        x0F_ready, silu_ready, gated_ready, u_ready = sem("x0F_ready"), sem("silu_ready"), sem("gated_ready"), sem("u_ready")
        relu_ready, absu_ready, expu_ready, sp_ready, delta_ready = sem("relu_ready"), sem("absu_ready"), sem("expu_ready"), sem("sp_ready"), sem("delta_ready")
        aexp_ready, aneg_ready, decay_ready, bx_ready = sem("aexp_ready"), sem("aneg_ready"), sem("decay_ready"), sem("bx_ready")
        state_ready, y_ready, pre_step = sem("state_ready"), sem("y_ready"), sem("pre_step")
        dve_step = sem("dve_step")
        pool_step = sem("pool_step")
        act_step = sem("act_step")
        guess_ready, rstd_ready = sem("guess_ready"), sem("rstd_ready")
        x1T_ready, x1F_ready = sem("x1T_ready"), sem("x1F_ready")
        rot_ready, kvc_ready, rope_ready, vT_ready = sem("rot_ready"), sem("kvc_ready"), sem("rope_ready"), sem("vT_ready")
        sum_ready, part_ready, rest_ready, third_ready = sem("sum_ready"), sem("part_ready"), sem("rest_ready"), sem("third_ready")
        split_stored = sem("split_stored")
        head_loaded = [sem(f"head_loaded{b}") for b in range(HB)]
        ones_ready, vh_ready = sem("ones_ready"), sem("vh_ready")
        st_full, exp_done, pv_done, pv_out = sem("st_full"), sem("exp_done"), sem("pv_done"), sem("pv_out")
        pv_stored = [sem(f"pv_stored{b}") for b in range(2)]
        mx_full, mx_free, mparts_ready = sem("mx_full"), sem("mx_free"), sem("mparts_ready")
        mcomb = sem("mcomb")
        mt_full, mrows_ready, mrows_placed = sem("mt_full"), sem("mrows_ready"), sem("mrows_placed")
        attn_loaded = [sem(f"attn_loaded{c}") for c in range(NC)]
        attn_ready = sem("attn_ready")
        xnT_ready, xnF_ready, silu0_ready, hid_ready = sem("xnT_ready"), sem("xnF_ready"), sem("silu0_ready"), sem("hid_ready")
        gate_ready, gexp_in, gexp_ready, wtop_ready = sem("gate_ready"), sem("gexp_in"), sem("gexp_ready"), sem("wtop_ready")
        x2T_ready, xrT_ready, xrF_ready = sem("x2T_ready"), sem("xrT_ready"), sem("xrF_ready")
        l1_act, kv_ready, hs_ready, y1_ready = sem("l1_act"), sem("kv_ready"), sem("hs_ready"), sem("y1_ready")
        x3T_ready, x3F_ready = sem("x3T_ready"), sem("x3F_ready")
        rexp_in, rexp_ready, onehot_ready, dest_ready = sem("rexp_in"), sem("rexp_ready"), sem("onehot_ready"), sem("dest_ready")
        scattered, spare_stored, ein_loaded, einF_ready = sem("scattered"), sem("spare_stored"), sem("ein_loaded"), sem("einF_ready")
        relu1_ready, eo_ready = sem("relu1_ready"), sem("eo_ready")
        eo_stored = [sem(f"eo_stored{b}") for b in range(4)]
        gathered, out_ready, out_stored = sem("gathered"), sem("out_ready"), sem("out_stored")

        qk_split, attn_out, disp, eout = scratch

        def ck(t, c, n=CH):
            return t[:, c * n:(c + 1) * n]

        def tl(t, i):
            return t[:, i * P:(i + 1) * P]

        def full(eng, key):
            b, n, _ = plan[key]
            eng.wait_ge(bank_full[b], n)
            return bank_ap[b]

        def released(key):
            kind, c = key[0], key[1] if len(key) > 1 else 0
            m = key[2] if len(key) > 2 else 0
            return {
                "xT": (x0F_ready, c + 1), "xr": (silu_ready, 4 * c + m + 1), "dt": (u_ready, c + 1),
                "bx": (bx_ready, c + 1), "mean": (decay_ready, c + 1), "ssum": (y_ready, 2 * c + 2),
                "outA": (resid_ready, c + 1), "x1T": (x1F_ready, c + 1),
                "q": (rope_ready, 4 * c + 1), "qr": (rope_ready, 4 * c + 2),
                "k": (rope_ready, 4 * c + 3), "kr": (rope_ready, 4 * c + 4),
                "kvc": (kvc_ready, 2 * c + 2), "v": (vT_ready, c + 1),
                "wo": (resid_ready, NC + c + 1), "xnT": (xnF_ready, c + 1), "gate": (gate_ready, 1),
                "ffn": (silu0_ready, 4 * c + m % 4 % 2 + 2 * (m // 4) + 1) if m % 4 < 2
                else (hid_ready, 4 * c + m % 2 + 2 * (m // 4) + 1),
                "sh": (acc_ready, 33 * 4 * (c // 1) + 1) if False else (acc_ready, 33 * c + 1),
                "rt": (acc_ready, 33 * (c // TC) + 1 + 8 * (c % TC) + 4 * (m + 1)),
                "xrT": (xrF_ready, c + 1),
                "pk": (l1_act, 4 * c + 1), "pq": (l1_act, 4 * c + 2), "pa": (l1_act, 4 * c + 3),
                "pg": (l1_act, 4 * c + 4), "pv": (kv_ready, c + 1),
                "wo1": (resid_ready, 2 * NC + c + 1), "x3T": (x3F_ready, c + 1),
                "route": (gate_ready, 2), "cum": (comb_ready, 1), "einT": (einF_ready, c + 1),
                "h1": (relu_act if m % 2 == 0 else relu_dve, 2 * c + m // 2 + 1),
                "eo": (eo_ready, 2 * c + 2),
            }[kind]

        def parts(i):
            t = slot[[16, 17, 2, 3][i // 2]][:, (i % 2) * 1024:(i % 2) * 1024 + 768].bitcast(BF16)
            return t.rearrange("p (s q) -> p s q", s=3)

        def pieces(e):
            lo, hi = e * CAP, (e + 1) * CAP
            if lo < S < hi:
                return [(0, lo, S), (1, S, hi)]
            return [(lo // S, lo, hi)]

        def rope_a(n):
            return [slot[6], slot[10]][n]

        def rope_b(n):
            return [slot[7], slot[11]][n]

        def take_expert(act, e):
            o = full(act, ("eo", e))
            if e >= 4:
                act.wait_ge(eo_stored[e % 4], 32 * (e // 4))
            dst = eoT[:, (e % 4) * 512:(e % 4) * 512 + 384]
            act.activation(dst[:, 0:256], o[:, 0:256], ACT.Copy).then_inc(eo_ready, 1)
            act.activation(dst[0:64, 256:384], o[0:64, 256:384], ACT.Copy).then_inc(eo_ready, 1)

        def tiles(t, c):
            return ck(t, c).rearrange("p (t d) -> p t d", d=D)

        block = ctx.enter_context(nc.Block())

        @block.sync
        def _(sp):
            xt = a["L0_attn_x"].rearrange("b (t p) d -> p (b t) d", p=P)
            col = lambda v: v.rearrange("(p o) -> p o", o=1)
            row = lambda v: v.rearrange("(o n) -> o n", o=1)

            def load_x(c):
                sp.dma_start(ck(x0T, c).rearrange("p (t d) -> p t d", d=D), xt[:, c * TC:(c + 1) * TC, :]).then_inc(ld_x[c], 16)

            load_x(0)
            sp.dma_start(w_in[:, :], a["L0_attn_W_in"]).then_inc(ld_a, 16)
            sp.dma_start(b_in[:, :], a["L0_attn_b_in"].rearrange("(m p) -> p m", p=P),
                         allow_slow_non_contiguous=True).then_inc(ld_a, 16)
            load_x(1)
            sp.dma_start(w_dt[:, :, :], a["L0_attn_W_dt"].rearrange("(k p) n -> p k n", p=P)).then_inc(ld_a1, 16)
            sp.dma_start(b_dt[:, :], col(a["L0_attn_b_dt"])).then_inc(ld_a1, 16)
            load_x(2)
            load_x(3)
            for dst, src in ((a_log[NSTATE:P, :], col(a["L0_attn_A_log"])),
                             (w_xp[:, :, :], a["L0_attn_W_xp"].rearrange("(k p) n -> p k n", p=P)),
                             (b_xp[:, :], col(a["L0_attn_b_xp"])),
                             (bc["d"][:, :], row(a["L0_attn_D"]).broadcast_to([P, D])),
                             (bc["bo"][:, :], row(a["L0_attn_b_out"]).broadcast_to([P, D])),
                             (w_out[:, :, :], a["L0_attn_W_out"].rearrange("(k p) n -> p k n", p=P)),
                             (w_r[:, :], a["L1_ffn_Wr"])):
                sp.dma_start(dst, src).then_inc(ld_a2, 16)
            for dst, src in ((wq[:, :], a["L0_ffn_Wq"]), (wkvc[:, 0:32], a["L0_ffn_Wk_c"]),
                             (wkvc[:, 32:64], a["L0_ffn_Wv_c"]), (wk[:, :], a["L0_ffn_Wk"]),
                             (wv[:, :], a["L0_ffn_Wv"]), (cosF[:, :], a["cos"]), (sinF[:, :], a["sin"])):
                sp.dma_start(dst, src).then_inc(ld_b, 16)
            sp.wait_ge(zeroed, 1)
            sp.dma_start(disp[0:SLOTS, :].rearrange("(p a) d -> p (a d)", p=P)[:, 0:2560].rearrange("p (b n) -> p b n", n=512),
                         zeros[:, :].rearrange("p (o n) -> p o n", o=1).broadcast_to([P, 5, 512])).then_inc(zeroed, 16)
            for dst, src in ((wo[:, :], a["L0_ffn_Wo"]), (w_ff[:, 0, :], a["L0_ffn_W_shared_in"]),
                             (w_ff[:, 1, :], a["L0_ffn_W1_shared"]),
                             (w_so[:, :, :], a["L0_ffn_W_shared_out"].rearrange("(k p) n -> p k n", p=P)),
                             (w2e[:, 0, :].rearrange("p (e n) -> p e n", e=E0), a["L0_ffn_W2_experts"][:, 0:P, :].rearrange("e p n -> p e n")),
                             (w2e[:, 1, :].rearrange("p (e n) -> p e n", e=E0), a["L0_ffn_W2_experts"][:, P:HID, :].rearrange("e p n -> p e n")),
                             (w_gate[:, 0:2], a["L0_ffn_Wg_gate"]), (w_gate[:, 2:], a["L0_ffn_We_gate"]),
                             (b_gate[:, 0:2], row(a["L0_ffn_group_bias"]).broadcast_to([P, 2])),
                             (b_gate[:, 2:], row(a["L0_ffn_expert_bias"]).broadcast_to([P, E0])),
                             (bc["n1"][:, :], row(a["L0_ffn_norm1_w"]).broadcast_to([P, D])),
                             (bc["n2"][:, :], row(a["L0_ffn_norm2_w"]).broadcast_to([P, D]))):
                sp.dma_start(dst, src).then_inc(ld_c, 16)
            for n in ("q", "k", "v", "a", "g", "o"):
                sp.dma_start(w_l1[n][:, :], a[f"L1_attn_w{n}"]).then_inc(ld_d, 16)
            sp.dma_start(gamma[:, :], col(a["L1_attn_gamma"])).then_inc(ld_d, 16)

            for c in range(NC):
                for n in range(2):
                    i = 2 * c + n
                    sp.wait_ge(third_ready, i + 1)
                    sp.dma_start(qk_split[n, :, :, c * CH:(c + 1) * CH].rearrange("s p q -> p s q"),
                                 parts(i)).then_inc(split_stored, 16)

            def load_head(hv, b):
                rows = bass.ds(hv * DH, DH)
                for i in range(3):
                    r = slice(i * 3 * DH, (i + 1) * 3 * DH)
                    sp.dma_start(heads_q[b][r, :], qk_split[0, i, rows, :].unsqueeze(0).broadcast_to([3, DH, S])).then_inc(head_loaded[b], 16)
                    sp.dma_start(heads_k[b][r, :], qk_split[1, :, rows, :]).then_inc(head_loaded[b], 16)

            def place_max(b):
                for s in range(2):
                    sp.dma_start(heads_q[b][TERMS + s:TERMS + s + 1, :].rearrange("o (t p) -> o t p", p=P),
                                 mrows[s * NT:(s + 1) * NT, :]).then_inc(mrows_placed, 16)

            sp.wait_ge(split_stored, 16 * 2 * NC)
            sp.wait_ge(ones_ready, HB)
            for h in range(3):
                load_head(h, h)
            sp.wait_ge(mrows_ready, 1)
            place_max(0)

            def head(hv, h, lap=0):
                if h + 3 < H:
                    if not (isinstance(hv, int) and hv == 0):
                        sp.wait_ge(st_full, hv * (NT * NC))
                    load_head(hv + 3, (h + 3) % HB)
                if h >= 1:
                    sp.wait_ge(pv_out, hv)
                    store_out(hv - 1, (h - 1) % 2)
                if h + 1 < H:
                    sp.wait_ge(mrows_ready, hv + 2)
                    place_max((h + 1) % HB)

            def store_out(hv, b):
                sp.dma_start(attn_out[bass.ds(hv * P, P), :], ck(pv_sb, b)).then_inc(pv_stored[b], 16)

            head(0, 0)
            for h in range(1, 4):
                head(h, h)
            with sp.Fori(1, LOOPED // 4) as it:
                for j in range(4):
                    head(it * 4 + j, 4 + j, it - 1)
            for h in range(LOOPED, H):
                head(h, h)
            sp.wait_ge(pv_out, H)
            store_out(H - 1, (H - 1) % 2)
            for b in range(2):
                sp.wait_ge(pv_stored[b], 16 * (H // 2))
            for c in range(NC):
                src = attn_out.rearrange("(h c r) q -> c h r q", h=H, r=32)[c]
                sp.dma_start(ck(numF, c), src[:, 0:DH, :]).then_inc(attn_loaded[c], 16)
                sp.dma_start(ck(denF, c), src[:, DH:2 * DH, :]).then_inc(attn_loaded[c], 16)

            sp.wait_ge(pv_done, NT * H)
            sp.wait_ge(vh_ready, H)
            for i in range(2):
                sp.dma_start(w1[i][:, :].rearrange("p (e f) -> p e f", f=DFF),
                             a["L1_ffn_W1"][4 * i:4 * i + 4].rearrange("e p f -> p e f")).then_inc(ld_e, 16)
                sp.dma_start(w2[i][:, :].rearrange("p (e n) -> p e n", n=D),
                             a["L1_ffn_W2"][4 * i:4 * i + 4].rearrange("e (k p) n -> p (e k) n", p=P)).then_inc(ld_e, 16)

            sp.wait_ge(x3T_ready, NC * TC)
            sp.dma_start(eout[SLOTS:SLOTS + S, :].rearrange("(t p) d -> p t d", p=P),
                         x3T[:, :].rearrange("p (t d) -> p t d", d=D)).then_inc(spare_stored, 16)
            sp.wait_ge(scattered, 16 * NT)
            for n in range(NST // TC):
                dst = einT[n // 4][:, (n % 4) * CH:(n % 4 + 1) * CH]
                sp.dma_start(dst.rearrange("p (t d) -> p t d", d=D),
                             disp[n * CH:(n + 1) * CH, :].rearrange("(t p) d -> p t d", p=P)).then_inc(ein_loaded, 16)
            for e in range(E1):
                sp.wait_ge(eo_ready, 2 * (e + 1))
                src = eoT[:, (e % 4) * 512:(e % 4) * 512 + 384]
                sp.dma_start(eout[e * CAP:e * CAP + 256, :].rearrange("(t p) d -> p t d", p=P),
                             src[:, 0:256].rearrange("p (t d) -> p t d", d=D)).then_inc(eo_stored[e % 4], 16)
                sp.dma_start(eout[e * CAP + 256:(e + 1) * CAP, :], src[0:64, 256:384]).then_inc(eo_stored[e % 4], 16)
            for c in range(NC):
                sp.wait_ge(out_ready, TC * (c + 1))
                sp.dma_start(out.rearrange("b (t p) d -> p (b t) d", p=P)[:, c * TC:(c + 1) * TC, :],
                             ck(yT, c).rearrange("p (t d) -> p t d", d=D)).then_inc(out_stored, 16)
            sp.wait_ge(out_stored, 16 * NC)

        @block.tensor
        def _(pe):
            def fill(key):
                b, _, before = plan[key]
                if before:
                    pe.wait_ge(*released(before))
                return bank_ap[b], bank_full[b]

            def transposes(key, src):
                o, s = fill(key)
                for j in range(TC):
                    mm = pe.transpose(tl(o, j), tl(src, j), ident[:, :])
                mm.then_inc(s, 1)

            pe.wait_ge(const_pool, 2)
            for i in range(12):
                if i < NC:
                    pe.wait_ge(ld_x[i], 16)
                    transposes(("xT", i), ck(x0T, i))
                if 1 <= i <= NC:
                    c = i - 1
                    if c == 0:
                        pe.wait_ge(ld_a, 32)
                    pe.wait_ge(x0F_ready, c + 1)
                    for m in range(4):
                        o, s = fill(("xr", c, m))
                        pe.matmul(o, w_in[:, m * P:(m + 1) * P], ck(x0F, c), start=True, stop=True).then_inc(s, 1)
                if 2 <= i <= NC + 1:
                    c = i - 2
                    pe.wait_ge(silu_ready, 4 * c + 2)
                    if c == 0:
                        pe.wait_ge(ld_a1, 32)
                        pe.wait_ge(const_dve, 4)
                    o, s = fill(("dt", c))
                    pe.matmul(o, w_dt[:, 0, :], ck(xin[0], c), start=True, stop=False)
                    pe.matmul(o, w_dt[:, 1, :], ck(xin[1], c), start=False, stop=True).then_inc(s, 1)
                if 5 <= i <= NC + 4:
                    c = i - 5
                    pe.wait_ge(delta_ready, c + 1)
                    if c == 0:
                        pe.wait_ge(ld_a2, 16 * 7)
                    o, s = fill(("bx", c))
                    pe.matmul(o[0:NSTATE, :], w_xp[:, 0, :], ck(xin[0], c), start=True, stop=False)
                    o2, s2 = fill(("mean", c))
                    pe.matmul(o2[NSTATE:P, :], mean_w[:, :], ck(sp_relu, c), start=True, stop=True).then_inc(s2, 1)
                    pe.matmul(o[0:NSTATE, :], w_xp[:, 1, :], ck(xin[1], c), start=False, stop=True).then_inc(s, 1)
                if 6 <= i <= NC + 5:
                    c = i - 6
                    pe.wait_ge(state_ready, c + 1)
                    o, s = fill(("ssum", c))
                    pe.matmul(o, ones[0:NSTATE, :], ck(stF, c)[0:NSTATE, :], start=True, stop=True).then_inc(s, 1)
                if 7 <= i <= NC + 6:
                    c = i - 7
                    pe.wait_ge(y_ready, 2 * (c + 1))
                    o, s = fill(("outA", c))
                    for j in range(TC):
                        t = c * TC + j
                        pe.matmul(tl(o, j), tl(gated[0], t), w_out[:, 0, :], start=True, stop=False)
                        mm = pe.matmul(tl(o, j), tl(gated[1], t), w_out[:, 1, :], start=False, stop=True)
                    mm.then_inc(s, 1)
                if i >= 8:
                    c = i - 8
                    pe.wait_ge(x1T_ready, TC * (c + 1))
                    transposes(("x1T", c), ck(x1T, c))

            pe.wait_ge(ld_b, 112)
            pe.wait_ge(rot_ready, 4)
            for c in range(NC):
                pe.wait_ge(x1F_ready, c + 1)
                x = ck(x1F, c)
                for key, w in (("q", wq), ("qr", wqr)):
                    o, s = fill((key, c))
                    pe.matmul(o, w[:, :], x, start=True, stop=True).then_inc(s, 1)
                o, s = fill(("kvc", c))
                pe.matmul(o[0:32, :], wkvc[:, 0:32], x, start=True, stop=True)
                pe.matmul(o[32:64, :], wkvc[:, 32:64], x, start=True, stop=True).then_inc(s, 1)
                pe.wait_ge(kvc_ready, 2 * (c + 1))
                kc = ck(kvcF[0], c)[0:32, :]
                for key, w in (("k", wk), ("kr", wkr)):
                    o, s = fill((key, c))
                    pe.matmul(o, w[:, :], kc, start=True, stop=True).then_inc(s, 1)
                o, s = fill(("v", c))
                for j in range(TC):
                    mm = pe.matmul(tl(o, j), tl(kvcF[1], c * TC + j)[0:32, :], wv[:, :], start=True, stop=True)
                mm.then_inc(s, 1)

            for key in before_attention:
                pe.wait_ge(*released(key))

            def max_half(hv, h, t, f):
                n = 32 * h + 2 * t + f
                if n >= 2:
                    pe.wait_ge(mx_free, hv * 32 + (2 * t + f - 1))
                if f == 1 and h >= 1 and t == 1:
                    pe.wait_ge(mrows_ready, hv)
                b = h % HB
                for i in range(2):
                    k0 = f * 1024 + i * CH
                    mm = pe.matmul(maxps[f][:, i * CH:(i + 1) * CH], heads_q[b][0:TERMS, t * P:(t + 1) * P],
                                   heads_k[b][0:TERMS, k0:k0 + CH], start=True, stop=True)
                mm.then_inc(mx_full, 1)

            def max_turn(hv, h):
                pe.wait_ge(mparts_ready, hv + 1)
                pe.wait_ge(mx_free, (hv + 1) * 32 + (2 if h + 1 < H else 0))
                pe.transpose(maxps[1][0:2 * NT, 0:P // 2].bitcast(BF16), mparts[:, :], identb[:, :]).then_inc(mt_full, 1)

            def score(hv, h, g, c):
                u = g * NC + c
                if u >= STB:
                    pe.wait_ge(exp_done, hv * 64 + (u - STB + 1))
                elif h >= 1:
                    pe.wait_ge(exp_done, hv * 64 - (63 - u) % STB)
                b = h % HB
                pe.matmul(bank[u % STB][:, :], heads_k[b][0:ROWS, g * P:(g + 1) * P],
                          heads_q[b][0:ROWS, c * CH:(c + 1) * CH], start=True, stop=True).then_inc(st_full, 1)

            def weigh(hv, h, g):
                pe.wait_ge(exp_done, hv * 64 + NC * (g + 1))
                if g == 0:
                    pe.wait_ge(vh_ready, hv + 1)
                    if h >= 1:
                        pe.wait_ge(pv_out, hv)
                for c in range(NC):
                    mm = pe.matmul(pvps[32 * c:32 * c + 32, :], vh[:, h % 2, g, :],
                                   prob[g % PR][:, c * CH:(c + 1) * CH], start=(g == 0), stop=(g == NT - 1))
                mm.then_inc(pv_done, 1)

            def head(hv, h, lap=0):
                pe.wait_ge(mrows_placed, (hv + 1) * 32)
                for g in range(NT):
                    t, k = (g + AHEAD, 1) if g + AHEAD < NT else (g + AHEAD - NT, 2)
                    more = h + k < H
                    if more and t == 0:
                        pe.wait_ge(head_loaded[(h + 2) % HB], ((h + 2) // HB + 1 + lap) * 96)
                    score(hv, h, g, 0)
                    score(hv, h, g, 1)
                    if more:
                        max_half(hv + k, h + k, t, 0)
                    score(hv, h, g, 2)
                    score(hv, h, g, 3)
                    if g == NT + 1 - AHEAD and h + 1 < H:
                        max_turn(hv + 1, h + 1)
                    if more:
                        max_half(hv + k, h + k, t, 1)
                    if g >= 1:
                        weigh(hv, h, g - 1)
                    elif h >= 1:
                        weigh(hv - 1, h - 1, NT - 1)

            pe.wait_ge(ones_ready, HB)
            pe.wait_ge(head_loaded[0], 96)
            for t in range(NT):
                max_half(0, 0, t, 0)
                max_half(0, 0, t, 1)
            pe.wait_ge(head_loaded[1], 96)
            for t in range(AHEAD):
                max_half(1, 1, t, 0)
                if t == 1:
                    max_turn(0, 0)
                max_half(1, 1, t, 1)
            for h in range(4):
                head(h, h)
            with pe.Fori(1, LOOPED // 4) as it:
                for j in range(4):
                    head(it * 4 + j, 4 + j, it - 1)
            for h in range(LOOPED, H):
                head(h, h)
            weigh(H - 1, H - 1, NT - 1)

            pe.wait_ge(exp_done, 64 * H)
            pe.wait_ge(mx_free, 32 * H)
            pe.wait_ge(mrows_ready, H)
            pe.wait_ge(pv_out, H)
            pe.wait_ge(ld_c, 192)
            for c in range(NC):
                pe.wait_ge(attn_ready, c + 1)
                o, s = fill(("wo", c))
                for j in range(TC):
                    mm = pe.matmul(tl(o, j), tl(numF, c * TC + j), wo[:, :], start=True, stop=True)
                mm.then_inc(s, 1)
            for c in range(NC):
                pe.wait_ge(xnT_ready, TC * (c + 1))
                transposes(("xnT", c), ck(xnT, c))
            pe.wait_ge(xnF_ready, NC)
            o, s = fill(("gate",))
            for t in range(NT):
                mm = pe.matmul(o[:, t * 10:t * 10 + 10], tl(xnF, t), w_gate[:, :], start=True, stop=True)
            mm.then_inc(s, 1)
            for c in range(NC):
                for m in range(8):
                    o, s = fill(("ffn", c, m))
                    pe.matmul(o, w_ff[:, m // 4, (m % 4) * P:(m % 4 + 1) * P], ck(xnF, c), start=True, stop=True).then_inc(s, 1)
            for t in range(NT):
                c = t // TC
                pe.wait_ge(hid_ready, 4 * (c + 1))
                if t % TC == 0:
                    sh, s_sh = fill(("sh", c))
                    for j in range(TC):
                        for k in range(2):
                            mm = pe.matmul(tl(sh, j), tl(hid[0][k], t + j), w_so[:, k, :], start=(k == 0), stop=(k == 1))
                    mm.then_inc(s_sh, 1)
                for f in range(2):
                    o, s = fill(("rt", t, f))
                    for k in range(2):
                        mm = pe.matmul(o, tl(hid[1][k], t), w2e[:, k, f * CH:(f + 1) * CH], start=(k == 0), stop=(k == 1))
                    mm.then_inc(s, 1)
            for c in range(NC):
                pe.wait_ge(xrT_ready, TC * (c + 1))
                transposes(("xrT", c), ck(xrT, c))
            pe.wait_ge(ld_d, 112)
            for i in range(NC + 1):
                if i < NC:
                    pe.wait_ge(xrF_ready, i + 1)
                    for key, w in (("pk", "k"), ("pv", "v"), ("pq", "q"), ("pa", "a"), ("pg", "g")):
                        o, s = fill((key, i))
                        pe.matmul(o, w_l1[w][:, :], ck(xrF, i), start=True, stop=True).then_inc(s, 1)
                if i >= 1:
                    c = i - 1
                    pe.wait_ge(y1_ready, c + 1)
                    o, s = fill(("wo1", c))
                    for j in range(TC):
                        mm = pe.matmul(tl(o, j), tl(yF, c * TC + j), w_l1["o"][:, :], start=True, stop=True)
                    mm.then_inc(s, 1)
            for c in range(NC):
                pe.wait_ge(x3T_ready, TC * (c + 1))
                transposes(("x3T", c), ck(x3T, c))
            pe.wait_ge(x3F_ready, NC)
            o, s = fill(("route",))
            for t in range(NT):
                mm = pe.matmul(o[:, t * E1:(t + 1) * E1], tl(x3F, t), w_r[:, :], start=True, stop=True)
            mm.then_inc(s, 1)
            pe.wait_ge(onehot_ready, 1)
            o, s = fill(("cum",))
            oh = onehot[:, :, :].rearrange("p e t -> p (e t)")
            pe.matmul(tl(o, 0), triu[:, :], oh, start=True, stop=True)
            pe.matmul(tl(o, 1), onesb[:, :], oh, start=True, stop=True).then_inc(s, 1)
            for n in range(NST // TC):
                if n == 0:
                    pe.wait_ge(ein_loaded, 16 * (NST // TC))
                transposes(("einT", n), einT[n // 4][:, (n % 4) * CH:(n % 4 + 1) * CH])
            pe.wait_ge(ld_e, 64)
            for e in range(E1):
                pe.wait_ge(einF_ready, NST // TC)
                for m in range(FM):
                    o, s = fill(("h1", e, m))
                    for (i, lo, hi) in pieces(e):
                        mm = pe.matmul(o[:, lo - e * CAP:hi - e * CAP], w1[e // 4][:, (e % 4) * DFF + m * P:(e % 4) * DFF + (m + 1) * P],
                                       einF[i][:, lo - i * S:hi - i * S], start=True, stop=True)
                    mm.then_inc(s, 1)
                pe.wait_ge(relu_act, 2 * (e + 1))
                pe.wait_ge(relu_dve, 2 * (e + 1))
                o, s = fill(("eo", e))
                for j in range(3):
                    n = P if j < 2 else 64
                    for k in range(FM):
                        w = w2[e // 4][:, ((e % 4) * FM + k) * D:((e % 4) * FM + k + 1) * D]
                        mm = pe.matmul(o[0:n, j * P:(j + 1) * P], hE[e % 2][:, k * CAP + j * P:k * CAP + j * P + n], w,
                                       start=(k == 0), stop=(k == FM - 1))
                mm.then_inc(s, 1)

        @block.scalar
        def _(act):
            for i in range(1, NC + 2):
                if i <= NC:
                    c = i - 1
                    if c == 0:
                        act.wait_ge(ld_a, 32)
                        act.wait_ge(ld_a1, 32)
                    for m in range(4):
                        o = full(act, ("xr", c, m))
                        dst = ck(xin[m], c) if m < 2 else ck(gated[m - 2], c)
                        act.activation(dst, o, ACT.Silu, bias=b_in[:, m:m + 1]).then_inc(silu_ready, 1)
                if i >= 2:
                    c = i - 2
                    o = full(act, ("dt", c))
                    act.activation(ck(sp_abs, c), o, ACT.Identity, bias=b_dt[:, :]).then_inc(u_ready, 1)
            act.wait_ge(ld_a2, 16 * 7)
            act.activation(a_exp[NSTATE:P, :], a_log[NSTATE:P, :], ACT.Exp).then_inc(aexp_ready, 1)
            for i in range(NC + 2):
                if i < NC:
                    act.wait_ge(absu_ready, i + 1)
                    act.activation(ck(sp_abs, i), ck(sp_abs, i), ACT.Exp, scale=-1.0).then_inc(expu_ready, 1)
                    act.wait_ge(expu_ready, i + 1)
                    act.activation(ck(sp_abs, i), ck(sp_abs, i), ACT.Ln, bias=1.0).then_inc(sp_ready, 1)
                if 1 <= i <= NC:
                    c = i - 1
                    o = full(act, ("mean", c))
                    if c == 0:
                        act.wait_ge(aneg_ready, 1)
                    act.activation(ck(aF, c)[0:NSTATE, :], o[NSTATE:P, :], ACT.Exp, scale=a_neg[NSTATE:P, :]).then_inc(decay_ready, 1)
            for c in range(NC):
                o = full(act, ("x1T", c))
                act.activation(ck(x1F, c), o, ACT.Copy).then_inc(x1F_ready, 1)

            for c in range(NC + 1):
                if c < NC:
                    o = full(act, ("kvc", c))
                    act.activation(ck(kvcF[0], c)[0:32, :], o[0:32, :], ACT.Copy).then_inc(kvc_ready, 1)
                    act.activation(ck(kvcF[1], c)[0:32, :], o[32:64, :], ACT.Copy).then_inc(kvc_ready, 1)
                if c >= 1:
                    for n in range(2):
                        i = 2 * (c - 1) + n
                        act.wait_ge(sum_ready, i + 1)
                        act.activation(parts(i)[:, 0, :], ck(rope_a(n), c - 1), ACT.Copy).then_inc(part_ready, 1)
                    for n in range(2):
                        i = 2 * (c - 1) + n
                        act.wait_ge(rest_ready, i + 1)
                        act.activation(parts(i)[:, 1, :], ck(rope_b(n), c - 1), ACT.Copy).then_inc(part_ready, 1)
                if c < NC:
                    o = full(act, ("v", c))
                    act.activation(ck(vT, c), o, ACT.Copy).then_inc(vT_ready, 1)

            def head(hv, h, lap=0):
                for g in range(NT):
                    if h * NT + g >= PR:
                        act.wait_ge(pv_done, hv * NT + (g - PR + 1))
                    for c in range(NC):
                        u = g * NC + c
                        act.wait_ge(st_full, hv * 64 + u + 1)
                        act.activation(prob[g % PR][:, c * CH:(c + 1) * CH], bank[u % STB][:, :], ACT.Exp,
                                       scale=1.0 / math.sqrt(DH)).then_inc(exp_done, 1)
                        if h >= 1 and g == 1 and c == 1:
                            take_out(hv - 1, h - 1, lap)

            def take_out(hv, h, lap=0):
                act.wait_ge(pv_done, (hv + 1) * NT)
                if h >= 2:
                    act.wait_ge(pv_stored[h % 2], (h // 2 + 2 * lap) * 16)
                act.activation(ck(pv_sb, h % 2), pvps[:, :], ACT.Copy).then_inc(pv_out, 1)

            for h in range(4):
                head(h, h)
            with act.Fori(1, LOOPED // 4) as it:
                for j in range(4):
                    head(it * 4 + j, 4 + j, it - 1)
            for h in range(LOOPED, H):
                head(h, h)
            take_out(H - 1, H - 1)

            for c in range(NC):
                o = full(act, ("xnT", c))
                act.activation(ck(xnF, c), o, ACT.Copy).then_inc(xnF_ready, 1)
            act.wait_ge(gexp_in, 1)
            act.activation(g_s[:, 2, :], g_s[:, 1, :], ACT.Exp).then_inc(gexp_ready, 1)
            act.activation(g4[:, 3, :, :], g4[:, 2, :, :], ACT.Exp).then_inc(gexp_ready, 1)
            for c in range(NC):
                for w in range(2):
                    for k in range(2):
                        o = full(act, ("ffn", c, 4 * w + k))
                        if c >= 1:
                            act.wait_ge(hid_ready, 4 * (c - 1) + 2 * w + k + 1)
                        act.activation(act_ff[:, (2 * w + k) * CH:(2 * w + k + 1) * CH], o, ACT.Silu).then_inc(silu0_ready, 1)
            act.wait_ge(ld_d, 112)
            for c in range(NC):
                o = full(act, ("xrT", c))
                act.activation(ck(xrF, c), o, ACT.Copy, scale=gamma[:, :]).then_inc(xrF_ready, 1)
            for c in range(NC):
                for key, dst, f in (("pk", kF, ACT.Copy), ("pq", qF, ACT.Copy), ("pa", decF, ACT.Sigmoid), ("pg", gsF, ACT.Silu)):
                    o = full(act, (key, c))
                    act.activation(ck(dst, c), o, f).then_inc(l1_act, 1)
            for c in range(NC):
                o = full(act, ("x3T", c))
                act.activation(ck(x3F, c), o, ACT.Copy).then_inc(x3F_ready, 1)
            act.wait_ge(rexp_in, 1)
            act.activation(r8[:, 2, :, :], r8[:, 1, :, :], ACT.Exp).then_inc(rexp_ready, 1)
            for n in range(NST // TC):
                o = full(act, ("einT", n))
                act.activation(ck(einF[n // 4], n % 4), o, ACT.Copy).then_inc(einF_ready, 1)
            for e in range(E1):
                for m in (0, 2):
                    o = full(act, ("h1", e, m))
                    if e >= 2 and m == 0:
                        full(act, ("eo", e - 2))
                    act.activation(hE[e % 2][:, m * CAP:(m + 1) * CAP], o[:, 0:CAP], ACT.Relu).then_inc(relu_act, 1)
                if e >= 1:
                    take_expert(act, e - 1)
            take_expert(act, E1 - 1)

        @block.vector
        def _(v):
            steps = [0]

            def link(ins):
                steps[0] += 1
                ins.then_inc(dve_step, 1)
                v.wait_ge(dve_step, steps[0])

            def stats(k, src, c):
                n = norms.index((k, c))
                for j in range(TC):
                    ins = v.bn_stats(bn[:, n % 2, j, :], tl(src, c * TC + j))
                    if j < TC - 1:
                        ins.then_inc(dve_step, 1)
                        steps[0] += 1
                link(ins)
                for j in range(TC):
                    ins = v.bn_aggr(mv[:, n, j, :], bn[:, n % 2, j, :])
                    if j < TC - 1:
                        ins.then_inc(dve_step, 1)
                        steps[0] += 1
                link(ins)
                mean, vr = mv[:, n, :, 0], mv[:, n, :, 1]
                if k in (N_RMSX, N_RMSO, N_RMS1):
                    link(v.tensor_tensor(msq[:, n, :], mean, mean, ALU.mult))
                    eps = RMS1_EPS / D if k == N_RMS1 else RMS0_EPS
                    link(v.scalar_tensor_tensor(out=var[:, n, :], in0=msq[:, n, :], scalar=eps, in1=vr, op0=ALU.add, op1=ALU.add))
                else:
                    link(v.tensor_scalar(var[:, n, :], vr, LN_EPS, None, ALU.add))
                v.tensor_scalar(rs[:, n, :].bitcast(I32), var[:, n, :].bitcast(I32), -0.5, RSQRT_MAGIC,
                                ALU.mult, ALU.add).then_inc(guess_ready, 1)

            def root(k, c):
                n = norms.index((k, c))
                v.wait_ge(rstd_ready, n + 1)
                return mv[:, n, :, 0], rs[:, n, :]

            def normalize(k, c, dst, src, done):
                mean, r = root(k, c)
                for j in range(TC):
                    v.tensor_scalar(tl(dst, c * TC + j), tl(src, c * TC + j), mean[:, j:j + 1], r[:, j:j + 1],
                                    ALU.subtract, ALU.mult).then_inc(done, 1)

            v.memset(ones[:, :], 1.0).then_inc(const_dve, 1)
            v.memset(mean_w[:, :], 1.0 / D).then_inc(const_dve, 1)
            v.memset(onesb[:, :], 1.0).then_inc(const_dve, 1)
            v.memset(zeros[:, :], 0.0).then_inc(zeroed, 1)
            v.memset(keep_scan[:, :], 1.0).then_inc(const_dve, 1)
            v.wait_ge(const_dve, 4)
            v.memset(keep_scan[:, :].rearrange("p (e t) -> p e t", t=NT)[:, :, 0:1], 0.0).then_inc(const_dve, 1)

            for i in range(NC + 2):
                if i < NC:
                    o = full(v, ("xT", i))
                    v.tensor_copy(ck(x0F, i), o).then_inc(x0F_ready, 1)
                if i >= 2:
                    c = i - 2
                    v.wait_ge(u_ready, c + 1)
                    v.tensor_scalar(ck(sp_relu, c), ck(sp_abs, c), 0.0, None, ALU.max).then_inc(relu_ready, 1)
                    v.wait_ge(relu_ready, c + 1)
                    v.scalar_tensor_tensor(out=ck(sp_abs, c), in0=ck(sp_abs, c), scalar=-1.0, in1=ck(sp_abs, c),
                                           op0=ALU.mult, op1=ALU.max).then_inc(absu_ready, 1)
            v.wait_ge(aexp_ready, 1)
            v.tensor_scalar(a_neg[NSTATE:P, :], a_exp[NSTATE:P, :], -1.0, None, ALU.mult).then_inc(aneg_ready, 1)
            for i in range(NC + 3):
                for c in ((0, 1) if i == 0 else (i + 1,)) if i < NC - 1 else ():
                    v.wait_ge(sp_ready, c + 1)
                    v.tensor_tensor(ck(sp_relu, c), ck(sp_relu, c), ck(sp_abs, c), ALU.add).then_inc(delta_ready, 1)
                if i < NC:
                    o = full(v, ("bx", i))
                    v.wait_ge(ld_a2, 16 * 7)
                    v.tensor_scalar(ck(bxF, i)[0:NSTATE, :], o[0:NSTATE, :], b_xp[:, :], None, ALU.add).then_inc(bx_ready, 1)
                    v.wait_ge(decay_ready, i + 1)
                    v.wait_ge(bx_ready, i + 1)
                    if i >= 1:
                        v.wait_ge(state_ready, i)
                    before = 0.0 if i == 0 else stF[0:NSTATE, i * CH - 1:i * CH]
                    v.tensor_tensor_scan(ck(stF, i)[0:NSTATE, :], ck(aF, i)[0:NSTATE, :], ck(bxF, i)[0:NSTATE, :],
                                         before, ALU.mult, ALU.add).then_inc(state_ready, 1)
                if 1 <= i <= NC:
                    c = i - 1
                    o = full(v, ("ssum", c))
                    v.wait_ge(gated_ready, 2 * (c + 1))
                    for k in range(2):
                        v.tensor_tensor(ck(gated[k], c), o, ck(gated[k], c), ALU.mult).then_inc(y_ready, 1)
                if 2 <= i <= NC + 1:
                    c = i - 2
                    o = full(v, ("outA", c))
                    v.wait_ge(pre_step, 3)
                    v.tensor_tensor(ck(x1T, c), o, ck(pre, c), ALU.add).then_inc(resid_ready, 1)
                    v.wait_ge(resid_ready, c + 1)
                    stats(N_LN1, x1T, c)
                if i >= 3:
                    normalize(N_LN1, i - 3, x1T, x1T, x1T_ready)

            for c in range(NC + 1):
                for n, (key, keyr) in enumerate((("q", "qr"), ("k", "kr")) if c < NC else ()):
                    i = 2 * c + n
                    o = full(v, (key, c))
                    v.wait_ge(ld_b, 112)
                    v.tensor_tensor(ck(rope_a(n), c), o, ck(cosF, c), ALU.mult).then_inc(rope_ready, 1)
                    o = full(v, (keyr, c))
                    v.tensor_tensor(ck(rope_b(n), c), o, ck(sinF, c), ALU.mult).then_inc(rope_ready, 1)
                    v.wait_ge(rope_ready, 2 * i + 2)
                    v.tensor_tensor(ck(rope_a(n), c), ck(rope_a(n), c), ck(rope_b(n), c), ALU.add).then_inc(sum_ready, 1)
                for n in range(2) if c >= 1 else ():
                    i = 2 * (c - 1) + n
                    v.wait_ge(rest_ready, i + 1)
                    v.wait_ge(part_ready, 4 * (c - 1) + n + 3)
                    v.tensor_tensor(parts(i)[:, 2, :], ck(rope_b(n), c - 1), parts(i)[:, 1, :], ALU.subtract).then_inc(third_ready, 1)

            def reduce_half(hv, h, t, f):
                v.wait_ge(mx_full, hv * 32 + (2 * t + f + 1))
                v.tensor_reduce(maxes[:, h % 2, t, f:f + 1], maxps[f][:, :], AX.X, ALU.max).then_inc(mx_free, 1)

            def combine(hv, h):
                v.wait_ge(mx_free, hv * 32 + 32)
                if h >= 1:
                    v.wait_ge(mparts_ready, hv)
                v.tensor_tensor(mneg[:, :], maxes[:, h % 2, :, 0], maxes[:, h % 2, :, 1], ALU.max).then_inc(mcomb, 1)
                v.wait_ge(mcomb, hv * 2 + 1)
                v.tensor_scalar(mparts[:, 0:NT], mneg[:, :], -1.0, None, ALU.mult).then_inc(mcomb, 1)
                v.wait_ge(mcomb, hv * 2 + 2)
                v.scalar_tensor_tensor(out=mparts[:, NT:2 * NT], in0=mneg[:, :], scalar=-1.0, in1=mparts[:, 0:NT],
                                       op0=ALU.mult, op1=ALU.subtract).then_inc(mparts_ready, 1)

            def turn(hv, h):
                v.wait_ge(mt_full, hv + 1)
                if h >= 1:
                    v.wait_ge(mrows_placed, hv * 32)
                v.tensor_copy(mrows[:, :], maxps[1][0:2 * NT, 0:P // 2].bitcast(BF16)).then_inc(mrows_ready, 1)

            def head(hv, h, lap=0):
                for g in range(NT):
                    t, k = (g + AHEAD, 1) if g + AHEAD < NT else (g + AHEAD - NT, 2)
                    more = h + k < H
                    if more:
                        reduce_half(hv + k, h + k, t, 0)
                    if g == NT + 1 - AHEAD and h + 1 < H:
                        turn(hv + 1, h + 1)
                    if more:
                        reduce_half(hv + k, h + k, t, 1)
                    if t == NT - 1 and h + 1 < H:
                        combine(hv + 1, h + 1)

            for t in range(NT):
                reduce_half(0, 0, t, 0)
                reduce_half(0, 0, t, 1)
            combine(0, 0)
            for t in range(AHEAD):
                reduce_half(1, 1, t, 0)
                if t == 1:
                    turn(0, 0)
                reduce_half(1, 1, t, 1)
            for h in range(4):
                head(h, h)
            with v.Fori(1, LOOPED // 4) as it:
                for j in range(4):
                    head(it * 4 + j, 4 + j, it - 1)
            for h in range(LOOPED, H):
                head(h, h)

            for c in range(NC):
                v.wait_ge(attn_loaded[c], 32)
                link(v.reciprocal(ck(denF, c), ck(denF, c)))
                v.tensor_tensor(ck(numF, c), ck(numF, c), ck(denF, c), ALU.mult).then_inc(attn_ready, 1)
            v.wait_ge(ld_c, 192)
            for i in range(NC + 1):
                if i < NC:
                    o = full(v, ("wo", i))
                    v.tensor_tensor(ck(xnT, i), o, ck(x1T, i), ALU.add).then_inc(resid_ready, 1)
                    v.wait_ge(resid_ready, NC + i + 1)
                    stats(N_RMSX, xnT, i)
                if i >= 1:
                    c = i - 1
                    _, r = root(N_RMSX, c)
                    for j in range(TC):
                        x = tl(xnT, c * TC + j)
                        v.scalar_tensor_tensor(out=x, in0=x, scalar=r[:, j:j + 1], in1=bc["n1"][:, :],
                                               op0=ALU.mult, op1=ALU.mult).then_inc(xnT_ready, 1)

            def wide(x, n=EPG):
                return x.unsqueeze(2).broadcast_to([P, NT, n])

            def first_best(score, rank, rev, n, top, hit, oh):
                link(v.tensor_reduce(top, score, AX.X, ALU.max))
                link(v.tensor_tensor(hit, score, wide(top, n), ALU.is_equal))
                link(v.tensor_tensor(hit, hit, rev[:, :].unsqueeze(1).broadcast_to([P, NT, n]), ALU.mult))
                link(v.tensor_reduce(rank, hit, AX.X, ALU.max))
                link(v.tensor_tensor(oh, hit, wide(rank, n), ALU.is_equal))

            o = full(v, ("gate",))
            v.tensor_tensor(gl[:, :, :], o[:, 0:NT * 10].rearrange("p (t n) -> p t n", n=10),
                            b_gate[:, :].unsqueeze(1).broadcast_to([P, NT, 10]), ALU.add).then_inc(gate_ready, 1)
            v.wait_ge(gate_ready, 1)
            g0, g1 = gl[:, :, 0], gl[:, :, 1]
            second, diff, ediff, first_, top, summ, rank, top2, rank2 = (g_s[:, i, :] for i in range(9))
            link(v.tensor_tensor(second, g1, g0, ALU.is_gt))
            link(v.tensor_scalar(first_, second, -1.0, 1.0, ALU.mult, ALU.add))
            link(v.tensor_tensor(diff, g1, g0, ALU.subtract))
            link(v.tensor_scalar(summ, diff, -1.0, None, ALU.mult))
            link(v.tensor_tensor(diff, diff, summ, ALU.min))
            e4, tmp4, z4, x4, hit4, oh4, e4b, hit4b, oh4b = (g4[:, i, :, :] for i in range(9))
            link(v.tensor_tensor(e4, gl[:, :, 2:6], wide(first_), ALU.mult))
            link(v.tensor_tensor(tmp4, gl[:, :, 6:10], wide(second), ALU.mult))
            link(v.tensor_tensor(e4, e4, tmp4, ALU.add))
            first_best(e4, rank, rev4, EPG, top, hit4, oh4)
            v.tensor_tensor(z4, e4, wide(top), ALU.subtract).then_inc(gexp_in, 1)
            link(v.scalar_tensor_tensor(out=e4b, in0=oh4, scalar=-BIG, in1=e4, op0=ALU.mult, op1=ALU.add))
            first_best(e4b, rank2, rev4, EPG, top2, hit4b, oh4b)
            link(v.tensor_tensor(oh4, oh4, oh4b, ALU.add))
            v.wait_ge(gexp_ready, 2)
            link(v.tensor_reduce(summ, x4, AX.X, ALU.add))
            link(v.scalar_tensor_tensor(out=summ, in0=ediff, scalar=1.0, in1=summ, op0=ALU.add, op1=ALU.mult))
            link(v.reciprocal(summ, summ))
            link(v.tensor_tensor(x4, x4, oh4, ALU.mult))
            link(v.tensor_tensor(x4, x4, wide(summ), ALU.mult))
            link(v.tensor_tensor(wtop[:, :, 0:EPG], x4, wide(first_), ALU.mult))
            link(v.tensor_tensor(wtop[:, :, EPG:], x4, wide(second), ALU.mult))

            for c in range(NC):
                for w in range(2):
                    for k in range(2):
                        i = 2 * w + k
                        o = full(v, ("ffn", c, 4 * w + 2 + k))
                        v.wait_ge(silu0_ready, 4 * c + i + 1)
                        v.tensor_tensor(ck(hid[w][k], c), o, act_ff[:, i * CH:(i + 1) * CH], ALU.mult).then_inc(hid_ready, 1)

            for i in range(NC + 3):
                if i < NC:
                    o = full(v, ("sh", i))
                    v.tensor_tensor(ck(oT, i), o, ck(xnT, i), ALU.add).then_inc(acc_ready, 1)
                    n = 33 * i + 1
                    v.wait_ge(acc_ready, n)
                    for j in range(TC):
                        t = i * TC + j
                        for e in range(E0):
                            if e % 4 == 0:
                                o = full(v, ("rt", t, e // 4))
                            v.scalar_tensor_tensor(out=tl(oT, t), in0=tl(o, e % 4), scalar=wtop[:, t, e:e + 1], in1=tl(oT, t),
                                                   op0=ALU.mult, op1=ALU.add).then_inc(acc_ready, 1)
                            n += 1
                            v.wait_ge(acc_ready, n)
                    stats(N_RMSO, oT, i)
                if 1 <= i <= NC:
                    c = i - 1
                    _, r = root(N_RMSO, c)
                    for j in range(TC):
                        x = tl(oT, c * TC + j)
                        link(v.scalar_tensor_tensor(out=x, in0=x, scalar=r[:, j:j + 1], in1=bc["n2"][:, :],
                                                    op0=ALU.mult, op1=ALU.mult))
                    link(v.tensor_tensor(ck(oT, c), ck(oT, c), ck(x1T, c), ALU.add))
                    stats(N_LN2, oT, c)
                if 2 <= i <= NC + 1:
                    c = i - 2
                    normalize(N_LN2, c, x2T, oT, x2T_ready)
                    v.wait_ge(x2T_ready, TC * (c + 1))
                    stats(N_RMS1, x2T, c)
                if i >= 3:
                    c = i - 3
                    _, r = root(N_RMS1, c)
                    for j in range(TC):
                        v.tensor_scalar(tl(xrT, c * TC + j), tl(x2T, c * TC + j), r[:, j:j + 1], None, ALU.mult).then_inc(xrT_ready, 1)

            for i in range(NC + 2):
                if i < NC:
                    o = full(v, ("pv", i))
                    v.wait_ge(l1_act, 4 * i + 1)
                    v.tensor_tensor(ck(kvF, i), o, ck(kF, i), ALU.mult).then_inc(kv_ready, 1)
                    v.wait_ge(kv_ready, i + 1)
                    v.wait_ge(l1_act, 4 * i + 4)
                    before = 0.0 if i == 0 else hsF[:, i * CH - 1:i * CH]
                    v.tensor_tensor_scan(ck(hsF, i), ck(decF, i), ck(kvF, i), before, ALU.mult, ALU.add).then_inc(hs_ready, 1)
                    v.wait_ge(hs_ready, i + 1)
                    link(v.tensor_tensor(ck(yF, i), ck(hsF, i), ck(qF, i), ALU.mult))
                    v.tensor_tensor(ck(yF, i), ck(yF, i), ck(gsF, i), ALU.mult).then_inc(y1_ready, 1)
                if 1 <= i <= NC:
                    c = i - 1
                    o = full(v, ("wo1", c))
                    v.tensor_tensor(ck(x3T, c), o, ck(x2T, c), ALU.add).then_inc(resid_ready, 1)
                    v.wait_ge(resid_ready, 2 * NC + c + 1)
                    stats(N_LN3, x3T, c)
                if i >= 2:
                    normalize(N_LN3, i - 2, x3T, x3T, x3T_ready)

            lg, z8, x8, hit8, oh8 = (r8[:, i, :, :] for i in range(5))
            top, rank, ssum, pmax, place, base, kept, at, factor, tmp = (r_s[:, i, :] for i in range(10))
            o = full(v, ("route",))
            v.tensor_copy(lg, o[:, 0:NT * E1].rearrange("p (t e) -> p t e", e=E1)).then_inc(gate_ready, 1)
            v.wait_ge(gate_ready, 2)
            v.wait_ge(const_pool, 7)
            first_best(lg, rank, rev8, E1, top, hit8, oh8)
            v.tensor_tensor(z8, lg, wide(top, E1), ALU.subtract).then_inc(rexp_in, 1)
            oh_et = oh8.rearrange("p t e -> p e t")
            v.tensor_copy(onehot[:, :, :], oh_et).then_inc(onehot_ready, 1)
            link(v.tensor_tensor(hit8, oh8, base8[:, :].unsqueeze(1).broadcast_to([P, NT, E1]), ALU.mult))
            link(v.tensor_reduce(base, hit8, AX.X, ALU.add))
            v.wait_ge(rexp_ready, 1)
            link(v.tensor_reduce(ssum, x8, AX.X, ALU.add))
            link(v.reciprocal(pmax, ssum))
            o = full(v, ("cum",))
            tot, inc, cum, sel = (et[:, i, :, :] for i in range(4))
            fl = lambda x: x.rearrange("p e t -> p (e t)")
            link(v.tensor_copy(fl(tot), tl(o, 1)))
            v.tensor_copy(fl(cum), tl(o, 0)).then_inc(comb_ready, 1)
            v.wait_ge(comb_ready, 1)
            link(v.tensor_tensor_scan(fl(inc), keep_scan[:, :], fl(tot), 0.0, ALU.mult, ALU.add))
            link(v.tensor_tensor(inc, inc, tot, ALU.subtract))
            link(v.tensor_tensor(cum, cum, inc, ALU.add))
            link(v.tensor_tensor(sel, cum, oh_et, ALU.mult))
            link(v.tensor_reduce(place, sel.rearrange("p e t -> p t e"), AX.X, ALU.add))
            link(v.tensor_scalar(kept, place, float(CAP) + 0.5, None, ALU.is_lt))
            link(v.scalar_tensor_tensor(out=at, in0=place, scalar=-1.0, in1=base, op0=ALU.add, op1=ALU.add))
            link(v.tensor_tensor(at, at, spare[:, :], ALU.subtract))
            link(v.tensor_tensor(at, at, kept, ALU.mult))
            link(v.tensor_tensor(at, at, spare[:, :], ALU.add))
            v.tensor_copy(dest[:, :], at).then_inc(dest_ready, 1)
            link(v.scalar_tensor_tensor(out=tmp, in0=pmax, scalar=-1.0, in1=kept, op0=ALU.add, op1=ALU.mult))
            link(v.tensor_scalar(factor, tmp, 1.0, None, ALU.add))
            for e in range(E1):
                for m in (1, 3):
                    o = full(v, ("h1", e, m))
                    if e >= 2 and m == 1:
                        full(v, ("eo", e - 2))
                    v.tensor_scalar(hE[e % 2][:, m * CAP:(m + 1) * CAP], o[:, 0:CAP], 0.0, None, ALU.max).then_inc(relu_dve, 1)
            for i in range(NC + 1):
                if i < NC:
                    for j in range(TC):
                        t = i * TC + j
                        v.wait_ge(gathered, 16 * NT)
                        link(v.scalar_tensor_tensor(out=tl(finT, t), in0=tl(combT, t), scalar=factor[:, t:t + 1], in1=tl(x3T, t),
                                                    op0=ALU.mult, op1=ALU.add))
                    stats(N_LN4, finT, i)
                if i >= 1:
                    normalize(N_LN4, i - 1, yT, finT, out_ready)

        @block.gpsimd
        def _(g):
            steps = [0]

            def link(ins):
                steps[0] += 1
                ins.then_inc(pool_step, 1)
                g.wait_ge(pool_step, steps[0])

            def refine(k, c):
                n = norms.index((k, c))
                g.wait_ge(guess_ready, n + 1)
                y, x, w = rs[:, n, :], var[:, n, :], nw[:, 0, :]
                for i in range(3):
                    link(g.tensor_tensor(w, y, y, ALU.mult))
                    link(g.tensor_tensor(w, w, x, ALU.mult))
                    link(g.tensor_scalar(w, w, -0.5, 1.5, ALU.mult, ALU.add))
                    ins = g.tensor_tensor(y, y, w, ALU.mult)
                    if i < 2:
                        link(ins)
                ins.then_inc(rstd_ready, 1)
                g.wait_ge(rstd_ready, n + 1)

            link(g.memset(ident[:, :], 0.0))
            g.affine_select(out=ident[:, :], in_=ident[:, :], compare_op=ALU.not_equal, fill=1.0, base=0,
                            pattern=[[-1, P]], channel_multiplier=1).then_inc(const_pool, 1)
            g.wait_ge(const_pool, 1)
            g.tensor_copy(identb[:, :], ident[:, :]).then_inc(const_pool, 1)
            link(g.memset(triu[:, :], 1.0))
            g.affine_select(out=triu[:, :], in_=triu[:, :], compare_op=ALU.is_ge, fill=0.0, base=0,
                            pattern=[[1, P]], channel_multiplier=-1).then_inc(const_pool, 1)
            for t, n, lo, step in ((rev4, EPG, EPG, -1), (rev8, E1, E1, -1), (base8, E1, 0, CAP)):
                for e in range(n):
                    ins = g.memset(t[:, e:e + 1], float(lo + e * step))
                    if e < n - 1:
                        link(ins)
                ins.then_inc(const_pool, 1)
            link(g.iota(token_i[:, :], pattern=[[P, NT]], base=SLOTS, channel_multiplier=1))
            g.tensor_copy(spare[:, :], token_i[:, :]).then_inc(const_pool, 1)
            g.memset(vh[:, :, :, :], 1.0).then_inc(const_pool, 1)

            def rows(x):
                return x[:, :].unsqueeze(1).broadcast_to([P, NT, D])

            for c in range(NC):
                g.wait_ge(ld_x[c], 16)
            g.wait_ge(ld_a2, 16 * 7)
            x3 = x0T[:, :].rearrange("p (t d) -> p t d", d=D)
            p3 = pre[:, :].rearrange("p (t d) -> p t d", d=D)
            for c in range(NC):
                g.wait_ge(silu_ready, 4 * (c + 1))
                for k in range(2):
                    g.tensor_tensor(ck(gated[k], c), ck(gated[k], c), ck(xin[k], c), ALU.mult).then_inc(gated_ready, 1)
            g.tensor_tensor(p3, x3, rows(bc["d"]), ALU.mult).then_inc(pre_step, 1)
            g.wait_ge(pre_step, 1)
            g.tensor_tensor(p3, p3, rows(bc["bo"]), ALU.add).then_inc(pre_step, 1)
            g.wait_ge(pre_step, 2)
            g.tensor_tensor(pre[:, :], pre[:, :], x0T[:, :], ALU.add).then_inc(pre_step, 1)

            g.wait_ge(ld_b, 112)
            for w, wr in ((wq, wqr), (wk, wkr)):
                src = w[:, :].rearrange("p (n two) -> p n two", two=2)
                dst = wr[:, :].rearrange("p (n two) -> p n two", two=2)
                g.tensor_scalar(dst[:, :, 0], src[:, :, 1], -1.0, None, ALU.mult).then_inc(rot_ready, 1)
                g.tensor_copy(dst[:, :, 1], src[:, :, 0]).then_inc(rot_ready, 1)

            for c in range(NC):
                refine(N_LN1, c)

            g.wait_ge(x1T_ready, NT)
            for b in range(HB):
                g.memset(slot[4 + b // 2][64:96, (b % 2) * 1024:(b % 2) * 1024 + 1024], ONE_PAIR).then_inc(ones_ready, 1)
                g.wait_ge(ones_ready, b + 1)

            for c in range(NC):
                for n in range(2):
                    i = 2 * c + n
                    g.wait_ge(part_ready, 4 * c + n + 1)
                    g.tensor_tensor(ck(rope_b(n), c), ck(rope_a(n), c), parts(i)[:, 0, :], ALU.subtract).then_inc(rest_ready, 1)

            g.wait_ge(vT_ready, NC)
            g.wait_ge(const_pool, 8)

            def head(hv, h, lap=0):
                if h >= 2:
                    g.wait_ge(pv_done, (hv - 1) * NT)
                g.tensor_copy(vh[:, h % 2, :, 0:DH],
                              vT[:, :].rearrange("p (t d) -> p t d", d=D)[:, :, bass.ds(hv * DH, DH)]).then_inc(vh_ready, 1)

            head(0, 0)
            head(1, 1)
            with g.Fori(1, H // 2) as it:
                for j in range(2):
                    head(it * 2 + j, 2 + j)

            for k, c in norms[NC:-NC]:
                refine(k, c)

            g.wait_ge(zeroed, 17)
            g.wait_ge(x3T_ready, NT)
            g.wait_ge(dest_ready, 1)
            for t in range(NT):
                g.indirect_dma_start(out=disp[:, :], out_offset=bass.IndirectOffsetOnAxis(ap=dest[:, t:t + 1], axis=0),
                                     in_=tl(x3T, t), in_offset=None).then_inc(scattered, 16)
            g.wait_ge(spare_stored, 16)
            for b in range(4):
                g.wait_ge(eo_stored[b], 32 * (E1 // 4))
            for t in range(NT):
                g.indirect_dma_start(out=tl(combT, t), out_offset=None, in_=eout[:, :],
                                     in_offset=bass.IndirectOffsetOnAxis(ap=dest[:, t:t + 1], axis=0)).then_inc(gathered, 16)
            for c in range(NC):
                refine(N_LN4, c)


_INS = [
    "L0_attn_x", "L0_attn_W_in", "L0_attn_b_in", "L0_attn_W_xp", "L0_attn_b_xp", "L0_attn_W_dt", "L0_attn_b_dt",
    "L0_attn_W_out", "L0_attn_b_out", "L0_attn_A_log", "L0_attn_D", "L0_ffn_Wq", "L0_ffn_Wk_c", "L0_ffn_Wv_c",
    "L0_ffn_Wk", "L0_ffn_Wv", "L0_ffn_Wo", "L0_ffn_W_shared_in", "L0_ffn_W_shared_out", "L0_ffn_W1_shared",
    "L0_ffn_W2_experts", "L0_ffn_Wg_gate", "L0_ffn_We_gate", "L0_ffn_group_bias", "L0_ffn_expert_bias",
    "L0_ffn_norm1_w", "L0_ffn_norm2_w", "L1_attn_gamma", "L1_attn_wq", "L1_attn_wk", "L1_attn_wv", "L1_attn_wa",
    "L1_attn_wg", "L1_attn_wo", "L1_ffn_Wr", "L1_ffn_W1", "L1_ffn_W2",
]


def kernel(**inputs):
    import numpy as np
    import concourse.bacc as bacc
    from concourse.bass_utils import run_bass_kernel_spmd as run

    nc = bacc.Bacc("TRN2", target_bir_lowering=False, num_devices=1)
    arrays, args = {}, {}
    for name in _INS:
        arrays[f"in_{name}"] = np.ascontiguousarray(inputs[name])
    inv_freq = np.float32(1.0) / np.float32(10000.0) ** (np.arange(0, DH, 2, dtype=np.float32) / np.float32(DH))
    angle = np.repeat(inv_freq.astype(np.float32), 2)[:, None] * np.arange(S, dtype=np.float32)[None, :]
    angle = np.tile(angle.astype(np.float32), (H, 1))
    arrays["in_cos"], arrays["in_sin"] = np.cos(angle), np.sin(angle)
    for name, array in arrays.items():
        args[name[3:]] = nc.dram_tensor(name, array.shape, mybir.dt.from_np(array.dtype), kind="ExternalInput").ap()
    out = nc.dram_tensor("out_0", (1, S, D), F32, kind="ExternalOutput").ap()
    scratch = (
        nc.dram_tensor("qk_split", (2, 3, P, S), BF16).ap(),
        nc.dram_tensor("attn_out", (H * P, CH), F32).ap(),
        nc.dram_tensor("disp", (SLOTS + S, D), F32).ap(),
        nc.dram_tensor("eout", (SLOTS + S, D), F32).ap(),
    )
    build(nc, args, scratch, out)
    r = run(nc, [arrays], core_ids=[0])
    return r.results[0]["out_0"]
```

```python
import math
import struct
from contextlib import ExitStack
from functools import partial

import concourse.bass as bass
from concourse import mybir

F32 = mybir.dt.float32
BF16 = mybir.dt.bfloat16
I32 = mybir.dt.int32
ACT = mybir.ActivationFunctionType
ALU = mybir.AluOpType
AX = mybir.AxisListType

P = 128
D = 128
S = 2048
NT = S // P
CH = 512
NC = S // CH
TC = CH // P
NSTATE = 64
H, DH = 16, 8
HID = 256
E0, EPG = 8, 4
E1, CAP, DFF = 8, 320, 512
SLOTS = E1 * CAP
NST = SLOTS // P
FM = DFF // P
ACC = 1 + TC * E0
LN_EPS, RMS0_EPS, RMS1_EPS = 1e-5, 1e-6, 1e-5
BIG = 1e30
RSQRT_MAGIC = float(0x5F3759DF)
ONE_PAIR = struct.unpack("<f", struct.pack("<I", 0x3F803F80))[0]

TERMS = 72
ROWS = TERMS + 2
HB = 4
AHEAD = 3
PAIRS = 4
PR = 2
STB = 3
RP = 8
LOOPED = 12

N_LN1, N_RMSX, N_RMSO, N_LN2, N_RMS1, N_LN3, N_LN4 = range(7)


def psum_plan():
    first, rest = [], []
    for i in range(4 * NC):
        if i < NC:
            first.append((("xT", i), i % 2))
        if 1 <= i <= NC:
            first += [(("xr", i - 1, m), 2 + m) for m in range(2)]
        if 2 <= i <= NC + 1:
            first.append((("dt", i - 2), 6))
        if i == NC + 1:
            first += [(("xr", c, m), (2 + m + 2 * c) % 4 + 2) for c in (0, 1) for m in (2, 3)]
        if 5 <= i <= NC + 4:
            first += [(("bx", i - 5), (i - 5) % 2), (("mean", i - 5), 7 - (i - 5) % 2)]
        if i == NC + 4:
            first += [(("xr", c, m), (2 + m + 2 * c) % 4 + 2) for c in (2, 3) for m in (2, 3)]
        if 8 <= i <= NC + 7:
            first.append((("ssum", i - 8), i % 2))
        if 9 <= i <= NC + 8:
            first.append((("outA", i - 9), 2 + i - 9))
        if i == 3 * NC:
            first += [(("wT",), 0), (("wkv",), 1)]
        if i >= 3 * NC:
            first.append((("x1T", i - 3 * NC), 6 + i % 2))
    for c in range(NC):
        first += [((key, c), (5 * c + n) % 8) for n, key in enumerate(("q", "qr", "k", "kr", "v"))]
    rest += [(("wo", c), c) for c in range(NC)]
    for c in range(NC + 1):
        if c < NC:
            rest.append((("xnT", c), 4 + c % 2))
        if c >= NC - 1:
            rest.append(((("gateF",), 7), (("gate",), 6))[c - NC + 1])
        if c >= 1:
            rest += [(("ffn", c - 1, m), m) for m in range(8)]
    for t in range(0, NT, 2):
        if t % TC == 0:
            rest.append((("sh", t // TC), (t // TC) % 2))
        rest += [(("rt", t + j, f), 2 + 2 * ((t + f) % 3) + j) for f in range(2) for j in range(2)]
    for c in range(NC + 1):
        if c < NC:
            rest += [(("xrT", c), 6 + c % 2), (("pk", c), 0), (("pv", c), 1), (("pq", c), 2), (("pa", c), 3), (("pg", c), 4)]
        if c >= 1:
            rest.append((("wo1", c - 1), 5))
    rest += [(("x3T", c), 6 + c % 2) for c in range(NC)]
    rest += [(("routeF",), 2), (("route",), 0), (("cum",), 1)]
    rest += [(("einT", n), 2 + n % 2) for n in range(NST // TC)]
    for e in range(E1 + 1):
        if e < E1:
            rest += [(("h1", e, m), 4 + m) for m in range(FM)]
        if e >= 1:
            rest.append((("eo", e - 1), (e - 1) % 2))
    plan, fills = {}, [0] * 8
    for order in (first, rest):
        tenant = [None] * 8
        for key, b in order:
            fills[b] += 1
            plan[key] = (b, fills[b], tenant[b])
            tenant[b] = key
        if order is first:
            last = list(tenant)
    return plan, last


def norm_order():
    order = [(k, c) for k in (N_LN1, N_RMSX) for c in range(NC)]
    for j in range(NC + 5):
        order += [(k, j - lag) for k, lag in ((N_RMS1, 2), (N_RMSO, 0), (N_LN2, 1), (N_LN3, 5)) if 0 <= j - lag < NC]
    return order + [(N_LN4, c) for c in range(NC)]


def build(nc, a, scratch, out):
    plan, before_attention = psum_plan()
    norms = norm_order()
    pool_norms = [(k, c) for k, c in norms if c < NC - 1 and k != N_LN4]
    with ExitStack() as ctx:
        def sb(name, shape, dt=F32):
            return ctx.enter_context(nc.sbuf_tensor(name, shape, dt))

        def sem(name):
            return ctx.enter_context(nc.semaphore(name))

        bank = [ctx.enter_context(nc.psum_tensor(f"bank{i}", [P, CH], F32)) for i in range(3)]
        maxps = [ctx.enter_context(nc.psum_tensor(f"maxps{i}", [P, 2 * CH], F32)) for i in range(2)]
        pvps = ctx.enter_context(nc.psum_tensor("pvps", [P, CH], F32))
        bank_ap = [bank[0][:, :], bank[1][:, :], bank[2][:, :], maxps[0][:, 0:CH], maxps[0][:, CH:],
                   maxps[1][:, 0:CH], maxps[1][:, CH:], pvps[:, :]]

        slot = [sb(f"slot{i}", [P, S]) for i in range(18)]

        def two(i):
            return [slot[i], slot[i + 1]]

        x0T, x0F = slot[0], slot[1]
        xin, gated = two(2), two(4)
        sp_abs, sp_relu = slot[6], slot[7]
        aF, bxF, stF = slot[8], slot[9], slot[10]
        pre, x1T, x1F = slot[11], slot[12], slot[1]
        cosF, sinF = slot[13], slot[14]
        vT = slot[15]
        rope_t = [slot[6], slot[7]]
        rope_s = slot[10]
        heads_q = [slot[2 + i // 2][:, (i % 2) * 1024:(i % 2) * 1024 + 1024].bitcast(BF16) for i in range(HB)]
        heads_k = [slot[4 + i // 2][:, (i % 2) * 1024:(i % 2) * 1024 + 1024].bitcast(BF16) for i in range(HB)]
        prob = [slot[16], slot[17]]
        copied = slot[0]
        running = [slot[10 + i // PAIRS][:, (i % PAIRS) * CH:(i % PAIRS + 1) * CH] for i in range(2 * PAIRS)]
        pv_sb = slot[0][:, :].rearrange("p (k b q) -> p k b q", k=2, b=2)
        numF, rdenF = slot[6], slot[7]
        xnT, xnF = slot[8], slot[1]
        act_ff = slot[9]
        hid = [two(2), two(4)]
        oT = slot[10]
        x2T, xrT, xrF = slot[0], slot[11], slot[1]
        qF, kvF, decF, gsF, kF, hsF, yF = slot[13], slot[6], slot[7], slot[2], slot[3], slot[4], slot[5]
        x3T, x3F = slot[12], slot[1]
        w1 = [slot[14], slot[15]]
        w2 = [slot[16], slot[17]]
        einT = [slot[2], slot[3]]
        einF = [slot[4], slot[5]]
        hE = [slot[6], slot[7]]
        eoT = slot[8]
        combT, finT, yT = slot[9], slot[10], slot[11]

        w_in = sb("w_in", [P, 512])
        w_xp = sb("w_xp", [P, 2, NSTATE])
        w_dt = sb("w_dt", [P, 2, D])
        w_out = sb("w_out", [P, 2, D])
        b_in = sb("b_in", [P, 4])
        b_xp = sb("b_xp", [NSTATE, 1])
        b_dt = sb("b_dt", [P, 1])
        a_log = sb("a_log", [P, 1])
        a_exp = sb("a_exp", [P, 1])
        a_neg = sb("a_neg", [P, 1])
        bc = {n: sb(f"bc_{n}", [P, D]) for n in ("d", "bo", "n1", "n2")}
        wq = sb("wq", [P, D])
        wqr = sb("wqr", [P, D])
        wkvc = sb("wkvc", [P, 64])
        wk = sb("wk", [32, D])
        wcT = sb("wcT", [32, 2, P])
        wkv = sb("wkv", [P, 2, D])
        wkr = sb("wkr", [P, D])
        wv = sb("wv", [32, D])
        wo = sb("wo", [P, D])
        w_ff = sb("w_ff", [P, 2, 512])
        w_so = sb("w_so", [P, 2, D])
        w2e = sb("w2e", [P, 2, E0 * D])
        w_gate = sb("w_gate", [P, 32])
        logitF = sb("logitF", [P, CH])
        b_gate = sb("b_gate", [P, 2 + E0])
        w_l1 = {n: sb(f"l1_{n}", [P, D]) for n in ("q", "k", "v", "a", "g", "o")}
        gamma = sb("gamma", [P, 1])
        w_r = sb("w_r", [P, 32])

        ident = sb("ident", [P, P])
        identb = sb("identb", [P, P], BF16)
        ones = sb("ones", [P, P])
        mean_w = sb("mean_w", [P, NSTATE])
        triu = sb("triu", [P, P], BF16)
        onesb = sb("onesb", [P, P], BF16)
        rev4 = sb("rev4", [P, EPG])
        rev8 = sb("rev8", [P, E1])
        base8 = sb("base8", [P, E1])
        keep_scan = sb("keep_scan", [P, E1 * NT])
        token_i = sb("token_i", [P, NT], I32)
        spare = sb("spare", [P, NT])
        zeros = sb("zeros", [P, 512])

        bn = sb("bn", [P, 2, TC, 6])
        mv = sb("mv", [P, 7 * NC, TC, 2])
        msq = sb("msq", [P, 7 * NC, TC])
        var = sb("var", [P, 7 * NC, TC])
        rs = sb("rs", [P, 7 * NC, TC])
        nw = sb("nw", [P, 2, TC])
        maxes = sb("maxes", [P, 2, NT, 2])
        mneg = sb("mneg", [P, NT])
        mparts = sb("mparts", [P, 2 * NT], BF16)
        mrows = sb("mrows", [2 * NT, P], BF16)
        vh = sb("vh", [P, 2, NT, 32])
        gl = sb("gl", [P, NT, 2 + E0])
        g_s = sb("g_s", [P, 12, NT])
        g4 = sb("g4", [P, 12, NT, EPG])
        wtop = sb("wtop", [P, NT, E0])
        r8 = sb("r8", [P, 6, NT, E1])
        onehot = sb("onehot", [P, E1, NT], BF16)
        et = sb("et", [P, 4, E1, NT])
        r_s = sb("r_s", [P, 12, NT])
        dest = sb("dest", [P, NT], I32)

        ld_x = [sem(f"ld_x{c}") for c in range(NC)]
        ld_a, ld_a1, ld_a2, ld_b, ld_c, ld_d, ld_e = (sem(f"ld_{n}") for n in ("w_in", "w_dt", "layer0", "attn", "ffn", "layer1", "experts"))
        logitF_ready = sem("logitF_ready")
        const_pool, const_dve, zeroed = sem("const_pool"), sem("const_dve"), sem("zeroed")
        bank_full = [sem(f"bank_full{i}") for i in range(8)]
        resid_ready, acc_ready, l1_ps = sem("resid_ready"), sem("acc_ready"), sem("l1_ps")
        relu_act, relu_dve, comb_ready = sem("relu_act"), sem("relu_dve"), sem("comb_ready")
        res_ready = sem("res_ready")
        x0F_ready, silu_ready, gated_ready, u_ready = sem("x0F_ready"), sem("silu_ready"), sem("gated_ready"), sem("u_ready")
        relu_ready, absu_ready, expu_ready, sp_ready, delta_ready = sem("relu_ready"), sem("absu_ready"), sem("expu_ready"), sem("sp_ready"), sem("delta_ready")
        aexp_ready, aneg_ready, decay_ready, bx_ready = sem("aexp_ready"), sem("aneg_ready"), sem("decay_ready"), sem("bx_ready")
        state_ready, y_ready, pre_step = sem("state_ready"), sem("y_ready"), sem("pre_step")
        dve_step = sem("dve_step")
        pool_step = sem("pool_step")
        act_step = sem("act_step")
        guess_ready, rstd_ready = sem("guess_ready"), sem("rstd_ready")
        x1T_ready, x1F_ready = sem("x1T_ready"), sem("x1F_ready")
        wcT_ready, wkv_ready = sem("wcT_ready"), sem("wkv_ready")
        rot_ready, rope_ready, vT_ready = sem("rot_ready"), sem("rope_ready"), sem("vT_ready")
        sum_ready, part_ready, rest_ready, third_ready = sem("sum_ready"), sem("part_ready"), sem("rest_ready"), sem("third_ready")
        split_stored = sem("split_stored")
        head_loaded = [sem(f"head_loaded{b}") for b in range(HB)]
        ones_ready, vh_ready = sem("ones_ready"), sem("vh_ready")
        st_full, exp_done, pv_done, pv_out = sem("st_full"), sem("exp_done"), sem("pv_done"), sem("pv_out")
        pv_stored = [sem(f"pv_stored{b}") for b in range(2)]
        mx_full, mx_free, mparts_ready = sem("mx_full"), sem("mx_free"), sem("mparts_ready")
        mcomb = sem("mcomb")
        half_copied, scan_done = sem("half_copied"), sem("scan_done")
        mt_full, mrows_ready, mrows_placed = sem("mt_full"), sem("mrows_ready"), sem("mrows_placed")
        rcp_ready, attn_loaded = sem("rcp_ready"), sem("attn_loaded")
        last_head_loaded = [sem(f"last_head_loaded{c}") for c in range(NC)]
        attn_ready = sem("attn_ready")
        xnT_ready, xnF_ready, silu0_ready, hid_ready = sem("xnT_ready"), sem("xnF_ready"), sem("silu0_ready"), sem("hid_ready")
        gate_ready, gexp_in, gexp_ready, wtop_ready = sem("gate_ready"), sem("gexp_in"), sem("gexp_ready"), sem("wtop_ready")
        x2T_ready, xrT_ready, xrF_ready = sem("x2T_ready"), sem("xrT_ready"), sem("xrF_ready")
        l1_act, kv_ready, hs_ready, y1_ready = sem("l1_act"), sem("kv_ready"), sem("hs_ready"), sem("y1_ready")
        x3T_ready, x3F_ready = sem("x3T_ready"), sem("x3F_ready")
        rexp_in, rexp_ready, onehot_ready, dest_ready = sem("rexp_in"), sem("rexp_ready"), sem("onehot_ready"), sem("dest_ready")
        scattered, spare_stored, ein_loaded, einF_ready = sem("scattered"), sem("spare_stored"), sem("ein_loaded"), sem("einF_ready")
        relu1_ready, eo_ready = sem("relu1_ready"), sem("eo_ready")
        eo_stored = [sem(f"eo_stored{b}") for b in range(4)]
        gathered = [sem(f"gathered{c}") for c in range(NC)]
        out_ready, out_stored = sem("out_ready"), sem("out_stored")

        q_split, k_split, attn_out, disp, eout = scratch

        def ck(t, c, n=CH):
            return t[:, c * n:(c + 1) * n]

        def tl(t, i):
            return t[:, i * P:(i + 1) * P]

        def full(eng, key):
            b, n, _ = plan[key]
            eng.wait_ge(bank_full[b], n)
            return bank_ap[b]

        def released(key):
            kind, c = key[0], key[1] if len(key) > 1 else 0
            m = key[2] if len(key) > 2 else 0
            return {
                "xT": (x0F_ready, c + 1), "xr": (silu_ready, 2 * c + m + 1) if m < 2 else (res_ready, 2 * c + m - 1), "dt": (u_ready, c + 1),
                "bx": (bx_ready, c + 1), "mean": (decay_ready, c + 1), "ssum": (y_ready, 2 * c + 2),
                "outA": (resid_ready, c + 1), "x1T": (x1F_ready, c + 1),
                "q": (rope_ready, 4 * c + 1), "qr": (rope_ready, 4 * c + 2),
                "k": (rope_ready, 4 * c + 3), "kr": (rope_ready, 4 * c + 4),
                "wT": (wcT_ready, 1), "wkv": (wkv_ready, 1), "v": (vT_ready, c + 1),
                "wo": (resid_ready, NC + c + 1), "xnT": (xnF_ready, c + 1), "gate": (gate_ready, 1),
                "gateF": (logitF_ready, 1), "routeF": (logitF_ready, 2),
                "ffn": (silu0_ready, 4 * c + m % 4 % 2 + 2 * (m // 4) + 1) if m % 4 < 2
                else (hid_ready, 4 * c + m % 2 + 2 * (m // 4) + 1),
                "sh": (acc_ready, ACC * c + 1),
                "rt": (acc_ready, ACC * (c // TC) + 1 + 16 * (c % TC // 2) + 8 * m + 7 + c % 2),
                "xrT": (xrF_ready, c + 1),
                "pk": (l1_act, 4 * c + 1), "pq": (l1_act, 4 * c + 2), "pa": (l1_act, 4 * c + 3),
                "pg": (l1_act, 4 * c + 4), "pv": (kv_ready, c + 1),
                "wo1": (resid_ready, 2 * NC + c + 1), "x3T": (x3F_ready, c + 1),
                "route": (gate_ready, 2), "cum": (comb_ready, 1), "einT": (einF_ready, c + 1),
                "h1": (relu_act if m % 2 == 0 else relu_dve, 2 * c + m // 2 + 1),
                "eo": (eo_ready, 2 * c + 2),
            }[kind]

        def parts(i):
            t = slot[[16, 17, 2, 3][i // 2]][:, (i % 2) * 1024:(i % 2) * 1024 + 768].bitcast(BF16)
            return t.rearrange("p (s q) -> p s q", s=3)

        units = [(h, t, f) for h, tiles in ((0, NT), (1, AHEAD)) for t in range(tiles) for f in range(2)]
        pair = [(3, 4), (5, 6), (0, 1), (2, 7)]
        assert len(pair) == PAIRS

        def pieces(e):
            lo, hi = e * CAP, (e + 1) * CAP
            if lo < S < hi:
                return [(0, lo, S), (1, S, hi)]
            return [(lo // S, lo, hi)]

        def rope_a(n):
            return [slot[6], slot[10]][n]

        def rope_b(n):
            return [slot[7], slot[11]][n]

        def take_expert(act, e):
            o = full(act, ("eo", e))
            if e >= 4:
                act.wait_ge(eo_stored[e % 4], 32 * (e // 4))
            dst = eoT[:, (e % 4) * 512:(e % 4) * 512 + 384]
            act.activation(dst[:, 0:256], o[:, 0:256], ACT.Copy).then_inc(eo_ready, 1)
            act.activation(dst[0:64, 256:384], o[0:64, 256:384], ACT.Copy).then_inc(eo_ready, 1)

        def tiles(t, c):
            return ck(t, c).rearrange("p (t d) -> p t d", d=D)

        block = ctx.enter_context(nc.Block())

        @block.sync
        def _(sp):
            xt = a["L0_attn_x"].rearrange("b (t p) d -> p (b t) d", p=P)
            col = lambda v: v.rearrange("(p o) -> p o", o=1)
            row = lambda v: v.rearrange("(o n) -> o n", o=1)

            def load_x(c):
                sp.dma_start(ck(x0T, c).rearrange("p (t d) -> p t d", d=D), xt[:, c * TC:(c + 1) * TC, :]).then_inc(ld_x[c], 16)

            load_x(0)
            sp.dma_start(w_in[:, :], a["L0_attn_W_in"]).then_inc(ld_a, 16)
            sp.dma_start(b_in[:, :], a["L0_attn_b_in"].rearrange("(m p) -> p m", p=P),
                         allow_slow_non_contiguous=True).then_inc(ld_a, 16)
            load_x(1)
            sp.dma_start(w_dt[:, :, :], a["L0_attn_W_dt"].rearrange("(k p) n -> p k n", p=P)).then_inc(ld_a1, 16)
            sp.dma_start(b_dt[:, :], col(a["L0_attn_b_dt"])).then_inc(ld_a1, 16)
            load_x(2)
            load_x(3)
            for dst, src in ((a_log[NSTATE:P, :], col(a["L0_attn_A_log"])),
                             (w_xp[:, :, :], a["L0_attn_W_xp"].rearrange("(k p) n -> p k n", p=P)),
                             (b_xp[:, :], col(a["L0_attn_b_xp"])),
                             (bc["d"][:, :], row(a["L0_attn_D"]).broadcast_to([P, D])),
                             (bc["bo"][:, :], row(a["L0_attn_b_out"]).broadcast_to([P, D])),
                             (w_out[:, :, :], a["L0_attn_W_out"].rearrange("(k p) n -> p k n", p=P)),
                             (w_r[:, 0:E1], a["L1_ffn_Wr"])):
                sp.dma_start(dst, src).then_inc(ld_a2, 16)
            for dst, src in ((wq[:, :], a["L0_ffn_Wq"]), (wkvc[:, 0:32], a["L0_ffn_Wk_c"]),
                             (wkvc[:, 32:64], a["L0_ffn_Wv_c"]), (wk[:, :], a["L0_ffn_Wk"]),
                             (wv[:, :], a["L0_ffn_Wv"]), (cosF[:, :], a["cos"]), (sinF[:, :], a["sin"])):
                sp.dma_start(dst, src).then_inc(ld_b, 16)
            sp.wait_ge(zeroed, 1)
            sp.dma_start(disp[0:SLOTS, :].rearrange("(p a) d -> p (a d)", p=P)[:, 0:2560].rearrange("p (b n) -> p b n", n=512),
                         zeros[:, :].rearrange("p (o n) -> p o n", o=1).broadcast_to([P, 5, 512])).then_inc(zeroed, 16)
            for dst, src in ((wo[:, :], a["L0_ffn_Wo"]), (w_ff[:, 0, :], a["L0_ffn_W_shared_in"]),
                             (w_ff[:, 1, :], a["L0_ffn_W1_shared"]),
                             (w_so[:, :, :], a["L0_ffn_W_shared_out"].rearrange("(k p) n -> p k n", p=P)),
                             (w2e[:, 0, :].rearrange("p (e n) -> p e n", e=E0), a["L0_ffn_W2_experts"][:, 0:P, :].rearrange("e p n -> p e n")),
                             (w2e[:, 1, :].rearrange("p (e n) -> p e n", e=E0), a["L0_ffn_W2_experts"][:, P:HID, :].rearrange("e p n -> p e n")),
                             (w_gate[:, 0:2], a["L0_ffn_Wg_gate"]), (w_gate[:, 2:2 + E0], a["L0_ffn_We_gate"]),
                             (b_gate[:, 0:2], row(a["L0_ffn_group_bias"]).broadcast_to([P, 2])),
                             (b_gate[:, 2:], row(a["L0_ffn_expert_bias"]).broadcast_to([P, E0])),
                             (bc["n1"][:, :], row(a["L0_ffn_norm1_w"]).broadcast_to([P, D])),
                             (bc["n2"][:, :], row(a["L0_ffn_norm2_w"]).broadcast_to([P, D]))):
                sp.dma_start(dst, src).then_inc(ld_c, 16)
            for n in ("q", "k", "v", "a", "g", "o"):
                sp.dma_start(w_l1[n][:, :], a[f"L1_attn_w{n}"]).then_inc(ld_d, 16)
            sp.dma_start(gamma[:, :], col(a["L1_attn_gamma"])).then_inc(ld_d, 16)

            for c in range(NC):
                i = 2 * c + 1
                for part in range(3):
                    if part < 2:
                        sp.wait_ge(part_ready, 4 * c + 2 * part + 2)
                    else:
                        sp.wait_ge(third_ready, i)
                        sp.dma_start(q_split[:, :, c * CH:(c + 1) * CH].rearrange("s p q -> p s q"),
                                     parts(i - 1)).then_inc(split_stored, 16)
                        sp.wait_ge(third_ready, i + 1)
                    sp.dma_start(k_split[:, part, :, c * CH:(c + 1) * CH],
                                 parts(i)[:, part, :]).then_inc(split_stored, 16)

            def load_head(hv, b):
                q = q_split[:, bass.ds(hv * DH, DH), :]
                k = k_split[bass.ds(hv, 1)].rearrange("o s r q -> o (s r) q")
                sp.dma_start(heads_k[b][0:TERMS, :], k.broadcast_to([3, 3 * DH, S])).then_inc(head_loaded[b], 16)
                for i in range(3):
                    sp.dma_start(heads_q[b][i * 3 * DH:(i + 1) * 3 * DH, :],
                                 q[i:i + 1].broadcast_to([3, DH, S])).then_inc(head_loaded[b], 16)

            def place_max(b):
                for s in range(2):
                    sp.dma_start(heads_q[b][TERMS + s:TERMS + s + 1, :].rearrange("o (t p) -> o t p", p=P),
                                 mrows[s * NT:(s + 1) * NT, :]).then_inc(mrows_placed, 16)

            sp.wait_ge(split_stored, 16 * 4 * NC)
            sp.wait_ge(ones_ready, HB)
            for h in range(3):
                load_head(h, h)
            sp.wait_ge(mrows_ready, 1)
            place_max(0)

            def head(hv, h, lap=0):
                if h + 3 < H:
                    if not (isinstance(hv, int) and hv == 0):
                        sp.wait_ge(st_full, hv * (NT * NC))
                    load_head(hv + 3, (h + 3) % HB)
                if h >= 1:
                    store_out(hv - 1, (h - 1) % 2)
                if h + 1 < H:
                    sp.wait_ge(mrows_ready, hv + 2)
                    place_max((h + 1) % HB)

            def store_out(hv, b):
                sp.wait_ge(rcp_ready, (hv + 1) * RP)
                sp.dma_start(attn_out[bass.ds(hv, 1)].rearrange("o k p q -> p (o k) q"), pv_sb[:, :, b, :]).then_inc(pv_stored[b], 16)

            head(0, 0)
            for h in range(1, 4):
                head(h, h)
            with sp.Fori(1, LOOPED // 4) as it:
                for j in range(4):
                    head(it * 4 + j, 4 + j, it - 1)
            for h in range(LOOPED, H):
                head(h, h)
            for b in range(2):
                sp.wait_ge(pv_stored[b], 16 * (H // 2 - b))
            for c in range(NC):
                for k, t in ((0, numF), (1, rdenF)):
                    src = attn_out[0:H - 1, k].rearrange("h (c r) q -> c h r q", c=NC)[c]
                    sp.dma_start(ck(t, c)[0:(H - 1) * DH, :], src[:, k * DH:(k + 1) * DH, :]).then_inc(attn_loaded, 16)
            sp.wait_ge(pv_out, H)
            sp.wait_ge(rcp_ready, H * RP)
            for c in range(NC):
                for k, t in ((0, numF), (1, rdenF)):
                    r0 = 32 * c + k * DH
                    sp.dma_start(ck(t, c)[(H - 1) * DH:, :], pv_sb[r0:r0 + DH, k, (H - 1) % 2, :]).then_inc(last_head_loaded[c], 16)

            sp.wait_ge(pv_done, NT * H)
            sp.wait_ge(vh_ready, H)
            for i in range(2):
                sp.dma_start(w1[i][:, :].rearrange("p (e f) -> p e f", f=DFF),
                             a["L1_ffn_W1"][4 * i:4 * i + 4].rearrange("e p f -> p e f")).then_inc(ld_e, 16)
                sp.dma_start(w2[i][:, :].rearrange("p (e n) -> p e n", n=D),
                             a["L1_ffn_W2"][4 * i:4 * i + 4].rearrange("e (k p) n -> p (e k) n", p=P)).then_inc(ld_e, 16)

            sp.wait_ge(x3T_ready, NC * TC)
            sp.dma_start(eout[SLOTS:SLOTS + S, :].rearrange("(t p) d -> p t d", p=P),
                         x3T[:, :].rearrange("p (t d) -> p t d", d=D)).then_inc(spare_stored, 16)
            sp.wait_ge(scattered, 16 * NT)
            for n in range(NST // TC):
                dst = einT[n // 4][:, (n % 4) * CH:(n % 4 + 1) * CH]
                sp.dma_start(dst.rearrange("p (t d) -> p t d", d=D),
                             disp[n * CH:(n + 1) * CH, :].rearrange("(t p) d -> p t d", p=P)).then_inc(ein_loaded, 16)
            for e in range(E1):
                sp.wait_ge(eo_ready, 2 * (e + 1))
                src = eoT[:, (e % 4) * 512:(e % 4) * 512 + 384]
                sp.dma_start(eout[e * CAP:e * CAP + 256, :].rearrange("(t p) d -> p t d", p=P),
                             src[:, 0:256].rearrange("p (t d) -> p t d", d=D)).then_inc(eo_stored[e % 4], 16)
                sp.dma_start(eout[e * CAP + 256:(e + 1) * CAP, :], src[0:64, 256:384]).then_inc(eo_stored[e % 4], 16)
            for c in range(NC):
                sp.wait_ge(out_ready, TC * (c + 1))
                sp.dma_start(out.rearrange("b (t p) d -> p (b t) d", p=P)[:, c * TC:(c + 1) * TC, :],
                             ck(yT, c).rearrange("p (t d) -> p t d", d=D)).then_inc(out_stored, 16)
            sp.wait_ge(out_stored, 16 * NC)

        @block.tensor
        def _(pe):
            def fill(key):
                b, _, before = plan[key]
                if before:
                    pe.wait_ge(*released(before))
                return bank_ap[b], bank_full[b]

            def logits(key, xF, ready, w):
                pe.wait_ge(ready, NC)
                o, s = fill(key)
                for c in range(NC):
                    mm = pe.matmul(o[32 * c:32 * (c + 1), :], w[:, :], ck(xF, c), start=True, stop=True)
                mm.then_inc(s, 1)

            def transposes(key, src):
                o, s = fill(key)
                for j in range(TC):
                    mm = pe.transpose(tl(o, j), tl(src, j), ident[:, :])
                mm.then_inc(s, 1)

            pe.wait_ge(const_pool, 2)
            def project(c, m):
                o, s = fill(("xr", c, m))
                pe.matmul(o, w_in[:, m * P:(m + 1) * P], ck(x0F, c), start=True, stop=True).then_inc(s, 1)

            for i in range(4 * NC):
                if i < NC:
                    pe.wait_ge(ld_x[i], 16)
                    transposes(("xT", i), ck(x0T, i))
                if 1 <= i <= NC:
                    c = i - 1
                    if c == 0:
                        pe.wait_ge(ld_a, 32)
                    pe.wait_ge(x0F_ready, c + 1)
                    for m in range(2):
                        project(c, m)
                if 2 <= i <= NC + 1:
                    c = i - 2
                    pe.wait_ge(silu_ready, 2 * c + 2)
                    if c == 0:
                        pe.wait_ge(ld_a1, 32)
                        pe.wait_ge(const_dve, 4)
                    o, s = fill(("dt", c))
                    pe.matmul(o, w_dt[:, 0, :], ck(xin[0], c), start=True, stop=False)
                    pe.matmul(o, w_dt[:, 1, :], ck(xin[1], c), start=False, stop=True).then_inc(s, 1)
                if i == NC + 1:
                    for c in (0, 1):
                        project(c, 2)
                        project(c, 3)
                if 5 <= i <= NC + 4:
                    c = i - 5
                    pe.wait_ge(delta_ready, c + 1)
                    if c == 0:
                        pe.wait_ge(ld_a2, 16 * 7)
                    o, s = fill(("bx", c))
                    pe.matmul(o[0:NSTATE, :], w_xp[:, 0, :], ck(xin[0], c), start=True, stop=False)
                    o2, s2 = fill(("mean", c))
                    pe.matmul(o2[NSTATE:P, :], mean_w[:, :], ck(sp_relu, c), start=True, stop=True).then_inc(s2, 1)
                    pe.matmul(o[0:NSTATE, :], w_xp[:, 1, :], ck(xin[1], c), start=False, stop=True).then_inc(s, 1)
                if i == NC + 4:
                    for c in (2, 3):
                        project(c, 2)
                        project(c, 3)
                if 8 <= i <= NC + 7:
                    c = i - 8
                    pe.wait_ge(state_ready, c + 1)
                    o, s = fill(("ssum", c))
                    pe.matmul(o, ones[0:NSTATE, :], ck(stF, c)[0:NSTATE, :], start=True, stop=True).then_inc(s, 1)
                if 9 <= i <= NC + 8:
                    c = i - 9
                    pe.wait_ge(y_ready, 2 * (c + 1))
                    o, s = fill(("outA", c))
                    for j in range(TC):
                        t = c * TC + j
                        pe.matmul(tl(o, j), tl(gated[0], t), w_out[:, 0, :], start=True, stop=False)
                        mm = pe.matmul(tl(o, j), tl(gated[1], t), w_out[:, 1, :], start=False, stop=True)
                    mm.then_inc(s, 1)
                if i == 3 * NC:
                    pe.wait_ge(ld_b, 112)
                    o, s = fill(("wT",))
                    pe.transpose(o[0:32, 0:P], wkvc[:, 0:32], ident[:, :])
                    pe.transpose(o[0:32, P:2 * P], wkvc[:, 32:64], ident[:, :]).then_inc(s, 1)
                    pe.wait_ge(wcT_ready, 1)
                    o, s = fill(("wkv",))
                    pe.matmul(tl(o, 0), wcT[:, 0, :], wk[:, :], start=True, stop=True)
                    pe.matmul(tl(o, 1), wcT[:, 1, :], wv[:, :], start=True, stop=True).then_inc(s, 1)
                if i >= 3 * NC:
                    c = i - 3 * NC
                    pe.wait_ge(x1T_ready, TC * (c + 1))
                    transposes(("x1T", c), ck(x1T, c))

            pe.wait_ge(rot_ready, 4)
            for c in range(NC):
                pe.wait_ge(x1F_ready, c + 1)
                x = ck(x1F, c)
                for key, w in (("q", wq[:, :]), ("qr", wqr[:, :]), ("k", wkv[:, 0, :]), ("kr", wkr[:, :])):
                    o, s = fill((key, c))
                    pe.matmul(o, w, x, start=True, stop=True).then_inc(s, 1)
                o, s = fill(("v", c))
                for j in range(TC):
                    mm = pe.matmul(tl(o, j), tl(x1F, c * TC + j), wkv[:, 1, :], start=True, stop=True)
                mm.then_inc(s, 1)

            for key in before_attention:
                pe.wait_ge(*released(key))

            def max_half(hv, h, t, f):
                n = 32 * h + 2 * t + f
                if n >= 2:
                    pe.wait_ge(mx_free, hv * 32 + (2 * t + f - 1))
                if f == 1 and h >= 1 and t == 1:
                    pe.wait_ge(mrows_ready, hv)
                b = h % HB
                for i in range(2):
                    k0 = f * 1024 + i * CH
                    mm = pe.matmul(maxps[f][:, i * CH:(i + 1) * CH], heads_q[b][0:TERMS, t * P:(t + 1) * P],
                                   heads_k[b][0:TERMS, k0:k0 + CH], start=True, stop=True)
                mm.then_inc(mx_full, 1)

            def max_turn(hv, h, ps=maxps[1]):
                pe.wait_ge(mparts_ready, hv + 1)
                if ps is not pvps:
                    pe.wait_ge(mx_free, (hv + 1) * 32 + (2 if h + 1 < H else 0))
                pe.transpose(ps[0:2 * NT, 0:P // 2].bitcast(BF16), mparts[:, :], identb[:, :]).then_inc(mt_full, 1)

            def score(hv, h, g, c):
                u = g * NC + c
                if u >= STB:
                    pe.wait_ge(exp_done, hv * 64 + (u - STB + 1))
                elif h >= 1:
                    pe.wait_ge(exp_done, hv * 64 - (63 - u) % STB)
                b = h % HB
                pe.matmul(bank[u % STB][:, :], heads_k[b][0:ROWS, g * P:(g + 1) * P],
                          heads_q[b][0:ROWS, c * CH:(c + 1) * CH], start=True, stop=True).then_inc(st_full, 1)

            def weigh(hv, h, g):
                pe.wait_ge(exp_done, hv * 64 + NC * (g + 1))
                if g == 0:
                    pe.wait_ge(vh_ready, hv + 1)
                    if h >= 1:
                        pe.wait_ge(pv_out, hv)
                for c in range(NC):
                    mm = pe.matmul(pvps[32 * c:32 * c + 32, :], vh[:, h % 2, g, :],
                                   prob[g % PR][:, c * CH:(c + 1) * CH], start=(g == 0), stop=(g == NT - 1))
                mm.then_inc(pv_done, 1)

            def head(hv, h, lap=0):
                pe.wait_ge(mrows_placed, (hv + 1) * 32)
                for g in range(NT):
                    t, k = (g + AHEAD, 1) if g + AHEAD < NT else (g + AHEAD - NT, 2)
                    more = h + k < H
                    if more and t == 0:
                        pe.wait_ge(head_loaded[(h + 2) % HB], ((h + 2) // HB + 1 + lap) * 64)
                    score(hv, h, g, 0)
                    score(hv, h, g, 1)
                    if more:
                        max_half(hv + k, h + k, t, 0)
                    score(hv, h, g, 2)
                    score(hv, h, g, 3)
                    if g == NT + 1 - AHEAD and h + 1 < H:
                        max_turn(hv + 1, h + 1)
                    if more:
                        max_half(hv + k, h + k, t, 1)
                    if g >= 1:
                        weigh(hv, h, g - 1)
                    elif h >= 1:
                        weigh(hv - 1, h - 1, NT - 1)

            pe.wait_ge(ones_ready, HB)
            pe.wait_ge(head_loaded[0], 64)
            for u, (h, t, f) in enumerate(units):
                if h == 1 and t == 0 and f == 0:
                    pe.wait_ge(head_loaded[1], 64)
                if u >= PAIRS:
                    pe.wait_ge(half_copied, u - PAIRS + 1)
                    pe.wait_ge(scan_done, u - PAIRS + 1)
                if h == 1 and u % PAIRS == PAIRS - 1:
                    max_turn(0, 0, pvps)
                    pe.wait_ge(mrows_ready, 1)
                for i, b in enumerate(pair[u % PAIRS]):
                    k0 = (2 * f + i) * CH
                    mm = pe.matmul(bank_ap[b], heads_q[h][0:TERMS, t * P:(t + 1) * P],
                                   heads_k[h][0:TERMS, k0:k0 + CH], start=True, stop=True)
                mm.then_inc(mx_full, 1)
            pe.wait_ge(half_copied, len(units) - 2)
            pe.wait_ge(scan_done, len(units) - 2)
            for h in range(4):
                head(h, h)
            with pe.Fori(1, LOOPED // 4) as it:
                for j in range(4):
                    head(it * 4 + j, 4 + j, it - 1)
            for h in range(LOOPED, H):
                head(h, h)
            weigh(H - 1, H - 1, NT - 1)

            pe.wait_ge(exp_done, 64 * H)
            pe.wait_ge(mx_free, 32 * H)
            pe.wait_ge(mrows_ready, H)
            pe.wait_ge(pv_out, H)
            pe.wait_ge(ld_c, 192)
            for c in range(NC):
                pe.wait_ge(attn_ready, c + 2)
                o, s = fill(("wo", c))
                for j in range(TC):
                    mm = pe.matmul(tl(o, j), tl(numF, c * TC + j), wo[:, :], start=True, stop=True)
                mm.then_inc(s, 1)
            for i in range(NC + 1):
                if i < NC:
                    pe.wait_ge(xnT_ready, TC * (i + 1))
                    transposes(("xnT", i), ck(xnT, i))
                if i == NC - 1:
                    logits(("gateF",), xnF, xnF_ready, w_gate)
                if i == NC:
                    pe.wait_ge(logitF_ready, 1)
                    transposes(("gate",), logitF)
                if i >= 1:
                    c = i - 1
                    pe.wait_ge(xnF_ready, c + 1)
                    for m in range(8):
                        o, s = fill(("ffn", c, m))
                        pe.matmul(o, w_ff[:, m // 4, (m % 4) * P:(m % 4 + 1) * P], ck(xnF, c), start=True, stop=True).then_inc(s, 1)
            for t in range(0, NT, 2):
                c = t // TC
                pe.wait_ge(hid_ready, 4 * (c + 1))
                if t % TC == 0:
                    sh, s_sh = fill(("sh", c))
                    for j in range(TC):
                        for k in range(2):
                            mm = pe.matmul(tl(sh, j), tl(hid[0][k], t + j), w_so[:, k, :], start=(k == 0), stop=(k == 1))
                    mm.then_inc(s_sh, 1)
                for f, j in ((0, 0), (0, 1), (1, 0), (1, 1)):
                    o, s = fill(("rt", t + j, f))
                    for k in range(2):
                        mm = pe.matmul(o, tl(hid[1][k], t + j), w2e[:, k, f * CH:(f + 1) * CH], start=(k == 0), stop=(k == 1))
                    mm.then_inc(s, 1)
            pe.wait_ge(ld_d, 112)
            for i in range(NC + 1):
                if i < NC:
                    pe.wait_ge(xrT_ready, TC * (i + 1))
                    transposes(("xrT", i), ck(xrT, i))
                    pe.wait_ge(xrF_ready, i + 1)
                    for key, w in (("pk", "k"), ("pv", "v"), ("pq", "q"), ("pa", "a"), ("pg", "g")):
                        o, s = fill((key, i))
                        pe.matmul(o, w_l1[w][:, :], ck(xrF, i), start=True, stop=True).then_inc(s, 1)
                if i >= 1:
                    c = i - 1
                    pe.wait_ge(y1_ready, c + 1)
                    o, s = fill(("wo1", c))
                    for j in range(TC):
                        mm = pe.matmul(tl(o, j), tl(yF, c * TC + j), w_l1["o"][:, :], start=True, stop=True)
                    mm.then_inc(s, 1)
            for c in range(NC):
                pe.wait_ge(x3T_ready, TC * (c + 1))
                transposes(("x3T", c), ck(x3T, c))
            logits(("routeF",), x3F, x3F_ready, w_r)
            pe.wait_ge(logitF_ready, 2)
            transposes(("route",), logitF)
            pe.wait_ge(onehot_ready, 1)
            o, s = fill(("cum",))
            oh = onehot[:, :, :].rearrange("p e t -> p (e t)")
            pe.matmul(tl(o, 0), triu[:, :], oh, start=True, stop=True)
            pe.matmul(tl(o, 1), onesb[:, :], oh, start=True, stop=True).then_inc(s, 1)
            for n in range(NST // TC):
                if n == 0:
                    pe.wait_ge(ein_loaded, 16 * (NST // TC))
                transposes(("einT", n), einT[n // 4][:, (n % 4) * CH:(n % 4 + 1) * CH])
            pe.wait_ge(ld_e, 64)
            pe.wait_ge(einF_ready, NST // TC)
            for i in range(E1 + 1):
                if i < E1:
                    e = i
                    for m in range(FM):
                        o, s = fill(("h1", e, m))
                        for (n, lo, hi) in pieces(e):
                            mm = pe.matmul(o[:, lo - e * CAP:hi - e * CAP], w1[e // 4][:, (e % 4) * DFF + m * P:(e % 4) * DFF + (m + 1) * P],
                                           einF[n][:, lo - n * S:hi - n * S], start=True, stop=True)
                        mm.then_inc(s, 1)
                if i >= 1:
                    e = i - 1
                    pe.wait_ge(relu_act, 2 * (e + 1))
                    pe.wait_ge(relu_dve, 2 * (e + 1))
                    o, s = fill(("eo", e))
                    for j in range(3):
                        n = P if j < 2 else 64
                        for k in range(FM):
                            w = w2[e // 4][:, ((e % 4) * FM + k) * D:((e % 4) * FM + k + 1) * D]
                            mm = pe.matmul(o[0:n, j * P:(j + 1) * P], hE[e % 2][:, k * CAP + j * P:k * CAP + j * P + n], w,
                                           start=(k == 0), stop=(k == FM - 1))
                    mm.then_inc(s, 1)

        @block.scalar
        def _(act):
            for i in range(1, NC + 2):
                if i <= NC:
                    c = i - 1
                    if c == 0:
                        act.wait_ge(ld_a, 32)
                        act.wait_ge(ld_a1, 32)
                    for m in range(2):
                        o = full(act, ("xr", c, m))
                        act.activation(ck(xin[m], c), o, ACT.Silu, bias=b_in[:, m:m + 1]).then_inc(silu_ready, 1)
                if i >= 2:
                    c = i - 2
                    o = full(act, ("dt", c))
                    act.activation(ck(sp_abs, c), o, ACT.Identity, bias=b_dt[:, :]).then_inc(u_ready, 1)
            act.wait_ge(ld_a2, 16 * 7)
            act.activation(a_exp[NSTATE:P, :], a_log[NSTATE:P, :], ACT.Exp).then_inc(aexp_ready, 1)
            for c in range(NC):
                act.wait_ge(absu_ready, c + 1)
                act.activation(ck(sp_abs, c), ck(sp_abs, c), ACT.Exp, scale=-1.0).then_inc(expu_ready, 1)
            for c in range(NC):
                act.wait_ge(expu_ready, c + 1)
                act.activation(ck(sp_abs, c), ck(sp_abs, c), ACT.Ln, bias=1.0).then_inc(sp_ready, 1)
            for c in range(NC):
                o = full(act, ("mean", c))
                act.wait_ge(aneg_ready, 1)
                act.activation(ck(aF, c)[0:NSTATE, :], o[NSTATE:P, :], ACT.Exp, scale=a_neg[NSTATE:P, :]).then_inc(decay_ready, 1)
            for c in range(NC):
                for m in (2, 3):
                    o = full(act, ("xr", c, m))
                    act.activation(ck(gated[m - 2], c), o, ACT.Silu, bias=b_in[:, m:m + 1]).then_inc(res_ready, 1)
            o = full(act, ("wT",))
            act.activation(wcT[:, :, :].rearrange("p k n -> p (k n)"), o[0:32, 0:2 * P], ACT.Copy).then_inc(wcT_ready, 1)
            o = full(act, ("wkv",))
            act.activation(wkv[:, :, :].rearrange("p k n -> p (k n)"), o[:, 0:2 * D], ACT.Copy).then_inc(wkv_ready, 1)
            for c in range(NC):
                o = full(act, ("x1T", c))
                act.activation(ck(x1F, c), o, ACT.Copy).then_inc(x1F_ready, 1)

            for c in range(NC + 1):
                if c >= 1:
                    for n in range(2):
                        i = 2 * (c - 1) + n
                        act.wait_ge(sum_ready, i + 1)
                        act.activation(parts(i)[:, 0, :], ck(rope_a(n), c - 1), ACT.Copy).then_inc(part_ready, 1)
                    for n in range(2):
                        i = 2 * (c - 1) + n
                        act.wait_ge(rest_ready, i + 1)
                        act.activation(parts(i)[:, 1, :], ck(rope_b(n), c - 1), ACT.Copy).then_inc(part_ready, 1)
                if c < NC:
                    o = full(act, ("v", c))
                    act.activation(ck(vT, c), o, ACT.Copy).then_inc(vT_ready, 1)

            act.wait_ge(pre_step, 3)
            for u in range(len(units)):
                act.wait_ge(mx_full, u + 1)
                if u >= PAIRS:
                    act.wait_ge(scan_done, u - PAIRS + 1)
                act.activation(ck(copied, u % PAIRS), bank_ap[pair[u % PAIRS][1]], ACT.Copy).then_inc(half_copied, 1)

            def head(hv, h, lap=0):
                for g in range(NT):
                    if h * NT + g >= PR:
                        act.wait_ge(pv_done, hv * NT + (g - PR + 1))
                    for c in range(NC):
                        u = g * NC + c
                        act.wait_ge(st_full, hv * 64 + u + 1)
                        act.activation(prob[g % PR][:, c * CH:(c + 1) * CH], bank[u % STB][:, :], ACT.Exp,
                                       scale=1.0 / math.sqrt(DH)).then_inc(exp_done, 1)
                        if h >= 1 and g == 1 and c == 1:
                            take_out(hv - 1, h - 1, lap)

            def take_out(hv, h, lap=0):
                act.wait_ge(pv_done, (hv + 1) * NT)
                if h >= 2:
                    act.wait_ge(pv_stored[h % 2], (h // 2 + 2 * lap) * 16)
                act.activation(pv_sb[:, 0, h % 2, :], pvps[:, :], ACT.Copy).then_inc(pv_out, 1)

            for h in range(4):
                head(h, h)
            with act.Fori(1, LOOPED // 4) as it:
                for j in range(4):
                    head(it * 4 + j, 4 + j, it - 1)
            for h in range(LOOPED, H):
                head(h, h)
            take_out(H - 1, H - 1)

            for i in range(NC + 1):
                if i < NC:
                    o = full(act, ("xnT", i))
                    act.activation(ck(xnF, i), o, ACT.Copy).then_inc(xnF_ready, 1)
                if i == NC - 1:
                    o = full(act, ("gateF",))
                    act.activation(logitF[:, :], o, ACT.Copy).then_inc(logitF_ready, 1)
                for w in range(2) if i >= 1 else ():
                    c = i - 1
                    for k in range(2):
                        o = full(act, ("ffn", c, 4 * w + k))
                        if c >= 1:
                            act.wait_ge(hid_ready, 4 * (c - 1) + 2 * w + k + 1)
                        act.activation(act_ff[:, (2 * w + k) * CH:(2 * w + k + 1) * CH], o, ACT.Silu).then_inc(silu0_ready, 1)
            act.wait_ge(gexp_in, 1)
            act.activation(g_s[:, 2, :], g_s[:, 1, :], ACT.Exp).then_inc(gexp_ready, 1)
            act.activation(g4[:, 3, :, :], g4[:, 2, :, :], ACT.Exp).then_inc(gexp_ready, 1)
            act.wait_ge(ld_d, 112)
            for c in range(NC):
                o = full(act, ("xrT", c))
                act.activation(ck(xrF, c), o, ACT.Copy, scale=gamma[:, :]).then_inc(xrF_ready, 1)
                for key, dst, f in (("pk", kF, ACT.Copy), ("pq", qF, ACT.Copy), ("pa", decF, ACT.Sigmoid), ("pg", gsF, ACT.Silu)):
                    o = full(act, (key, c))
                    act.activation(ck(dst, c), o, f).then_inc(l1_act, 1)
            for c in range(NC):
                o = full(act, ("x3T", c))
                act.activation(ck(x3F, c), o, ACT.Copy).then_inc(x3F_ready, 1)
            o = full(act, ("routeF",))
            act.wait_ge(gate_ready, 1)
            act.activation(logitF[:, :], o, ACT.Copy).then_inc(logitF_ready, 1)
            act.wait_ge(rexp_in, 1)
            act.activation(r8[:, 2, :, :], r8[:, 1, :, :], ACT.Exp).then_inc(rexp_ready, 1)
            for n in range(NST // TC):
                o = full(act, ("einT", n))
                act.activation(ck(einF[n // 4], n % 4), o, ACT.Copy).then_inc(einF_ready, 1)
            for e in range(E1):
                for m in (0, 2):
                    o = full(act, ("h1", e, m))
                    if e >= 2 and m == 0:
                        full(act, ("eo", e - 2))
                    act.activation(hE[e % 2][:, m * CAP:(m + 1) * CAP], o[:, 0:CAP], ACT.Relu).then_inc(relu_act, 1)
                if e >= 1:
                    take_expert(act, e - 1)
            take_expert(act, E1 - 1)

        @block.vector
        def _(v):
            steps = [0]

            def link(ins, meanwhile=None):
                steps[0] += 1
                n = steps[0]
                ins.then_inc(dve_step, 1)
                if meanwhile:
                    meanwhile()
                v.wait_ge(dve_step, n)

            def stats(k, src, c, meanwhile=()):
                n = norms.index((k, c))
                if k == N_RMS1:
                    n2 = norms.index((N_LN2, c))
                    link(v.tensor_tensor(msq[:, n, :], rs[:, n2, :], rs[:, n2, :], ALU.mult))
                    link(v.tensor_tensor(msq[:, n, :], msq[:, n, :], mv[:, n2, :, 1], ALU.mult))
                    link(v.tensor_scalar(var[:, n, :], msq[:, n, :], RMS1_EPS / D, None, ALU.add))
                    return guess_root(k, c)
                for j in range(TC):
                    ins = v.bn_stats(bn[:, n % 2, j, :], tl(src, c * TC + j))
                    if j < TC - 1:
                        ins.then_inc(dve_step, 1)
                        steps[0] += 1
                link(ins)
                for j in range(TC):
                    ins = v.bn_aggr(mv[:, n, j, :], bn[:, n % 2, j, :])
                    if j < TC - 1:
                        ins.then_inc(dve_step, 1)
                        steps[0] += 1
                link(ins)
                mean, vr = mv[:, n, :, 0], mv[:, n, :, 1]
                if k in (N_RMSX, N_RMSO):
                    link(v.tensor_tensor(msq[:, n, :], mean, mean, ALU.mult))
                    link(v.scalar_tensor_tensor(out=var[:, n, :], in0=msq[:, n, :], scalar=RMS0_EPS, in1=vr, op0=ALU.add, op1=ALU.add))
                else:
                    link(v.tensor_scalar(var[:, n, :], vr, LN_EPS, None, ALU.add))
                guess_root(k, c, meanwhile)

            def guess_root(k, c, meanwhile=()):
                n = norms.index((k, c))
                y, x, w = rs[:, n, :], var[:, n, :], nw[:, 1, :]
                guess = v.tensor_scalar(y.bitcast(I32), x.bitcast(I32), -0.5, RSQRT_MAGIC, ALU.mult, ALU.add)
                if (k, c) in pool_norms:
                    guess.then_inc(guess_ready, 1)
                    return
                link(guess)
                for i in range(3):
                    other = meanwhile[2 * i:2 * i + 2] + (None, None)
                    link(v.tensor_tensor(w, y, y, ALU.mult), other[0])
                    link(v.scalar_tensor_tensor(out=w, in0=w, scalar=-0.5, in1=x, op0=ALU.mult, op1=ALU.mult), other[1])
                    link(v.scalar_tensor_tensor(out=y, in0=w, scalar=1.5, in1=y, op0=ALU.add, op1=ALU.mult))

            def root(k, c):
                n = norms.index((k, c))
                if (k, c) in pool_norms:
                    v.wait_ge(rstd_ready, pool_norms.index((k, c)) + 1)
                return mv[:, n, :, 0], rs[:, n, :]

            def normalize(k, c, dst, src, done):
                mean, r = root(k, c)
                for j in range(TC):
                    v.tensor_scalar(tl(dst, c * TC + j), tl(src, c * TC + j), mean[:, j:j + 1], r[:, j:j + 1],
                                    ALU.subtract, ALU.mult).then_inc(done, 1)

            v.memset(ones[:, :], 1.0).then_inc(const_dve, 1)
            v.memset(mean_w[:, :], 1.0 / D).then_inc(const_dve, 1)
            v.memset(onesb[:, :], 1.0).then_inc(const_dve, 1)
            v.memset(zeros[:, :], 0.0).then_inc(zeroed, 1)
            v.memset(keep_scan[:, :], 1.0).then_inc(const_dve, 1)
            v.wait_ge(const_dve, 4)
            v.memset(keep_scan[:, :].rearrange("p (e t) -> p e t", t=NT)[:, :, 0:1], 0.0).then_inc(const_dve, 1)

            for i in range(NC + 2):
                if i < NC:
                    o = full(v, ("xT", i))
                    v.tensor_copy(ck(x0F, i), o).then_inc(x0F_ready, 1)
                if i >= 2:
                    c = i - 2
                    v.wait_ge(u_ready, c + 1)
                    v.tensor_scalar(ck(sp_relu, c), ck(sp_abs, c), 0.0, None, ALU.max).then_inc(relu_ready, 1)
                    v.wait_ge(relu_ready, c + 1)
                    v.scalar_tensor_tensor(out=ck(sp_abs, c), in0=ck(sp_abs, c), scalar=-1.0, in1=ck(sp_abs, c),
                                           op0=ALU.mult, op1=ALU.max).then_inc(absu_ready, 1)
            v.wait_ge(aexp_ready, 1)
            v.tensor_scalar(a_neg[NSTATE:P, :], a_exp[NSTATE:P, :], -1.0, None, ALU.mult).then_inc(aneg_ready, 1)
            for c in range(NC):
                v.wait_ge(sp_ready, c + 1)
                v.tensor_tensor(ck(sp_relu, c), ck(sp_relu, c), ck(sp_abs, c), ALU.add).then_inc(delta_ready, 1)
            for i in range(NC):
                o = full(v, ("bx", i))
                v.wait_ge(ld_a2, 16 * 7)
                v.tensor_scalar(ck(bxF, i)[0:NSTATE, :], o[0:NSTATE, :], b_xp[:, :], None, ALU.add).then_inc(bx_ready, 1)
                v.wait_ge(decay_ready, i + 1)
                v.wait_ge(bx_ready, i + 1)
                if i >= 1:
                    v.wait_ge(state_ready, i)
                before = 0.0 if i == 0 else stF[0:NSTATE, i * CH - 1:i * CH]
                v.tensor_tensor_scan(ck(stF, i)[0:NSTATE, :], ck(aF, i)[0:NSTATE, :], ck(bxF, i)[0:NSTATE, :],
                                     before, ALU.mult, ALU.add).then_inc(state_ready, 1)
            for i in range(1, NC + 3):
                if 1 <= i <= NC:
                    c = i - 1
                    o = full(v, ("ssum", c))
                    v.wait_ge(gated_ready, 2 * (c + 1))
                    for k in range(2):
                        v.tensor_tensor(ck(gated[k], c), o, ck(gated[k], c), ALU.mult).then_inc(y_ready, 1)
                if 2 <= i <= NC + 1:
                    c = i - 2
                    o = full(v, ("outA", c))
                    v.wait_ge(pre_step, 3)
                    v.tensor_tensor(ck(x1T, c), o, ck(pre, c), ALU.add).then_inc(resid_ready, 1)
                    v.wait_ge(resid_ready, c + 1)
                    stats(N_LN1, x1T, c)
                if i >= 3:
                    normalize(N_LN1, i - 3, x1T, x1T, x1T_ready)

            for c in range(NC + 1):
                for n, (key, keyr) in enumerate((("q", "qr"), ("k", "kr")) if c < NC else ()):
                    i = 2 * c + n
                    o = full(v, (key, c))
                    v.wait_ge(ld_b, 112)
                    v.tensor_tensor(ck(rope_a(n), c), o, ck(cosF, c), ALU.mult).then_inc(rope_ready, 1)
                    o = full(v, (keyr, c))
                    v.tensor_tensor(ck(rope_b(n), c), o, ck(sinF, c), ALU.mult).then_inc(rope_ready, 1)
                    v.wait_ge(rope_ready, 2 * i + 2)
                    v.tensor_tensor(ck(rope_a(n), c), ck(rope_a(n), c), ck(rope_b(n), c), ALU.add).then_inc(sum_ready, 1)
                for n in range(2) if c >= 1 else ():
                    i = 2 * (c - 1) + n
                    v.wait_ge(rest_ready, i + 1)
                    v.wait_ge(part_ready, 4 * (c - 1) + n + 3)
                    v.tensor_tensor(parts(i)[:, 2, :], ck(rope_b(n), c - 1), parts(i)[:, 1, :], ALU.subtract).then_inc(third_ready, 1)

            def reduce_half(hv, h, t, f):
                v.wait_ge(mx_full, hv * 32 + (2 * t + f + 1))
                v.tensor_reduce(maxes[:, h % 2, t, f:f + 1], maxps[f][:, :], AX.X, ALU.max).then_inc(mx_free, 1)

            def combine(hv, h):
                v.wait_ge(mx_free, hv * 32 + 32)
                if h >= 1:
                    v.wait_ge(mparts_ready, hv)
                v.tensor_tensor(mneg[:, :], maxes[:, h % 2, :, 0], maxes[:, h % 2, :, 1], ALU.max).then_inc(mcomb, 1)
                v.wait_ge(mcomb, hv * 2 + 1)
                v.tensor_scalar(mparts[:, 0:NT], mneg[:, :], -1.0, None, ALU.mult).then_inc(mcomb, 1)
                v.wait_ge(mcomb, hv * 2 + 2)
                v.scalar_tensor_tensor(out=mparts[:, NT:2 * NT], in0=mneg[:, :], scalar=-1.0, in1=mparts[:, 0:NT],
                                       op0=ALU.mult, op1=ALU.subtract).then_inc(mparts_ready, 1)

            def invert(hv, h, i):
                if i == 0:
                    v.wait_ge(pv_out, hv + 1)
                q = slice(i * CH // RP, (i + 1) * CH // RP)
                v.reciprocal(pv_sb[:, 1, h % 2, q], pv_sb[:, 0, h % 2, q]).then_inc(rcp_ready, 1)

            def turn(hv, h, ps=maxps[1]):
                v.wait_ge(mt_full, hv + 1)
                if h >= 1:
                    v.wait_ge(mrows_placed, hv * 32)
                v.tensor_copy(mrows[:, :], ps[0:2 * NT, 0:P // 2].bitcast(BF16)).then_inc(mrows_ready, 1)

            def head(hv, h, lap=0):
                for g in range(NT):
                    t, k = (g + AHEAD, 1) if g + AHEAD < NT else (g + AHEAD - NT, 2)
                    more = h + k < H
                    if more:
                        reduce_half(hv + k, h + k, t, 0)
                    if g == NT + 1 - AHEAD and h + 1 < H:
                        turn(hv + 1, h + 1)
                    if more:
                        reduce_half(hv + k, h + k, t, 1)
                    if t == NT - 1 and h + 1 < H:
                        combine(hv + 1, h + 1)
                    if h >= 1 and 3 <= g < 3 + RP:
                        invert(hv - 1, h - 1, g - 3)

            def keep_maxima(u, n):
                h, t, _ = units[u]
                v.wait_ge(scan_done, u + n)
                ends = slot[10 + u // PAIRS % 2][:, :].rearrange("p (t f q) -> p t f q", f=2, q=CH)[:, 0:n // 2, :, CH - 1]
                v.tensor_copy(maxes[:, h, t:t + n // 2, :], ends).then_inc(mx_free, n)

            for u, (h, t, f) in enumerate(units):
                v.wait_ge(half_copied, u + 1)
                if u == 0:
                    v.wait_ge(third_ready, 2 * NC)
                if u >= 2 * PAIRS:
                    v.wait_ge(mx_free, (u // PAIRS - 1) * PAIRS)
                v.tensor_tensor_scan(running[u % (2 * PAIRS)], bank_ap[pair[u % PAIRS][0]], ck(copied, u % PAIRS),
                                     -BIG, ALU.max, ALU.max).then_inc(scan_done, 1)
                if u % PAIRS == 0 and u >= PAIRS and u != 2 * NT:
                    keep_maxima(u - PAIRS, PAIRS)
                if u == 2 * NT - 1:
                    keep_maxima(u + 1 - PAIRS, PAIRS)
                    combine(0, 0)
                if u == 2 * NT + 2:
                    turn(0, 0, pvps)
            keep_maxima(2 * NT + PAIRS, 2 * AHEAD - PAIRS)
            for h in range(4):
                head(h, h)
            with v.Fori(1, LOOPED // 4) as it:
                for j in range(4):
                    head(it * 4 + j, 4 + j, it - 1)
            for h in range(LOOPED, H):
                head(h, h)

            v.wait_ge(attn_loaded, 16 * 2 * NC)
            early = 96
            v.tensor_tensor(numF[0:early, :], numF[0:early, :], rdenF[0:early, :], ALU.mult).then_inc(attn_ready, 1)
            for i in range(RP):
                invert(H - 1, H - 1, i)
            for c in range(NC):
                v.wait_ge(last_head_loaded[c], 32)
                v.tensor_tensor(ck(numF, c)[early:, :], ck(numF, c)[early:, :], ck(rdenF, c)[early:, :], ALU.mult).then_inc(attn_ready, 1)
            v.wait_ge(ld_c, 192)
            for i in range(NC + 1):
                if i < NC:
                    o = full(v, ("wo", i))
                    v.tensor_tensor(ck(xnT, i), o, ck(x1T, i), ALU.add).then_inc(resid_ready, 1)
                    v.wait_ge(resid_ready, NC + i + 1)
                    stats(N_RMSX, xnT, i)
                if i >= 1:
                    c = i - 1
                    _, r = root(N_RMSX, c)
                    for j in range(TC):
                        x = tl(xnT, c * TC + j)
                        v.scalar_tensor_tensor(out=x, in0=x, scalar=r[:, j:j + 1], in1=bc["n1"][:, :],
                                               op0=ALU.mult, op1=ALU.mult).then_inc(xnT_ready, 1)

            def turned(o, n):
                return o.rearrange("p (j c n) -> p c j n", j=TC, c=NC)[:, :, :, 0:n]

            def wide(x, n=EPG):
                return x.unsqueeze(2).broadcast_to([P, NT, n])

            def first_best(score, rank, rev, n, top, hit, oh):
                link(v.tensor_reduce(top, score, AX.X, ALU.max))
                link(v.tensor_tensor(hit, score, wide(top, n), ALU.is_equal))
                link(v.tensor_tensor(hit, hit, rev[:, :].unsqueeze(1).broadcast_to([P, NT, n]), ALU.mult))
                link(v.tensor_reduce(rank, hit, AX.X, ALU.max))
                link(v.tensor_tensor(oh, hit, wide(rank, n), ALU.is_equal))

            def hidden(c, between=()):
                for w in range(2):
                    for k in range(2):
                        i = 2 * w + k
                        o = full(v, ("ffn", c, 4 * w + 2 + k))
                        v.wait_ge(silu0_ready, 4 * c + i + 1)
                        v.tensor_tensor(ck(hid[w][k], c), o, act_ff[:, i * CH:(i + 1) * CH], ALU.mult).then_inc(hid_ready, 1)
                        if between:
                            between[i]()

            hidden(0)
            hidden(1)
            g0, g1 = gl[:, :, 0], gl[:, :, 1]
            second, diff, ediff, first_, top, summ, rank, top2, rank2 = (g_s[:, i, :] for i in range(9))
            e4, tmp4, z4, x4, hit4, oh4, e4b, hit4b, oh4b = (g4[:, i, :, :] for i in range(9))

            def choose_group():
                o = full(v, ("gate",))
                v.tensor_copy(gl[:, :, :].rearrange("p (c j) n -> p c j n", j=TC), turned(o, 2 + E0)).then_inc(gate_ready, 1)
                v.wait_ge(gate_ready, 1)
                link(v.tensor_tensor(gl[:, :, :], gl[:, :, :], b_gate[:, :].unsqueeze(1).broadcast_to([P, NT, 2 + E0]), ALU.add))
                link(v.tensor_tensor(second, g1, g0, ALU.is_gt))
                link(v.tensor_scalar(first_, second, -1.0, 1.0, ALU.mult, ALU.add))
                link(v.tensor_tensor(diff, g1, g0, ALU.subtract))
                link(v.tensor_scalar(summ, diff, -1.0, None, ALU.mult))
                link(v.tensor_tensor(diff, diff, summ, ALU.min))

            def choose_first():
                link(v.tensor_tensor(e4, gl[:, :, 2:6], wide(first_), ALU.mult))
                link(v.tensor_tensor(tmp4, gl[:, :, 6:10], wide(second), ALU.mult))
                link(v.tensor_tensor(e4, e4, tmp4, ALU.add))
                first_best(e4, rank, rev4, EPG, top, hit4, oh4)

            def choose_second():
                v.tensor_tensor(z4, e4, wide(top), ALU.subtract).then_inc(gexp_in, 1)
                link(v.scalar_tensor_tensor(out=e4b, in0=oh4, scalar=-BIG, in1=e4, op0=ALU.mult, op1=ALU.add))
                first_best(e4b, rank2, rev4, EPG, top2, hit4b, oh4b)

            def both():
                link(v.tensor_tensor(oh4, oh4, oh4b, ALU.add))

            hidden(2)
            hidden(3, (choose_group, choose_first, choose_second, both))
            v.wait_ge(gexp_ready, 2)
            link(v.tensor_reduce(summ, x4, AX.X, ALU.add))
            link(v.scalar_tensor_tensor(out=summ, in0=ediff, scalar=1.0, in1=summ, op0=ALU.add, op1=ALU.mult))
            link(v.reciprocal(summ, summ))
            link(v.tensor_tensor(x4, x4, oh4, ALU.mult))
            link(v.tensor_tensor(x4, x4, wide(summ), ALU.mult))
            link(v.tensor_tensor(wtop[:, :, 0:EPG], x4, wide(first_), ALU.mult))
            link(v.tensor_tensor(wtop[:, :, EPG:], x4, wide(second), ALU.mult))

            def sum_experts(i):
                o = full(v, ("sh", i))
                v.tensor_tensor(ck(oT, i), o, ck(xnT, i), ALU.add).then_inc(acc_ready, 1)
                n = ACC * i + 1
                v.wait_ge(acc_ready, n)
                for t in range(i * TC, (i + 1) * TC, 2):
                    for e in range(E0):
                        for j in range(2):
                            o = full(v, ("rt", t + j, e // 4))
                            v.wait_ge(acc_ready, n - 1)
                            v.scalar_tensor_tensor(out=tl(oT, t + j), in0=tl(o, e % 4), scalar=wtop[:, t + j, e:e + 1],
                                                   in1=tl(oT, t + j), op0=ALU.mult, op1=ALU.add).then_inc(acc_ready, 1)
                            n += 1
                    if t % TC == 0 and i >= 2:
                        norm_x2(i - 2)
                v.wait_ge(acc_ready, n)
                stats(N_RMSO, oT, i)

            def add_input(c):
                _, r = root(N_RMSO, c)
                for j in range(TC):
                    x = tl(oT, c * TC + j)
                    link(v.scalar_tensor_tensor(out=x, in0=x, scalar=r[:, j:j + 1], in1=bc["n2"][:, :],
                                                op0=ALU.mult, op1=ALU.mult))
                link(v.tensor_tensor(ck(oT, c), ck(oT, c), ck(x1T, c), ALU.add))
                stats(N_LN2, oT, c)

            def norm_x2(c):
                normalize(N_LN2, c, x2T, oT, x2T_ready)
                v.wait_ge(x2T_ready, TC * (c + 1))
                stats(N_RMS1, x2T, c)

            def scale_x2(c):
                _, r = root(N_RMS1, c)
                for j in range(TC):
                    v.tensor_scalar(tl(xrT, c * TC + j), tl(x2T, c * TC + j), r[:, j:j + 1], None, ALU.mult).then_inc(xrT_ready, 1)

            def gated_scan(c):
                o = full(v, ("pv", c))
                v.wait_ge(l1_act, 4 * c + 1)
                v.tensor_tensor(ck(kvF, c), o, ck(kF, c), ALU.mult).then_inc(kv_ready, 1)
                v.wait_ge(kv_ready, c + 1)
                v.wait_ge(l1_act, 4 * c + 4)
                before = 0.0 if c == 0 else hsF[:, c * CH - 1:c * CH]
                v.tensor_tensor_scan(ck(hsF, c), ck(decF, c), ck(kvF, c), before, ALU.mult, ALU.add).then_inc(hs_ready, 1)
                v.wait_ge(hs_ready, c + 1)
                link(v.tensor_tensor(ck(yF, c), ck(hsF, c), ck(qF, c), ALU.mult))
                v.tensor_tensor(ck(yF, c), ck(yF, c), ck(gsF, c), ALU.mult).then_inc(y1_ready, 1)

            def add_x2(c):
                o = full(v, ("wo1", c))
                v.tensor_tensor(ck(x3T, c), o, ck(x2T, c), ALU.add).then_inc(resid_ready, 1)
                v.wait_ge(resid_ready, 2 * NC + c + 1)
                stats(N_LN3, x3T, c)

            def norm_x3(c):
                normalize(N_LN3, c, x3T, x3T, x3T_ready)

            for i in range(NC):
                if i >= 3:
                    scale_x2(i - 3)
                sum_experts(i)
                if i >= 1:
                    add_input(i - 1)
            add_input(3)
            norm_x2(2)
            scale_x2(1)
            norm_x2(3)
            gated_scan(0)
            scale_x2(2)
            scale_x2(3)
            gated_scan(1)
            add_x2(0)
            gated_scan(2)
            add_x2(1)
            norm_x3(0)
            gated_scan(3)
            add_x2(2)
            norm_x3(1)
            add_x2(3)
            norm_x3(2)
            norm_x3(3)

            z8, x8, hit8, oh8 = (r8[:, i, :, :] for i in range(1, 5))
            top, rank, ssum, pmax, place, base, kept, at, factor, tmp = (r_s[:, i, :] for i in range(10))
            lg = r8[:, 5, :, :]
            o = full(v, ("route",))
            v.tensor_copy(lg.rearrange("p (c j) e -> p c j e", j=TC), turned(o, E1)).then_inc(gate_ready, 1)
            v.wait_ge(gate_ready, 2)
            v.wait_ge(const_pool, 7)
            first_best(lg, rank, rev8, E1, top, hit8, oh8)
            oh_et = oh8.rearrange("p t e -> p e t")
            v.tensor_copy(onehot[:, :, :], oh_et).then_inc(onehot_ready, 1)
            v.tensor_tensor(z8, lg, wide(top, E1), ALU.subtract).then_inc(rexp_in, 1)
            link(v.tensor_tensor(hit8, oh8, base8[:, :].unsqueeze(1).broadcast_to([P, NT, E1]), ALU.mult))
            link(v.tensor_reduce(base, hit8, AX.X, ALU.add))
            link(v.scalar_tensor_tensor(out=base, in0=base, scalar=-1.0, in1=spare[:, :], op0=ALU.add, op1=ALU.subtract))
            tot, inc, cum, sel = (et[:, i, :, :] for i in range(4))
            fl = lambda x: x.rearrange("p e t -> p (e t)")
            o = full(v, ("cum",))
            link(v.tensor_copy(fl(tot), tl(o, 1)))
            link(v.tensor_tensor_scan(fl(inc), keep_scan[:, :], fl(tot), 0.0, ALU.mult, ALU.add))
            link(v.tensor_tensor(inc, inc, tot, ALU.subtract))
            v.tensor_tensor(fl(cum), tl(o, 0), fl(inc), ALU.add).then_inc(comb_ready, 1)
            v.wait_ge(comb_ready, 1)
            link(v.tensor_tensor(sel, cum, oh_et, ALU.mult))
            link(v.tensor_reduce(place, sel.rearrange("p e t -> p t e"), AX.X, ALU.add))
            link(v.tensor_tensor(at, place, base, ALU.add))
            link(v.scalar_tensor_tensor(out=at, in0=place, scalar=float(CAP) + 0.5, in1=at, op0=ALU.is_lt, op1=ALU.mult))
            v.tensor_tensor(dest[:, :], at, spare[:, :], ALU.add).then_inc(dest_ready, 1)
            v.wait_ge(rexp_ready, 1)
            link(v.tensor_reduce(ssum, x8, AX.X, ALU.add))
            link(v.reciprocal(pmax, ssum))
            link(v.tensor_scalar(kept, place, float(CAP) + 0.5, None, ALU.is_lt))
            link(v.scalar_tensor_tensor(out=tmp, in0=pmax, scalar=-1.0, in1=kept, op0=ALU.add, op1=ALU.mult))
            link(v.tensor_scalar(factor, tmp, 1.0, None, ALU.add))
            for e in range(E1):
                for m in (1, 3):
                    o = full(v, ("h1", e, m))
                    if e >= 2 and m == 1:
                        full(v, ("eo", e - 2))
                    v.tensor_scalar(hE[e % 2][:, m * CAP:(m + 1) * CAP], o[:, 0:CAP], 0.0, None, ALU.max).then_inc(relu_dve, 1)
            def weigh(t):
                if t % TC == 0:
                    v.wait_ge(gathered[t // TC], 16 * TC)
                steps[0] += 1
                v.scalar_tensor_tensor(out=tl(finT, t), in0=tl(combT, t), scalar=factor[:, t:t + 1], in1=tl(x3T, t),
                                       op0=ALU.mult, op1=ALU.add).then_inc(dve_step, 1)

            for j in range(TC):
                weigh(j)
            for c in range(NC):
                v.wait_ge(dve_step, steps[0])
                stats(N_LN4, finT, c, tuple(partial(weigh, (c + 1) * TC + j) for j in range(TC)) if c + 1 < NC else ())
                normalize(N_LN4, c, yT, finT, out_ready)

        @block.gpsimd
        def _(g):
            steps = [0]

            def link(ins):
                steps[0] += 1
                ins.then_inc(pool_step, 1)
                g.wait_ge(pool_step, steps[0])

            def refine(k, c):
                n, done = norms.index((k, c)), pool_norms.index((k, c)) + 1
                g.wait_ge(guess_ready, done)
                y, x, w = rs[:, n, :], var[:, n, :], nw[:, 0, :]
                for i in range(3):
                    link(g.tensor_tensor(w, y, y, ALU.mult))
                    link(g.tensor_tensor(w, w, x, ALU.mult))
                    link(g.tensor_scalar(w, w, -0.5, 1.5, ALU.mult, ALU.add))
                    ins = g.tensor_tensor(y, y, w, ALU.mult)
                    if i < 2:
                        link(ins)
                ins.then_inc(rstd_ready, 1)
                g.wait_ge(rstd_ready, done)

            link(g.memset(ident[:, :], 0.0))
            g.affine_select(out=ident[:, :], in_=ident[:, :], compare_op=ALU.not_equal, fill=1.0, base=0,
                            pattern=[[-1, P]], channel_multiplier=1).then_inc(const_pool, 1)
            g.wait_ge(const_pool, 1)
            g.tensor_copy(identb[:, :], ident[:, :]).then_inc(const_pool, 1)
            link(g.memset(triu[:, :], 1.0))
            g.affine_select(out=triu[:, :], in_=triu[:, :], compare_op=ALU.is_ge, fill=0.0, base=0,
                            pattern=[[1, P]], channel_multiplier=-1).then_inc(const_pool, 1)
            for t, n, lo, step in ((rev4, EPG, EPG, -1), (rev8, E1, E1, -1), (base8, E1, 0, CAP)):
                for e in range(n):
                    ins = g.memset(t[:, e:e + 1], float(lo + e * step))
                    if e < n - 1:
                        link(ins)
                ins.then_inc(const_pool, 1)
            link(g.iota(token_i[:, :], pattern=[[P, NT]], base=SLOTS, channel_multiplier=1))
            g.tensor_copy(spare[:, :], token_i[:, :]).then_inc(const_pool, 1)
            g.memset(vh[:, :, :, :], 1.0).then_inc(const_pool, 1)
            g.memset(w_r[:, E1:], 0.0).then_inc(const_pool, 1)
            g.memset(w_gate[:, 2 + E0:], 0.0).then_inc(const_pool, 1)

            def rows(x):
                return x[:, :].unsqueeze(1).broadcast_to([P, NT, D])

            for c in range(NC):
                g.wait_ge(ld_x[c], 16)
            g.wait_ge(ld_a2, 16 * 7)
            x3 = x0T[:, :].rearrange("p (t d) -> p t d", d=D)
            p3 = pre[:, :].rearrange("p (t d) -> p t d", d=D)
            g.tensor_tensor(p3, x3, rows(bc["d"]), ALU.mult).then_inc(pre_step, 1)
            g.wait_ge(pre_step, 1)
            g.tensor_tensor(p3, p3, rows(bc["bo"]), ALU.add).then_inc(pre_step, 1)
            g.wait_ge(pre_step, 2)
            g.tensor_tensor(pre[:, :], pre[:, :], x0T[:, :], ALU.add).then_inc(pre_step, 1)
            for c in range(NC):
                g.wait_ge(res_ready, 2 * (c + 1))
                for k in range(2):
                    g.tensor_tensor(ck(gated[k], c), ck(gated[k], c), ck(xin[k], c), ALU.mult).then_inc(gated_ready, 1)

            def rotate(w, wr):
                src = w.rearrange("p (n two) -> p n two", two=2)
                dst = wr[:, :].rearrange("p (n two) -> p n two", two=2)
                g.tensor_scalar(dst[:, :, 0], src[:, :, 1], -1.0, None, ALU.mult).then_inc(rot_ready, 1)
                g.tensor_copy(dst[:, :, 1], src[:, :, 0]).then_inc(rot_ready, 1)

            g.wait_ge(ld_b, 112)
            rotate(wq[:, :], wqr)
            refine(N_LN1, 0)
            refine(N_LN1, 1)
            g.wait_ge(wkv_ready, 1)
            rotate(wkv[:, 0, :], wkr)
            refine(N_LN1, 2)

            g.wait_ge(x1T_ready, NT)
            for b in range(HB):
                g.memset(slot[4 + b // 2][64:96, (b % 2) * 1024:(b % 2) * 1024 + 1024], ONE_PAIR).then_inc(ones_ready, 1)
                g.wait_ge(ones_ready, b + 1)

            for c in range(NC):
                for n in range(2):
                    i = 2 * c + n
                    g.wait_ge(part_ready, 4 * c + n + 1)
                    g.tensor_tensor(ck(rope_b(n), c), ck(rope_a(n), c), parts(i)[:, 0, :], ALU.subtract).then_inc(rest_ready, 1)

            g.wait_ge(vT_ready, NC)
            g.wait_ge(const_pool, 8)

            def head(hv, h, lap=0):
                if h >= 2:
                    g.wait_ge(pv_done, (hv - 1) * NT)
                g.tensor_copy(vh[:, h % 2, :, 0:DH],
                              vT[:, :].rearrange("p (t d) -> p t d", d=D)[:, :, bass.ds(hv * DH, DH)]).then_inc(vh_ready, 1)

            head(0, 0)
            head(1, 1)
            with g.Fori(1, H // 2) as it:
                for j in range(2):
                    head(it * 2 + j, 2 + j)

            for k, c in pool_norms[NC - 1:]:
                refine(k, c)

            g.wait_ge(zeroed, 17)
            g.wait_ge(x3T_ready, NT)
            g.wait_ge(dest_ready, 1)
            for t in range(NT):
                g.indirect_dma_start(out=disp[:, :], out_offset=bass.IndirectOffsetOnAxis(ap=dest[:, t:t + 1], axis=0),
                                     in_=tl(x3T, t), in_offset=None).then_inc(scattered, 16)
            g.wait_ge(spare_stored, 16)
            for b in range(4):
                g.wait_ge(eo_stored[b], 32 * (E1 // 4))
            for t in range(NT):
                g.indirect_dma_start(out=tl(combT, t), out_offset=None, in_=eout[:, :],
                                     in_offset=bass.IndirectOffsetOnAxis(ap=dest[:, t:t + 1], axis=0)).then_inc(gathered[t // TC], 16)


_INS = [
    "L0_attn_x", "L0_attn_W_in", "L0_attn_b_in", "L0_attn_W_xp", "L0_attn_b_xp", "L0_attn_W_dt", "L0_attn_b_dt",
    "L0_attn_W_out", "L0_attn_b_out", "L0_attn_A_log", "L0_attn_D", "L0_ffn_Wq", "L0_ffn_Wk_c", "L0_ffn_Wv_c",
    "L0_ffn_Wk", "L0_ffn_Wv", "L0_ffn_Wo", "L0_ffn_W_shared_in", "L0_ffn_W_shared_out", "L0_ffn_W1_shared",
    "L0_ffn_W2_experts", "L0_ffn_Wg_gate", "L0_ffn_We_gate", "L0_ffn_group_bias", "L0_ffn_expert_bias",
    "L0_ffn_norm1_w", "L0_ffn_norm2_w", "L1_attn_gamma", "L1_attn_wq", "L1_attn_wk", "L1_attn_wv", "L1_attn_wa",
    "L1_attn_wg", "L1_attn_wo", "L1_ffn_Wr", "L1_ffn_W1", "L1_ffn_W2",
]


def kernel(**inputs):
    import numpy as np
    import concourse.bacc as bacc
    from concourse.bass_utils import run_bass_kernel_spmd as run

    nc = bacc.Bacc("TRN2", target_bir_lowering=False, num_devices=1)
    arrays, args = {}, {}
    for name in _INS:
        arrays[f"in_{name}"] = np.ascontiguousarray(inputs[name])
    inv_freq = np.float32(1.0) / np.float32(10000.0) ** (np.arange(0, DH, 2, dtype=np.float32) / np.float32(DH))
    angle = np.repeat(inv_freq.astype(np.float32), 2)[:, None] * np.arange(S, dtype=np.float32)[None, :]
    angle = np.tile(angle.astype(np.float32), (H, 1))
    arrays["in_cos"], arrays["in_sin"] = np.cos(angle), np.sin(angle)
    for name, array in arrays.items():
        args[name[3:]] = nc.dram_tensor(name, array.shape, mybir.dt.from_np(array.dtype), kind="ExternalInput").ap()
    out = nc.dram_tensor("out_0", (1, S, D), F32, kind="ExternalOutput").ap()
    scratch = (
        nc.dram_tensor("q_split", (3, P, S), BF16).ap(),
        nc.dram_tensor("k_split", (H, 3, DH, S), BF16).ap(),
        nc.dram_tensor("attn_out", (H, 2, P, CH), F32).ap(),
        nc.dram_tensor("disp", (SLOTS + S, D), F32).ap(),
        nc.dram_tensor("eout", (SLOTS + S, D), F32).ap(),
    )
    build(nc, args, scratch, out)
    r = run(nc, [arrays], core_ids=[0])
    return r.results[0]["out_0"]
```

```python
import math
import struct
from contextlib import ExitStack
from functools import partial

import concourse.bass as bass
from concourse import mybir

F32 = mybir.dt.float32
BF16 = mybir.dt.bfloat16
I32 = mybir.dt.int32
ACT = mybir.ActivationFunctionType
ALU = mybir.AluOpType
AX = mybir.AxisListType

P = 128
D = 128
S = 2048
NT = S // P
CH = 512
NC = S // CH
TC = CH // P
NSTATE = 64
H, DH = 16, 8
HID = 256
E0, EPG = 8, 4
E1, CAP, DFF = 8, 320, 512
SLOTS = E1 * CAP
NST = SLOTS // P
FM = DFF // P
ACC = 1 + TC * E0
LN_EPS, RMS0_EPS, RMS1_EPS = 1e-5, 1e-6, 1e-5
BIG = 1e30
RSQRT_MAGIC = float(0x5F3759DF)
ONE_PAIR = struct.unpack("<f", struct.pack("<I", 0x3F803F80))[0]

TERMS = 72
ROWS = TERMS + 2
HB = 4
AHEAD = 3
PAIRS = 4
PR = 2
STB = 3
RP = 8
LOOPED = 12

N_LN1, N_RMSX, N_RMSO, N_LN2, N_RMS1, N_LN3, N_LN4 = range(7)


def turned_before(e):
    return [0, 1] if e == 0 else [e + 1] if e + 1 < NST // TC else []


def psum_plan():
    first, rest = [], []
    for i in range(3 * NC + 1):
        if i < NC:
            first.append((("xT", i), i % 2))
        if 1 <= i <= NC:
            first += [(("xr", i - 1, m), 2 + m) for m in range(2)]
        if 2 <= i <= NC + 1:
            first.append((("dt", i - 2), 6))
        if i == NC + 1:
            first += [(("xr", c, m), (2 + m + 2 * c) % 4 + 2) for c in (0, 1) for m in (2, 3)]
        if 5 <= i <= NC + 4:
            first += [(("bx", i - 5), (i - 5) % 2), (("mean", i - 5), 7 - (i - 5) % 2)]
        if i == NC + 4:
            first += [(("xr", c, m), (2 + m + 2 * c) % 4 + 2) for c in (2, 3) for m in (2, 3)]
        if 8 <= i <= NC + 7:
            first.append((("ssum", i - 8), i % 2))
        if i in (9, 10):
            first.append(((("wT",), 6), (("wkv",), 7))[i - 9])
        if 9 <= i <= NC + 8:
            first.append((("outA", i - 9), 2 + i - 9))
    for c in range(NC):
        turned = [("x1T", i) for i in ((0, 1) if c == 0 else (c + 1,)) if i < NC]
        first += [(key, 6 + key[1] % 2) for key in turned]
        first += [(key, (5 * c + n) % 6) for n, key in enumerate([(n, c) for n in ("q", "qr", "k", "kr", "v")])]
    rest += [(("wo", c), c) for c in range(NC)]
    rest.append((("xnT", 0), 7))
    for c in range(NC):
        rest += [(("ffn", c, m), m) for m in range(4)]
        rest.append((("xnT", c + 1), 7) if c + 1 < NC else (("gate",), 6))
        rest += [(("ffn", c, m), m) for m in range(4, 8)]
        if c == NC - 2:
            rest.append((("gateF",), 4))
    for t in range(0, NT, 2):
        if t % TC == 0:
            rest.append((("sh", t // TC), (t // TC) % 2))
        rest += [(("rt", t + j, f), 2 + 2 * ((t + f) % 3) + j) for f in range(2) for j in range(2)]
    for c in range(NC + 1):
        if c < NC:
            rest += [(("xrT", c), 6 + c % 2), (("pk", c), 0), (("pv", c), 1), (("pq", c), 2), (("pa", c), 3), (("pg", c), 4)]
        if c >= 1:
            rest.append((("wo1", c - 1), 5))
    rest += [(("x3T", c), 6 + c % 2) for c in range(NC)]
    rest += [(("routeF",), 2), (("route",), 0), (("cum",), 1)]
    for e in range(E1 + 1):
        rest += [(("einT", n), 2 + n % 2) for n in turned_before(e)]
        if e < E1:
            rest += [(("h1", e, m), 4 + m) for m in range(FM)]
        if e >= 1:
            rest.append((("eo", e - 1), (e - 1) % 2))
    plan, fills = {}, [0] * 8
    for order in (first, rest):
        tenant = [None] * 8
        for key, b in order:
            fills[b] += 1
            plan[key] = (b, fills[b], tenant[b])
            tenant[b] = key
        if order is first:
            last = list(tenant)
    return plan, last


def norm_order():
    order = [(k, c) for k in (N_LN1, N_RMSX) for c in range(NC)]
    for j in range(NC + 5):
        order += [(k, j - lag) for k, lag in ((N_RMS1, 2), (N_RMSO, 0), (N_LN2, 1), (N_LN3, 5)) if 0 <= j - lag < NC]
    return order + [(N_LN4, c) for c in range(NC)]


def build(nc, a, scratch, out):
    plan, before_attention = psum_plan()
    norms = norm_order()
    own = [(N_RMSX, 0), (N_LN4, 0), (N_LN4, 1)]
    pool_norms = [(k, c) for k, c in norms if c < NC - 1 and (k, c) not in own]
    with ExitStack() as ctx:
        def sb(name, shape, dt=F32):
            return ctx.enter_context(nc.sbuf_tensor(name, shape, dt))

        def sem(name):
            return ctx.enter_context(nc.semaphore(name))

        bank = [ctx.enter_context(nc.psum_tensor(f"bank{i}", [P, CH], F32)) for i in range(3)]
        maxps = [ctx.enter_context(nc.psum_tensor(f"maxps{i}", [P, 2 * CH], F32)) for i in range(2)]
        pvps = ctx.enter_context(nc.psum_tensor("pvps", [P, CH], F32))
        bank_ap = [bank[0][:, :], bank[1][:, :], bank[2][:, :], maxps[0][:, 0:CH], maxps[0][:, CH:],
                   maxps[1][:, 0:CH], maxps[1][:, CH:], pvps[:, :]]

        slot = [sb(f"slot{i}", [P, S]) for i in range(18)]

        def two(i):
            return [slot[i], slot[i + 1]]

        x0T, x0F = slot[0], slot[1]
        xin, gated = two(2), two(4)
        sp_abs, sp_relu = slot[6], slot[7]
        aF, bxF, stF = slot[8], slot[9], slot[10]
        pre, x1T, x1F = slot[11], slot[12], slot[1]
        cosF, sinF = slot[13], slot[14]
        vT = slot[15]
        heads_q = [slot[2 + i // 2][:, (i % 2) * 1024:(i % 2) * 1024 + 1024].bitcast(BF16) for i in range(HB)]
        heads_k = [slot[4 + i // 2][:, (i % 2) * 1024:(i % 2) * 1024 + 1024].bitcast(BF16) for i in range(HB)]
        prob = [slot[16], slot[17]]
        copied = slot[0]
        running = [slot[10 + i // PAIRS][:, (i % PAIRS) * CH:(i % PAIRS + 1) * CH] for i in range(2 * PAIRS)]
        pv_sb = slot[0][:, :].rearrange("p (k b q) -> p k b q", k=2, b=2)
        numF, rdenF = slot[6], slot[7]
        xnT, xnF = slot[8], slot[1]
        act_ff = slot[9]
        hid = [two(2), two(4)]
        oT = slot[10]
        x2T, xrT, xrF = slot[0], slot[11], slot[1]
        qF, kvF, decF, gsF, kF, hsF, yF = slot[13], slot[6], slot[7], slot[2], slot[3], slot[4], slot[5]
        x3T, x3F = slot[12], slot[1]
        w1 = [slot[14], slot[15]]
        w2 = [slot[16], slot[17]]
        einT = [slot[2], slot[3]]
        einF = [slot[4], slot[5]]
        hE = [slot[6], slot[7]]
        eoT = slot[8]
        combT, finT, yT = slot[9], slot[10], slot[11]

        w_in = sb("w_in", [P, 512])
        w_xp = sb("w_xp", [P, 2, NSTATE])
        w_dt = sb("w_dt", [P, 2, D])
        w_out = sb("w_out", [P, 2, D])
        b_in = sb("b_in", [P, 4])
        b_xp = sb("b_xp", [NSTATE, 1])
        b_dt = sb("b_dt", [P, 1])
        a_log = sb("a_log", [P, 1])
        a_exp = sb("a_exp", [P, 1])
        a_neg = sb("a_neg", [P, 1])
        bc = {n: sb(f"bc_{n}", [P, D]) for n in ("d", "bo", "n1", "n2")}
        wq = sb("wq", [P, D])
        wqr = sb("wqr", [P, D])
        wkvc = sb("wkvc", [P, 64])
        wk = sb("wk", [32, D])
        wcT = sb("wcT", [32, 2, P])
        wkv = sb("wkv", [P, 2, D])
        wkr = sb("wkr", [P, D])
        wv = sb("wv", [32, D])
        wo = sb("wo", [P, D])
        w_ff = sb("w_ff", [P, 2, 512])
        w_so = sb("w_so", [P, 2, D])
        w2e = sb("w2e", [P, 2, E0 * D])
        w_gate = sb("w_gate", [P, 32])
        logitF = sb("logitF", [P, CH])
        b_gate = sb("b_gate", [P, 2 + E0])
        w_l1 = {n: sb(f"l1_{n}", [P, D]) for n in ("q", "k", "v", "a", "g", "o")}
        gamma = sb("gamma", [P, 1])
        w_r = sb("w_r", [P, 32])

        ident = sb("ident", [P, P])
        identb = sb("identb", [P, P], BF16)
        ones = sb("ones", [P, P])
        mean_w = sb("mean_w", [P, NSTATE])
        triu = sb("triu", [P, P], BF16)
        onesb = sb("onesb", [P, P], BF16)
        rev4 = sb("rev4", [P, EPG])
        rev8 = sb("rev8", [P, E1])
        base8 = sb("base8", [P, E1])
        keep_scan = sb("keep_scan", [P, E1 * NT])
        token_i = sb("token_i", [P, NT], I32)
        spare = sb("spare", [P, NT])
        zeros = sb("zeros", [P, 512])

        bn = sb("bn", [P, 2, TC, 6])
        mv = sb("mv", [P, 7 * NC, TC, 2])
        msq = sb("msq", [P, 7 * NC, TC])
        var = sb("var", [P, 7 * NC, TC])
        rs = sb("rs", [P, 7 * NC, TC])
        nw = sb("nw", [P, 2, TC])
        maxes = sb("maxes", [P, 2, NT, 2])
        mneg = sb("mneg", [P, NT])
        mparts = sb("mparts", [P, 2 * NT], BF16)
        mrows = sb("mrows", [2 * NT, P], BF16)
        vh = sb("vh", [P, 2, NT, 32])
        gl = sb("gl", [P, NT, 2 + E0])
        g_s = sb("g_s", [P, 12, NT])
        g4 = sb("g4", [P, 12, NT, EPG])
        wtop = sb("wtop", [P, NT, E0])
        r8 = sb("r8", [P, 6, NT, E1])
        onehot = sb("onehot", [P, E1, NT], BF16)
        et = sb("et", [P, 4, E1, NT])
        r_s = sb("r_s", [P, 12, NT])
        dest = sb("dest", [P, NT], I32)

        ld_x = [sem(f"ld_x{c}") for c in range(NC)]
        ld_a, ld_a1, ld_a2, ld_b, ld_c, ld_d, ld_e = (sem(f"ld_{n}") for n in ("w_in", "w_dt", "layer0", "attn", "ffn", "layer1", "experts"))
        logitF_ready = sem("logitF_ready")
        const_pool, const_dve, zeroed = sem("const_pool"), sem("const_dve"), sem("zeroed")
        bank_full = [sem(f"bank_full{i}") for i in range(8)]
        resid_ready, acc_ready = sem("resid_ready"), sem("acc_ready")
        relu_act, relu_dve, comb_ready = sem("relu_act"), sem("relu_dve"), sem("comb_ready")
        res_ready = sem("res_ready")
        x0F_ready, silu_ready, u_ready = sem("x0F_ready"), sem("silu_ready"), sem("u_ready")
        gated_ready, gated_dve = sem("gated_ready"), sem("gated_dve")
        relu_ready, absu_ready, expu_ready, sp_ready, delta_ready = sem("relu_ready"), sem("absu_ready"), sem("expu_ready"), sem("sp_ready"), sem("delta_ready")
        aexp_ready, aneg_ready, decay_ready, bx_ready = sem("aexp_ready"), sem("aneg_ready"), sem("decay_ready"), sem("bx_ready")
        state_ready, y_ready, pre_step = sem("state_ready"), sem("y_ready"), sem("pre_step")
        dve_step = sem("dve_step")
        pool_step = sem("pool_step")
        guess_ready, rstd_ready = sem("guess_ready"), sem("rstd_ready")
        x1T_ready, x1F_ready = sem("x1T_ready"), sem("x1F_ready")
        wcT_ready, wkv_ready = sem("wcT_ready"), sem("wkv_ready")
        rot_ready, rope_ready, vT_ready = sem("rot_ready"), sem("rope_ready"), sem("vT_ready")
        sum_ready, part_ready, rest_ready = sem("sum_ready"), sem("part_ready"), sem("rest_ready")
        rest_dve, third_q, third_k = sem("rest_dve"), sem("third_q"), sem("third_k")
        split_stored = sem("split_stored")
        head_loaded = [sem(f"head_loaded{b}") for b in range(HB)]
        ones_ready, vh_ready = sem("ones_ready"), sem("vh_ready")
        st_full, exp_done, pv_done, pv_out = sem("st_full"), sem("exp_done"), sem("pv_done"), sem("pv_out")
        pv_stored = [sem(f"pv_stored{b}") for b in range(2)]
        mx_full, mx_free, mparts_ready = sem("mx_full"), sem("mx_free"), sem("mparts_ready")
        mcomb = sem("mcomb")
        half_copied, scan_done = sem("half_copied"), sem("scan_done")
        mt_full, mrows_ready, mrows_placed = sem("mt_full"), sem("mrows_ready"), sem("mrows_placed")
        rcp_ready, attn_loaded = sem("rcp_ready"), sem("attn_loaded")
        last_head_loaded = [sem(f"last_head_loaded{c}") for c in range(NC)]
        attn_ready = sem("attn_ready")
        xnT_ready, xnF_ready, silu0_ready, hid_ready = sem("xnT_ready"), sem("xnF_ready"), sem("silu0_ready"), sem("hid_ready")
        gate_ready, gexp_in, gexp_ready, wtop_ready = sem("gate_ready"), sem("gexp_in"), sem("gexp_ready"), sem("wtop_ready")
        x2T_ready, xrT_ready, xrF_ready = sem("x2T_ready"), sem("xrT_ready"), sem("xrF_ready")
        l1_act, kv_ready, hs_ready, y1_ready = sem("l1_act"), sem("kv_ready"), sem("hs_ready"), sem("y1_ready")
        x3T_ready, x3F_ready = sem("x3T_ready"), sem("x3F_ready")
        rexp_in, rexp_ready, onehot_ready, dest_ready = sem("rexp_in"), sem("rexp_ready"), sem("onehot_ready"), sem("dest_ready")
        scattered, spare_stored, einF_ready = sem("scattered"), sem("spare_stored"), sem("einF_ready")
        ein_loaded = [sem(f"ein_loaded{n}") for n in range(NST // TC)]
        eo_ready = sem("eo_ready")
        eo_stored = [sem(f"eo_stored{b}") for b in range(4)]
        gathered = [sem(f"gathered{c}") for c in range(NC)]
        out_ready, out_stored = sem("out_ready"), sem("out_stored")

        q_split, k_split, attn_out, disp, eout = scratch

        def ck(t, c, n=CH):
            return t[:, c * n:(c + 1) * n]

        def tl(t, i):
            return t[:, i * P:(i + 1) * P]

        def full(eng, key):
            b, n, _ = plan[key]
            eng.wait_ge(bank_full[b], n)
            return bank_ap[b]

        def released(key):
            kind, c = key[0], key[1] if len(key) > 1 else 0
            m = key[2] if len(key) > 2 else 0
            return {
                "xT": (x0F_ready, c + 1), "xr": (silu_ready, 2 * c + m + 1) if m < 2 else (res_ready, 2 * c + m - 1), "dt": (u_ready, c + 1),
                "bx": (bx_ready, c + 1), "mean": (decay_ready, c + 1), "ssum": (y_ready, 2 * c + 2),
                "outA": (resid_ready, c + 1), "x1T": (x1F_ready, c + 1),
                "q": (rope_ready, 4 * c + 1), "qr": (rope_ready, 4 * c + 2),
                "k": (rope_ready, 4 * c + 3), "kr": (rope_ready, 4 * c + 4),
                "wT": (wcT_ready, 1), "wkv": (wkv_ready, 1), "v": (vT_ready, c + 1),
                "wo": (resid_ready, NC + c + 1), "xnT": (xnF_ready, c + 1), "gate": (gate_ready, 1),
                "gateF": (logitF_ready, 1), "routeF": (logitF_ready, 2),
                "ffn": (silu0_ready, 4 * c + m % 4 % 2 + 2 * (m // 4) + 1) if m % 4 < 2
                else (hid_ready, 4 * c + m % 2 + 2 * (m // 4) + 1),
                "sh": (acc_ready, ACC * c + 1),
                "rt": (acc_ready, ACC * (c // TC) + 1 + 16 * (c % TC // 2) + 8 * m + 7 + c % 2),
                "xrT": (xrF_ready, c + 1),
                "pk": (l1_act, 4 * c + 1), "pq": (l1_act, 4 * c + 2), "pa": (l1_act, 4 * c + 3 + c % 2),
                "pg": (l1_act, 4 * c + 4 - c % 2), "pv": (kv_ready, c + 1),
                "wo1": (resid_ready, 2 * NC + c + 1), "x3T": (x3F_ready, c + 1),
                "route": (gate_ready, 2), "cum": (comb_ready, 1), "einT": (einF_ready, c + 1),
                "h1": (relu_act if m % 2 == 0 else relu_dve, 2 * c + m // 2 + 1),
                "eo": (eo_ready, 2 * c + 2),
            }[kind]

        def parts(i):
            t = slot[[16, 17, 2, 3][i // 2]][:, (i % 2) * 1024:(i % 2) * 1024 + 768].bitcast(BF16)
            return t.rearrange("p (s q) -> p s q", s=3)

        units = [(h, t, f) for h, tiles in ((0, NT), (1, AHEAD)) for t in range(tiles) for f in range(2)]
        pair = [(3, 4), (5, 6), (0, 1), (2, 7)]
        assert len(pair) == PAIRS and 2 * AHEAD - PAIRS == 2

        def pieces(e):
            lo, hi = e * CAP, (e + 1) * CAP
            if lo < S < hi:
                return [(0, lo, S), (1, S, hi)]
            return [(lo // S, lo, hi)]

        def rope_a(n):
            return [slot[6], slot[10]][n]

        def rope_b(n):
            return [slot[7], slot[11]][n]

        def take_expert(act, e):
            o = full(act, ("eo", e))
            if e >= 4:
                act.wait_ge(eo_stored[e % 4], 32 * (e // 4))
            dst = eoT[:, (e % 4) * 512:(e % 4) * 512 + 384]
            act.activation(dst[:, 0:256], o[:, 0:256], ACT.Copy).then_inc(eo_ready, 1)
            act.activation(dst[0:64, 256:384], o[0:64, 256:384], ACT.Copy).then_inc(eo_ready, 1)

        block = ctx.enter_context(nc.Block())

        @block.sync
        def _(sp):
            xt = a["L0_attn_x"].rearrange("b (t p) d -> p (b t) d", p=P)
            col = lambda v: v.rearrange("(p o) -> p o", o=1)
            row = lambda v: v.rearrange("(o n) -> o n", o=1)

            def load_x(c):
                sp.dma_start(ck(x0T, c).rearrange("p (t d) -> p t d", d=D), xt[:, c * TC:(c + 1) * TC, :]).then_inc(ld_x[c], 16)

            load_x(0)
            sp.dma_start(w_in[:, :], a["L0_attn_W_in"]).then_inc(ld_a, 16)
            sp.dma_start(b_in[:, :], a["L0_attn_b_in"].rearrange("(m p) -> p m", p=P),
                         allow_slow_non_contiguous=True).then_inc(ld_a, 16)
            load_x(1)
            sp.dma_start(w_dt[:, :, :], a["L0_attn_W_dt"].rearrange("(k p) n -> p k n", p=P)).then_inc(ld_a1, 16)
            sp.dma_start(b_dt[:, :], col(a["L0_attn_b_dt"])).then_inc(ld_a1, 16)
            load_x(2)
            load_x(3)
            for dst, src in ((a_log[NSTATE:P, :], col(a["L0_attn_A_log"])),
                             (w_xp[:, :, :], a["L0_attn_W_xp"].rearrange("(k p) n -> p k n", p=P)),
                             (b_xp[:, :], col(a["L0_attn_b_xp"])),
                             (bc["d"][:, :], row(a["L0_attn_D"]).broadcast_to([P, D])),
                             (bc["bo"][:, :], row(a["L0_attn_b_out"]).broadcast_to([P, D])),
                             (w_out[:, :, :], a["L0_attn_W_out"].rearrange("(k p) n -> p k n", p=P)),
                             (w_r[:, 0:E1], a["L1_ffn_Wr"])):
                sp.dma_start(dst, src).then_inc(ld_a2, 16)
            for dst, src in ((wq[:, :], a["L0_ffn_Wq"]), (wkvc[:, 0:32], a["L0_ffn_Wk_c"]),
                             (wkvc[:, 32:64], a["L0_ffn_Wv_c"]), (wk[:, :], a["L0_ffn_Wk"]),
                             (wv[:, :], a["L0_ffn_Wv"]), (cosF[:, :], a["cos"]), (sinF[:, :], a["sin"])):
                sp.dma_start(dst, src).then_inc(ld_b, 16)
            sp.wait_ge(zeroed, 1)
            sp.dma_start(disp[0:SLOTS, :].rearrange("(p a) d -> p (a d)", p=P)[:, 0:2560].rearrange("p (b n) -> p b n", n=512),
                         zeros[:, :].rearrange("p (o n) -> p o n", o=1).broadcast_to([P, 5, 512])).then_inc(zeroed, 16)
            for dst, src in ((wo[:, :], a["L0_ffn_Wo"]), (w_ff[:, 0, :], a["L0_ffn_W_shared_in"]),
                             (w_ff[:, 1, :], a["L0_ffn_W1_shared"]),
                             (w_so[:, :, :], a["L0_ffn_W_shared_out"].rearrange("(k p) n -> p k n", p=P)),
                             (w2e[:, 0, :].rearrange("p (e n) -> p e n", e=E0), a["L0_ffn_W2_experts"][:, 0:P, :].rearrange("e p n -> p e n")),
                             (w2e[:, 1, :].rearrange("p (e n) -> p e n", e=E0), a["L0_ffn_W2_experts"][:, P:HID, :].rearrange("e p n -> p e n")),
                             (w_gate[:, 0:2], a["L0_ffn_Wg_gate"]), (w_gate[:, 2:2 + E0], a["L0_ffn_We_gate"]),
                             (b_gate[:, 0:2], row(a["L0_ffn_group_bias"]).broadcast_to([P, 2])),
                             (b_gate[:, 2:], row(a["L0_ffn_expert_bias"]).broadcast_to([P, E0])),
                             (bc["n1"][:, :], row(a["L0_ffn_norm1_w"]).broadcast_to([P, D])),
                             (bc["n2"][:, :], row(a["L0_ffn_norm2_w"]).broadcast_to([P, D]))):
                sp.dma_start(dst, src).then_inc(ld_c, 16)
            for n in ("q", "k", "v", "a", "g", "o"):
                sp.dma_start(w_l1[n][:, :], a[f"L1_attn_w{n}"]).then_inc(ld_d, 16)
            sp.dma_start(gamma[:, :], col(a["L1_attn_gamma"])).then_inc(ld_d, 16)

            for c in range(NC):
                i = 2 * c + 1
                for part in range(3):
                    if part < 2:
                        sp.wait_ge(part_ready, 4 * c + 2 * part + 2)
                    else:
                        sp.wait_ge(third_q, c + 1)
                        sp.dma_start(q_split[:, :, c * CH:(c + 1) * CH].rearrange("s p q -> p s q"),
                                     parts(i - 1)).then_inc(split_stored, 16)
                        sp.wait_ge(third_k, c + 1)
                    sp.dma_start(k_split[:, part, :, c * CH:(c + 1) * CH],
                                 parts(i)[:, part, :]).then_inc(split_stored, 16)

            def load_head(hv, b):
                q = q_split[:, bass.ds(hv * DH, DH), :]
                k = k_split[bass.ds(hv, 1)].rearrange("o s r q -> o (s r) q")
                sp.dma_start(heads_k[b][0:TERMS, :], k.broadcast_to([3, 3 * DH, S])).then_inc(head_loaded[b], 16)
                for i in range(3):
                    sp.dma_start(heads_q[b][i * 3 * DH:(i + 1) * 3 * DH, :],
                                 q[i:i + 1].broadcast_to([3, DH, S])).then_inc(head_loaded[b], 16)

            def place_max(b):
                for s in range(2):
                    sp.dma_start(heads_q[b][TERMS + s:TERMS + s + 1, :].rearrange("o (t p) -> o t p", p=P),
                                 mrows[s * NT:(s + 1) * NT, :]).then_inc(mrows_placed, 16)

            sp.wait_ge(split_stored, 16 * 4 * NC)
            sp.wait_ge(ones_ready, HB)
            for h in range(3):
                load_head(h, h)
            sp.wait_ge(mrows_ready, 1)
            place_max(0)

            def head(hv, h, lap=0):
                if h + 3 < H:
                    if not (isinstance(hv, int) and hv == 0):
                        sp.wait_ge(st_full, hv * (NT * NC))
                    load_head(hv + 3, (h + 3) % HB)
                if h >= 1:
                    store_out(hv - 1, (h - 1) % 2)
                if h + 1 < H:
                    sp.wait_ge(mrows_ready, hv + 2)
                    place_max((h + 1) % HB)

            def store_out(hv, b):
                sp.wait_ge(rcp_ready, (hv + 1) * RP)
                sp.dma_start(attn_out[bass.ds(hv, 1)].rearrange("o k p q -> p (o k) q"), pv_sb[:, :, b, :]).then_inc(pv_stored[b], 16)

            head(0, 0)
            for h in range(1, 4):
                head(h, h)
            with sp.Fori(1, LOOPED // 4) as it:
                for j in range(4):
                    head(it * 4 + j, 4 + j, it - 1)
            for h in range(LOOPED, H):
                head(h, h)
            for b in range(2):
                sp.wait_ge(pv_stored[b], 16 * (H // 2 - b))
            for c in range(NC):
                for k, t in ((0, numF), (1, rdenF)):
                    src = attn_out[0:H - 1, k].rearrange("h (c r) q -> c h r q", c=NC)[c]
                    sp.dma_start(ck(t, c)[0:(H - 1) * DH, :], src[:, k * DH:(k + 1) * DH, :]).then_inc(attn_loaded, 16)
            sp.wait_ge(pv_out, H)
            for k, t in ((0, numF), (1, rdenF)):
                if k == 1:
                    sp.wait_ge(rcp_ready, H * RP)
                for c in range(NC):
                    r0 = 32 * c + k * DH
                    sp.dma_start(ck(t, c)[(H - 1) * DH:, :], pv_sb[r0:r0 + DH, k, (H - 1) % 2, :]).then_inc(last_head_loaded[c], 16)

            sp.wait_ge(pv_done, NT * H)
            sp.wait_ge(vh_ready, H)
            for i in range(2):
                sp.dma_start(w1[i][:, :].rearrange("p (e f) -> p e f", f=DFF),
                             a["L1_ffn_W1"][4 * i:4 * i + 4].rearrange("e p f -> p e f")).then_inc(ld_e, 16)
                sp.dma_start(w2[i][:, :].rearrange("p (e n) -> p e n", n=D),
                             a["L1_ffn_W2"][4 * i:4 * i + 4].rearrange("e (k p) n -> p (e k) n", p=P)).then_inc(ld_e, 16)

            sp.wait_ge(x3T_ready, NC * TC)
            sp.dma_start(eout[SLOTS:SLOTS + S, :].rearrange("(t p) d -> p t d", p=P),
                         x3T[:, :].rearrange("p (t d) -> p t d", d=D)).then_inc(spare_stored, 16)
            sp.wait_ge(scattered, 16 * NT)
            for n in range(NST // TC):
                dst = einT[n // 4][:, (n % 4) * CH:(n % 4 + 1) * CH]
                sp.dma_start(dst.rearrange("p (t d) -> p t d", d=D),
                             disp[n * CH:(n + 1) * CH, :].rearrange("(t p) d -> p t d", p=P)).then_inc(ein_loaded[n], 16)
            for e in range(E1):
                sp.wait_ge(eo_ready, 2 * (e + 1))
                src = eoT[:, (e % 4) * 512:(e % 4) * 512 + 384]
                sp.dma_start(eout[e * CAP:e * CAP + 256, :].rearrange("(t p) d -> p t d", p=P),
                             src[:, 0:256].rearrange("p (t d) -> p t d", d=D)).then_inc(eo_stored[e % 4], 16)
                sp.dma_start(eout[e * CAP + 256:(e + 1) * CAP, :], src[0:64, 256:384]).then_inc(eo_stored[e % 4], 16)
            for c in range(NC):
                sp.wait_ge(out_ready, TC * (c + 1))
                sp.dma_start(out.rearrange("b (t p) d -> p (b t) d", p=P)[:, c * TC:(c + 1) * TC, :],
                             ck(yT, c).rearrange("p (t d) -> p t d", d=D)).then_inc(out_stored, 16)
            sp.wait_ge(out_stored, 16 * NC)

        @block.tensor
        def _(pe):
            def fill(key):
                b, _, before = plan[key]
                if before:
                    pe.wait_ge(*released(before))
                return bank_ap[b], bank_full[b]

            def logits(key, xF, ready, w):
                pe.wait_ge(const_pool, 10)
                pe.wait_ge(ready, NC)
                o, s = fill(key)
                for c in range(NC):
                    mm = pe.matmul(o[32 * c:32 * (c + 1), :], w[:, :], ck(xF, c), start=True, stop=True)
                mm.then_inc(s, 1)

            def transposes(key, src):
                o, s = fill(key)
                for j in range(TC):
                    mm = pe.transpose(tl(o, j), tl(src, j), ident[:, :])
                mm.then_inc(s, 1)

            pe.wait_ge(const_pool, 2)
            def project(c, m):
                o, s = fill(("xr", c, m))
                pe.matmul(o, w_in[:, m * P:(m + 1) * P], ck(x0F, c), start=True, stop=True).then_inc(s, 1)

            for i in range(3 * NC + 1):
                if i < NC:
                    pe.wait_ge(ld_x[i], 16)
                    transposes(("xT", i), ck(x0T, i))
                if 1 <= i <= NC:
                    c = i - 1
                    if c == 0:
                        pe.wait_ge(ld_a, 32)
                    pe.wait_ge(x0F_ready, c + 1)
                    for m in range(2):
                        project(c, m)
                if 2 <= i <= NC + 1:
                    c = i - 2
                    pe.wait_ge(silu_ready, 2 * c + 2)
                    if c == 0:
                        pe.wait_ge(ld_a1, 32)
                        pe.wait_ge(const_dve, 4)
                    o, s = fill(("dt", c))
                    pe.matmul(o, w_dt[:, 0, :], ck(xin[0], c), start=True, stop=False)
                    pe.matmul(o, w_dt[:, 1, :], ck(xin[1], c), start=False, stop=True).then_inc(s, 1)
                if i == NC + 1:
                    for c in (0, 1):
                        project(c, 2)
                        project(c, 3)
                if 5 <= i <= NC + 4:
                    c = i - 5
                    pe.wait_ge(delta_ready, c + 1)
                    if c == 0:
                        pe.wait_ge(ld_a2, 16 * 7)
                    o, s = fill(("bx", c))
                    pe.matmul(o[0:NSTATE, :], w_xp[:, 0, :], ck(xin[0], c), start=True, stop=False)
                    o2, s2 = fill(("mean", c))
                    pe.matmul(o2[NSTATE:P, :], mean_w[:, :], ck(sp_relu, c), start=True, stop=True).then_inc(s2, 1)
                    pe.matmul(o[0:NSTATE, :], w_xp[:, 1, :], ck(xin[1], c), start=False, stop=True).then_inc(s, 1)
                if i == NC + 4:
                    for c in (2, 3):
                        project(c, 2)
                        project(c, 3)
                if 8 <= i <= NC + 7:
                    c = i - 8
                    pe.wait_ge(state_ready, c + 1)
                    o, s = fill(("ssum", c))
                    pe.matmul(o, ones[0:NSTATE, :], ck(stF, c)[0:NSTATE, :], start=True, stop=True).then_inc(s, 1)
                if i == 9:
                    pe.wait_ge(ld_b, 112)
                    o, s = fill(("wT",))
                    pe.transpose(o[0:32, 0:P], wkvc[:, 0:32], ident[:, :])
                    pe.transpose(o[0:32, P:2 * P], wkvc[:, 32:64], ident[:, :]).then_inc(s, 1)
                if i == 10:
                    pe.wait_ge(wcT_ready, 1)
                    o, s = fill(("wkv",))
                    pe.matmul(tl(o, 0), wcT[:, 0, :], wk[:, :], start=True, stop=True)
                    pe.matmul(tl(o, 1), wcT[:, 1, :], wv[:, :], start=True, stop=True).then_inc(s, 1)
                if 9 <= i <= NC + 8:
                    c = i - 9
                    pe.wait_ge(y_ready, 2 * (c + 1))
                    o, s = fill(("outA", c))
                    for j in range(TC):
                        t = c * TC + j
                        pe.matmul(tl(o, j), tl(gated[0], t), w_out[:, 0, :], start=True, stop=False)
                        mm = pe.matmul(tl(o, j), tl(gated[1], t), w_out[:, 1, :], start=False, stop=True)
                    mm.then_inc(s, 1)

            pe.wait_ge(rot_ready, 4)
            for c in range(NC):
                for i in ((0, 1) if c == 0 else (c + 1,)):
                    if i < NC:
                        pe.wait_ge(x1T_ready, TC * (i + 1))
                        transposes(("x1T", i), ck(x1T, i))
                pe.wait_ge(x1F_ready, c + 1)
                x = ck(x1F, c)
                for key, w in (("q", wq[:, :]), ("qr", wqr[:, :]), ("k", wkv[:, 0, :]), ("kr", wkr[:, :])):
                    o, s = fill((key, c))
                    pe.matmul(o, w, x, start=True, stop=True).then_inc(s, 1)
                o, s = fill(("v", c))
                for j in range(TC):
                    mm = pe.matmul(tl(o, j), tl(x1F, c * TC + j), wkv[:, 1, :], start=True, stop=True)
                mm.then_inc(s, 1)

            for key in before_attention:
                pe.wait_ge(*released(key))

            def max_half(hv, h, t, f):
                n = 32 * h + 2 * t + f
                if n >= 2:
                    pe.wait_ge(mx_free, hv * 32 + (2 * t + f - 1))
                if f == 1 and h >= 1 and t == 1:
                    pe.wait_ge(mrows_ready, hv)
                b = h % HB
                for i in range(2):
                    k0 = f * 1024 + i * CH
                    mm = pe.matmul(maxps[f][:, i * CH:(i + 1) * CH], heads_q[b][0:TERMS, t * P:(t + 1) * P],
                                   heads_k[b][0:TERMS, k0:k0 + CH], start=True, stop=True)
                mm.then_inc(mx_full, 1)

            def max_turn(hv, h, ps=maxps[1]):
                pe.wait_ge(mparts_ready, hv + 1)
                if ps is not pvps:
                    pe.wait_ge(mx_free, (hv + 1) * 32 + (2 if h + 1 < H else 0))
                pe.transpose(ps[0:2 * NT, 0:P // 2].bitcast(BF16), mparts[:, :], identb[:, :]).then_inc(mt_full, 1)

            def score(hv, h, g, c):
                u = g * NC + c
                if u >= STB:
                    pe.wait_ge(exp_done, hv * 64 + (u - STB + 1))
                elif h >= 1:
                    pe.wait_ge(exp_done, hv * 64 - (63 - u) % STB)
                b = h % HB
                pe.matmul(bank[u % STB][:, :], heads_k[b][0:ROWS, g * P:(g + 1) * P],
                          heads_q[b][0:ROWS, c * CH:(c + 1) * CH], start=True, stop=True).then_inc(st_full, 1)

            def weigh(hv, h, g):
                pe.wait_ge(exp_done, hv * 64 + NC * (g + 1))
                if g == 0:
                    pe.wait_ge(vh_ready, hv + 1)
                    if h >= 1:
                        pe.wait_ge(pv_out, hv)
                for c in range(NC):
                    mm = pe.matmul(pvps[32 * c:32 * c + 32, :], vh[:, h % 2, g, :],
                                   prob[g % PR][:, c * CH:(c + 1) * CH], start=(g == 0), stop=(g == NT - 1))
                mm.then_inc(pv_done, 1)

            def head(hv, h, lap=0):
                pe.wait_ge(mrows_placed, (hv + 1) * 32)
                for g in range(NT):
                    t, k = (g + AHEAD, 1) if g + AHEAD < NT else (g + AHEAD - NT, 2)
                    more = h + k < H
                    if more and t == 0:
                        pe.wait_ge(head_loaded[(h + 2) % HB], ((h + 2) // HB + 1 + lap) * 64)
                    score(hv, h, g, 0)
                    score(hv, h, g, 1)
                    if more:
                        max_half(hv + k, h + k, t, 0)
                    score(hv, h, g, 2)
                    score(hv, h, g, 3)
                    turn = g == NT + 1 - AHEAD and h + 1 < H
                    if turn:
                        max_turn(hv + 1, h + 1)
                    elif more:
                        max_half(hv + k, h + k, t, 1)
                    if g >= 1:
                        weigh(hv, h, g - 1)
                    elif h >= 1:
                        weigh(hv - 1, h - 1, NT - 1)
                    if turn and more:
                        max_half(hv + k, h + k, t, 1)

            pe.wait_ge(ones_ready, HB)
            pe.wait_ge(head_loaded[0], 64)
            for u, (h, t, f) in enumerate(units):
                if h == 1 and t == 0 and f == 0:
                    pe.wait_ge(head_loaded[1], 64)
                if u >= PAIRS:
                    pe.wait_ge(half_copied, u - PAIRS + 1)
                    pe.wait_ge(scan_done, u - PAIRS + 1)
                if h == 1 and u % PAIRS == PAIRS - 1:
                    max_turn(0, 0, pvps)
                    pe.wait_ge(mrows_ready, 1)
                for i, b in enumerate(pair[u % PAIRS]):
                    k0 = (2 * f + i) * CH
                    mm = pe.matmul(bank_ap[b], heads_q[h][0:TERMS, t * P:(t + 1) * P],
                                   heads_k[h][0:TERMS, k0:k0 + CH], start=True, stop=True)
                mm.then_inc(mx_full, 1)
            pe.wait_ge(half_copied, len(units) - 2)
            pe.wait_ge(scan_done, len(units) - 2)
            for h in range(4):
                head(h, h)
            with pe.Fori(1, LOOPED // 4) as it:
                for j in range(4):
                    head(it * 4 + j, 4 + j, it - 1)
            for h in range(LOOPED, H):
                head(h, h)
            weigh(H - 1, H - 1, NT - 1)

            pe.wait_ge(exp_done, 64 * H)
            pe.wait_ge(mx_free, 32 * H)
            pe.wait_ge(mrows_ready, H)
            pe.wait_ge(pv_out, H)
            pe.wait_ge(ld_c, 192)
            for c in range(NC):
                pe.wait_ge(attn_ready, c + 2)
                o, s = fill(("wo", c))
                for j in range(TC):
                    mm = pe.matmul(tl(o, j), tl(numF, c * TC + j), wo[:, :], start=True, stop=True)
                mm.then_inc(s, 1)
            def turn_xn(c):
                pe.wait_ge(xnT_ready, TC * (c + 1))
                transposes(("xnT", c), ck(xnT, c))

            def hidden(c, m0):
                pe.wait_ge(xnF_ready, c + 1)
                for m in range(m0, m0 + 4):
                    o, s = fill(("ffn", c, m))
                    pe.matmul(o, w_ff[:, m // 4, (m % 4) * P:(m % 4 + 1) * P], ck(xnF, c), start=True, stop=True).then_inc(s, 1)

            turn_xn(0)
            for c in range(NC):
                hidden(c, 0)
                if c + 1 < NC:
                    turn_xn(c + 1)
                else:
                    pe.wait_ge(logitF_ready, 1)
                    transposes(("gate",), logitF)
                hidden(c, 4)
                if c == NC - 2:
                    logits(("gateF",), xnF, xnF_ready, w_gate)
            for t in range(0, NT, 2):
                c = t // TC
                pe.wait_ge(hid_ready, 4 * (c + 1))
                if t % TC == 0:
                    sh, s_sh = fill(("sh", c))
                    for j in range(TC):
                        for k in range(2):
                            mm = pe.matmul(tl(sh, j), tl(hid[0][k], t + j), w_so[:, k, :], start=(k == 0), stop=(k == 1))
                    mm.then_inc(s_sh, 1)
                for f, j in ((0, 0), (0, 1), (1, 0), (1, 1)):
                    o, s = fill(("rt", t + j, f))
                    for k in range(2):
                        mm = pe.matmul(o, tl(hid[1][k], t + j), w2e[:, k, f * CH:(f + 1) * CH], start=(k == 0), stop=(k == 1))
                    mm.then_inc(s, 1)
            pe.wait_ge(ld_d, 112)
            for i in range(NC + 1):
                if i < NC:
                    pe.wait_ge(xrT_ready, TC * (i + 1))
                    transposes(("xrT", i), ck(xrT, i))
                    pe.wait_ge(xrF_ready, i + 1)
                    for key, w in (("pk", "k"), ("pv", "v"), ("pq", "q"), ("pa", "a"), ("pg", "g")):
                        o, s = fill((key, i))
                        pe.matmul(o, w_l1[w][:, :], ck(xrF, i), start=True, stop=True).then_inc(s, 1)
                if i >= 1:
                    c = i - 1
                    pe.wait_ge(y1_ready, c + 1)
                    o, s = fill(("wo1", c))
                    for j in range(TC):
                        mm = pe.matmul(tl(o, j), tl(yF, c * TC + j), w_l1["o"][:, :], start=True, stop=True)
                    mm.then_inc(s, 1)
            for c in range(NC):
                pe.wait_ge(x3T_ready, TC * (c + 1))
                transposes(("x3T", c), ck(x3T, c))
            logits(("routeF",), x3F, x3F_ready, w_r)
            pe.wait_ge(logitF_ready, 2)
            transposes(("route",), logitF)
            pe.wait_ge(onehot_ready, 1)
            o, s = fill(("cum",))
            oh = onehot[:, :, :].rearrange("p e t -> p (e t)")
            pe.matmul(tl(o, 0), triu[:, :], oh, start=True, stop=True)
            pe.matmul(tl(o, 1), onesb[:, :], oh, start=True, stop=True).then_inc(s, 1)
            pe.wait_ge(ld_e, 64)
            for i in range(E1 + 1):
                for n in turned_before(i):
                    pe.wait_ge(ein_loaded[n], 16)
                    transposes(("einT", n), einT[n // 4][:, (n % 4) * CH:(n % 4 + 1) * CH])
                if i < E1:
                    e = i
                    pe.wait_ge(einF_ready, -(-(e + 1) * CAP // CH))
                    for m in range(FM):
                        o, s = fill(("h1", e, m))
                        for (n, lo, hi) in pieces(e):
                            mm = pe.matmul(o[:, lo - e * CAP:hi - e * CAP], w1[e // 4][:, (e % 4) * DFF + m * P:(e % 4) * DFF + (m + 1) * P],
                                           einF[n][:, lo - n * S:hi - n * S], start=True, stop=True)
                        mm.then_inc(s, 1)
                if i >= 1:
                    e = i - 1
                    pe.wait_ge(relu_act, 2 * (e + 1))
                    pe.wait_ge(relu_dve, 2 * (e + 1))
                    o, s = fill(("eo", e))
                    for j in range(3):
                        n = P if j < 2 else 64
                        for k in range(FM):
                            w = w2[e // 4][:, ((e % 4) * FM + k) * D:((e % 4) * FM + k + 1) * D]
                            mm = pe.matmul(o[0:n, j * P:(j + 1) * P], hE[e % 2][:, k * CAP + j * P:k * CAP + j * P + n], w,
                                           start=(k == 0), stop=(k == FM - 1))
                    mm.then_inc(s, 1)

        @block.scalar
        def _(act):
            for i in range(1, NC + 2):
                if i <= NC:
                    c = i - 1
                    if c == 0:
                        act.wait_ge(ld_a, 32)
                        act.wait_ge(ld_a1, 32)
                    for m in range(2):
                        o = full(act, ("xr", c, m))
                        act.activation(ck(xin[m], c), o, ACT.Silu, bias=b_in[:, m:m + 1]).then_inc(silu_ready, 1)
                if i >= 2:
                    c = i - 2
                    o = full(act, ("dt", c))
                    act.activation(ck(sp_abs, c), o, ACT.Identity, bias=b_dt[:, :]).then_inc(u_ready, 1)
            act.wait_ge(ld_a2, 16 * 7)
            act.activation(a_exp[NSTATE:P, :], a_log[NSTATE:P, :], ACT.Exp).then_inc(aexp_ready, 1)
            for c in range(NC):
                act.wait_ge(absu_ready, c + 1)
                act.activation(ck(sp_abs, c), ck(sp_abs, c), ACT.Exp, scale=-1.0).then_inc(expu_ready, 1)
            for c in range(NC):
                act.wait_ge(expu_ready, c + 1)
                act.activation(ck(sp_abs, c), ck(sp_abs, c), ACT.Ln, bias=1.0).then_inc(sp_ready, 1)
            for c in range(NC):
                o = full(act, ("mean", c))
                act.wait_ge(aneg_ready, 1)
                act.activation(ck(aF, c)[0:NSTATE, :], o[NSTATE:P, :], ACT.Exp, scale=a_neg[NSTATE:P, :]).then_inc(decay_ready, 1)
            for c in range(NC):
                for m in (2, 3):
                    o = full(act, ("xr", c, m))
                    act.activation(ck(gated[m - 2], c), o, ACT.Silu, bias=b_in[:, m:m + 1]).then_inc(res_ready, 1)
            o = full(act, ("wT",))
            act.activation(wcT[:, :, :].rearrange("p k n -> p (k n)"), o[0:32, 0:2 * P], ACT.Copy).then_inc(wcT_ready, 1)
            o = full(act, ("wkv",))
            act.activation(wkv[:, :, :].rearrange("p k n -> p (k n)"), o[:, 0:2 * D], ACT.Copy).then_inc(wkv_ready, 1)

            for c in range(NC + 1):
                for i in ((0, 1) if c == 0 else (c + 1,)):
                    if i < NC:
                        o = full(act, ("x1T", i))
                        act.activation(ck(x1F, i), o, ACT.Copy).then_inc(x1F_ready, 1)
                if c >= 1:
                    for n in range(2):
                        i = 2 * (c - 1) + n
                        act.wait_ge(sum_ready, i + 1)
                        act.activation(parts(i)[:, 0, :], ck(rope_a(n), c - 1), ACT.Copy).then_inc(part_ready, 1)
                    for n in range(2):
                        i = 2 * (c - 1) + n
                        if i < 2 * NC - 1:
                            act.wait_ge(rest_ready, i + 1)
                        else:
                            act.wait_ge(rest_dve, 1)
                        act.activation(parts(i)[:, 1, :], ck(rope_b(n), c - 1), ACT.Copy).then_inc(part_ready, 1)
                if c < NC:
                    o = full(act, ("v", c))
                    act.activation(ck(vT, c), o, ACT.Copy).then_inc(vT_ready, 1)

            act.wait_ge(pre_step, 3)
            for u in range(len(units)):
                act.wait_ge(mx_full, u + 1)
                if u >= PAIRS:
                    act.wait_ge(scan_done, u - PAIRS + 1)
                act.activation(ck(copied, u % PAIRS), bank_ap[pair[u % PAIRS][1]], ACT.Copy).then_inc(half_copied, 1)

            def head(hv, h, lap=0):
                for g in range(NT):
                    if h * NT + g >= PR:
                        act.wait_ge(pv_done, hv * NT + (g - PR + 1))
                    for c in range(NC):
                        u = g * NC + c
                        act.wait_ge(st_full, hv * 64 + u + 1)
                        act.activation(prob[g % PR][:, c * CH:(c + 1) * CH], bank[u % STB][:, :], ACT.Exp,
                                       scale=1.0 / math.sqrt(DH)).then_inc(exp_done, 1)
                        if h >= 1 and g == 1 and c == 0:
                            take_out(hv - 1, h - 1, lap)

            def take_out(hv, h, lap=0):
                act.wait_ge(pv_done, (hv + 1) * NT)
                if h >= 2:
                    act.wait_ge(pv_stored[h % 2], (h // 2 + 2 * lap) * 16)
                act.activation(pv_sb[:, 0, h % 2, :], pvps[:, :], ACT.Copy).then_inc(pv_out, 1)

            for h in range(4):
                head(h, h)
            with act.Fori(1, LOOPED // 4) as it:
                for j in range(4):
                    head(it * 4 + j, 4 + j, it - 1)
            for h in range(LOOPED, H):
                head(h, h)
            take_out(H - 1, H - 1)

            o = full(act, ("xnT", 0))
            act.activation(ck(xnF, 0), o, ACT.Copy).then_inc(xnF_ready, 1)
            for c in range(NC):
                for w in range(2):
                    for k in range(2):
                        o = full(act, ("ffn", c, 4 * w + k))
                        if c >= 1:
                            act.wait_ge(hid_ready, 4 * (c - 1) + 2 * w + k + 1)
                        act.activation(act_ff[:, (2 * w + k) * CH:(2 * w + k + 1) * CH], o, ACT.Silu).then_inc(silu0_ready, 1)
                    if w == 0 and c + 1 < NC:
                        o = full(act, ("xnT", c + 1))
                        act.activation(ck(xnF, c + 1), o, ACT.Copy).then_inc(xnF_ready, 1)
                if c == NC - 2:
                    o = full(act, ("gateF",))
                    act.activation(logitF[:, :], o, ACT.Copy).then_inc(logitF_ready, 1)
            act.wait_ge(gexp_in, 1)
            act.activation(g_s[:, 2, :], g_s[:, 1, :], ACT.Exp).then_inc(gexp_ready, 1)
            act.activation(g4[:, 3, :, :], g4[:, 2, :, :], ACT.Exp).then_inc(gexp_ready, 1)
            act.wait_ge(ld_d, 112)
            for c in range(NC):
                o = full(act, ("xrT", c))
                act.activation(ck(xrF, c), o, ACT.Copy, scale=gamma[:, :]).then_inc(xrF_ready, 1)
                gates = (("pa", decF, ACT.Sigmoid), ("pg", gsF, ACT.Silu))
                for key, dst, f in (("pk", kF, ACT.Copy), ("pq", qF, ACT.Copy)) + (gates if c % 2 == 0 else gates[::-1]):
                    o = full(act, (key, c))
                    act.activation(ck(dst, c), o, f).then_inc(l1_act, 1)
            for c in range(NC):
                o = full(act, ("x3T", c))
                act.activation(ck(x3F, c), o, ACT.Copy).then_inc(x3F_ready, 1)
            o = full(act, ("routeF",))
            act.wait_ge(gate_ready, 1)
            act.activation(logitF[:, :], o, ACT.Copy).then_inc(logitF_ready, 1)
            act.wait_ge(rexp_in, 1)
            act.activation(r8[:, 2, :, :], r8[:, 1, :, :], ACT.Exp).then_inc(rexp_ready, 1)
            for e in range(E1):
                for n in turned_before(e):
                    o = full(act, ("einT", n))
                    act.activation(ck(einF[n // 4], n % 4), o, ACT.Copy).then_inc(einF_ready, 1)
                for m in (0, 2):
                    o = full(act, ("h1", e, m))
                    if e >= 2 and m == 0:
                        full(act, ("eo", e - 2))
                    act.activation(hE[e % 2][:, m * CAP:(m + 1) * CAP], o[:, 0:CAP], ACT.Relu).then_inc(relu_act, 1)
                if e >= 1:
                    take_expert(act, e - 1)
            take_expert(act, E1 - 1)

        @block.vector
        def _(v):
            steps = [0]

            def link(ins, meanwhile=None):
                steps[0] += 1
                n = steps[0]
                ins.then_inc(dve_step, 1)
                if meanwhile:
                    meanwhile()
                v.wait_ge(dve_step, n)

            def stats(k, src, c, meanwhile=()):
                n = norms.index((k, c))
                if k == N_RMS1:
                    n2 = norms.index((N_LN2, c))
                    link(v.tensor_tensor(msq[:, n, :], rs[:, n2, :], rs[:, n2, :], ALU.mult))
                    link(v.tensor_tensor(msq[:, n, :], msq[:, n, :], mv[:, n2, :, 1], ALU.mult))
                    link(v.tensor_scalar(var[:, n, :], msq[:, n, :], RMS1_EPS / D, None, ALU.add))
                    return guess_root(k, c, meanwhile)
                for j in range(TC):
                    ins = v.bn_stats(bn[:, n % 2, j, :], tl(src, c * TC + j))
                    if j < TC - 1:
                        ins.then_inc(dve_step, 1)
                        steps[0] += 1
                link(ins)
                for j in range(TC):
                    ins = v.bn_aggr(mv[:, n, j, :], bn[:, n % 2, j, :])
                    if j < TC - 1:
                        ins.then_inc(dve_step, 1)
                        steps[0] += 1
                link(ins)
                mean, vr = mv[:, n, :, 0], mv[:, n, :, 1]
                if k in (N_RMSX, N_RMSO):
                    link(v.tensor_tensor(msq[:, n, :], mean, mean, ALU.mult))
                    link(v.scalar_tensor_tensor(out=var[:, n, :], in0=msq[:, n, :], scalar=RMS0_EPS, in1=vr, op0=ALU.add, op1=ALU.add))
                else:
                    link(v.tensor_scalar(var[:, n, :], vr, LN_EPS, None, ALU.add))
                guess_root(k, c, meanwhile)

            def guess_root(k, c, meanwhile=()):
                n = norms.index((k, c))
                y, x, w = rs[:, n, :], var[:, n, :], nw[:, 1, :]
                guess = v.tensor_scalar(y.bitcast(I32), x.bitcast(I32), -0.5, RSQRT_MAGIC, ALU.mult, ALU.add)
                if (k, c) in pool_norms:
                    guess.then_inc(guess_ready, 1)
                    return
                link(guess)
                for i in range(3):
                    other = meanwhile[2 * i:2 * i + 2] + (None, None)
                    link(v.tensor_tensor(w, y, y, ALU.mult), other[0])
                    link(v.scalar_tensor_tensor(out=w, in0=w, scalar=-0.5, in1=x, op0=ALU.mult, op1=ALU.mult), other[1])
                    link(v.scalar_tensor_tensor(out=y, in0=w, scalar=1.5, in1=y, op0=ALU.add, op1=ALU.mult))

            def root(k, c):
                n = norms.index((k, c))
                if (k, c) in pool_norms:
                    v.wait_ge(rstd_ready, pool_norms.index((k, c)) + 1)
                return mv[:, n, :, 0], rs[:, n, :]

            def normalize_tile(k, dst, src, done, t):
                c, j = t // TC, t % TC
                n = norms.index((k, c))
                mean, r = root(k, c) if j == 0 else (mv[:, n, :, 0], rs[:, n, :])
                v.tensor_scalar(tl(dst, t), tl(src, t), mean[:, j:j + 1], r[:, j:j + 1],
                                ALU.subtract, ALU.mult).then_inc(done, 1)

            def normalize(k, c, dst, src, done):
                for j in range(TC):
                    normalize_tile(k, dst, src, done, c * TC + j)

            def tiles(step, c, *which):
                return tuple(partial(step, *which, c * TC + j) for j in range(TC))

            v.memset(ones[:, :], 1.0).then_inc(const_dve, 1)
            v.memset(mean_w[:, :], 1.0 / D).then_inc(const_dve, 1)
            v.memset(onesb[:, :], 1.0).then_inc(const_dve, 1)
            v.memset(zeros[:, :], 0.0).then_inc(zeroed, 1)
            v.memset(keep_scan[:, :], 1.0).then_inc(const_dve, 1)
            v.wait_ge(const_dve, 4)
            v.memset(keep_scan[:, :].rearrange("p (e t) -> p e t", t=NT)[:, :, 0:1], 0.0).then_inc(const_dve, 1)

            for i in range(NC + 2):
                if i < NC:
                    o = full(v, ("xT", i))
                    v.tensor_copy(ck(x0F, i), o).then_inc(x0F_ready, 1)
                if i >= 2:
                    c = i - 2
                    v.wait_ge(u_ready, c + 1)
                    v.tensor_scalar(ck(sp_relu, c), ck(sp_abs, c), 0.0, None, ALU.max).then_inc(relu_ready, 1)
                    v.wait_ge(relu_ready, c + 1)
                    v.scalar_tensor_tensor(out=ck(sp_abs, c), in0=ck(sp_abs, c), scalar=-1.0, in1=ck(sp_abs, c),
                                           op0=ALU.mult, op1=ALU.max).then_inc(absu_ready, 1)
            v.wait_ge(aexp_ready, 1)
            v.tensor_scalar(a_neg[NSTATE:P, :], a_exp[NSTATE:P, :], -1.0, None, ALU.mult).then_inc(aneg_ready, 1)
            for c in range(NC):
                v.wait_ge(sp_ready, c + 1)
                v.tensor_tensor(ck(sp_relu, c), ck(sp_relu, c), ck(sp_abs, c), ALU.add).then_inc(delta_ready, 1)
            for i in range(NC):
                o = full(v, ("bx", i))
                v.wait_ge(ld_a2, 16 * 7)
                v.tensor_scalar(ck(bxF, i)[0:NSTATE, :], o[0:NSTATE, :], b_xp[:, :], None, ALU.add).then_inc(bx_ready, 1)
                v.wait_ge(decay_ready, i + 1)
                v.wait_ge(bx_ready, i + 1)
                if i >= 1:
                    v.wait_ge(state_ready, i)
                before = 0.0 if i == 0 else stF[0:NSTATE, i * CH - 1:i * CH]
                v.tensor_tensor_scan(ck(stF, i)[0:NSTATE, :], ck(aF, i)[0:NSTATE, :], ck(bxF, i)[0:NSTATE, :],
                                     before, ALU.mult, ALU.add).then_inc(state_ready, 1)
            for c in range(NC):
                v.wait_ge(res_ready, 2 * c + 2)
                v.tensor_tensor(ck(gated[1], c), ck(gated[1], c), ck(xin[1], c), ALU.mult).then_inc(gated_dve, 1)

            def gate_sum(c):
                o = full(v, ("ssum", c))
                v.wait_ge(gated_ready, c + 1)
                v.wait_ge(gated_dve, c + 1)
                for k in range(2):
                    v.tensor_tensor(ck(gated[k], c), o, ck(gated[k], c), ALU.mult).then_inc(y_ready, 1)

            def add_x(c, meanwhile=()):
                o = full(v, ("outA", c))
                v.wait_ge(pre_step, 3)
                v.tensor_tensor(ck(x1T, c), o, ck(pre, c), ALU.add).then_inc(resid_ready, 1)
                v.wait_ge(resid_ready, c + 1)
                stats(N_LN1, x1T, c, meanwhile)

            def norm_x1(c):
                normalize(N_LN1, c, x1T, x1T, x1T_ready)

            gate_sum(0)
            gate_sum(1)
            add_x(0)
            gate_sum(2)
            add_x(1)
            gate_sum(3)
            norm_x1(0)
            add_x(2)
            norm_x1(1)
            add_x(3, tiles(normalize_tile, 2, N_LN1, x1T, x1T, x1T_ready))
            norm_x1(3)

            for c in range(NC + 1):
                for n, (key, keyr) in enumerate((("q", "qr"), ("k", "kr")) if c < NC else ()):
                    i = 2 * c + n
                    o = full(v, (key, c))
                    v.wait_ge(ld_b, 112)
                    v.tensor_tensor(ck(rope_a(n), c), o, ck(cosF, c), ALU.mult).then_inc(rope_ready, 1)
                    o = full(v, (keyr, c))
                    v.tensor_tensor(ck(rope_b(n), c), o, ck(sinF, c), ALU.mult).then_inc(rope_ready, 1)
                    v.wait_ge(rope_ready, 2 * i + 2)
                    v.tensor_tensor(ck(rope_a(n), c), ck(rope_a(n), c), ck(rope_b(n), c), ALU.add).then_inc(sum_ready, 1)
                if c >= 1:
                    i = 2 * (c - 1) + 1
                    if c == NC:
                        v.wait_ge(part_ready, 2 * i)
                        v.tensor_tensor(ck(rope_b(1), c - 1), ck(rope_a(1), c - 1), parts(i)[:, 0, :], ALU.subtract).then_inc(rest_dve, 1)
                        v.wait_ge(rest_ready, i)
                        v.wait_ge(part_ready, 2 * i + 1)
                        v.wait_ge(third_q, NC - 1)
                        v.tensor_tensor(parts(i - 1)[:, 2, :], ck(rope_b(0), c - 1), parts(i - 1)[:, 1, :], ALU.subtract).then_inc(third_q, 1)
                        v.wait_ge(rest_dve, 1)
                    else:
                        v.wait_ge(rest_ready, i + 1)
                    v.wait_ge(part_ready, 2 * i + 2)
                    v.tensor_tensor(parts(i)[:, 2, :], ck(rope_b(1), c - 1), parts(i)[:, 1, :], ALU.subtract).then_inc(third_k, 1)

            def reduce_half(hv, h, t, f):
                v.wait_ge(mx_full, hv * 32 + (2 * t + f + 1))
                v.tensor_reduce(maxes[:, h % 2, t, f:f + 1], maxps[f][:, :], AX.X, ALU.max).then_inc(mx_free, 1)

            def combine(hv, h):
                v.wait_ge(mx_free, hv * 32 + 32)
                if h >= 1:
                    v.wait_ge(mparts_ready, hv)
                v.tensor_tensor(mneg[:, :], maxes[:, h % 2, :, 0], maxes[:, h % 2, :, 1], ALU.max).then_inc(mcomb, 1)
                v.wait_ge(mcomb, hv * 2 + 1)
                v.tensor_scalar(mparts[:, 0:NT], mneg[:, :], -1.0, None, ALU.mult).then_inc(mcomb, 1)
                v.wait_ge(mcomb, hv * 2 + 2)
                v.scalar_tensor_tensor(out=mparts[:, NT:2 * NT], in0=mneg[:, :], scalar=-1.0, in1=mparts[:, 0:NT],
                                       op0=ALU.mult, op1=ALU.subtract).then_inc(mparts_ready, 1)

            def invert(hv, h, i):
                if i == 0:
                    v.wait_ge(pv_out, hv + 1)
                q = slice(i * CH // RP, (i + 1) * CH // RP)
                v.reciprocal(pv_sb[:, 1, h % 2, q], pv_sb[:, 0, h % 2, q]).then_inc(rcp_ready, 1)

            def turn(hv, h, ps=maxps[1]):
                v.wait_ge(mt_full, hv + 1)
                if h >= 1:
                    v.wait_ge(mrows_placed, hv * 32)
                v.tensor_copy(mrows[:, :], ps[0:2 * NT, 0:P // 2].bitcast(BF16)).then_inc(mrows_ready, 1)

            def head(hv, h, lap=0):
                for g in range(NT):
                    t, k = (g + AHEAD, 1) if g + AHEAD < NT else (g + AHEAD - NT, 2)
                    more = h + k < H
                    if more:
                        reduce_half(hv + k, h + k, t, 0)
                    if g == NT + 1 - AHEAD and h + 1 < H:
                        turn(hv + 1, h + 1)
                    if more:
                        reduce_half(hv + k, h + k, t, 1)
                    if t == NT - 1 and h + 1 < H:
                        combine(hv + 1, h + 1)
                    if h >= 1 and 3 <= g < 3 + RP:
                        invert(hv - 1, h - 1, g - 3)

            def keep_maxima(u, n):
                h, t, _ = units[u]
                v.wait_ge(scan_done, u + n)
                ends = slot[10 + u // PAIRS % 2][:, :].rearrange("p (t f q) -> p t f q", f=2, q=CH)[:, 0:n // 2, :, CH - 1]
                v.tensor_copy(maxes[:, h, t:t + n // 2, :], ends).then_inc(mx_free, n)

            for u, (h, t, f) in enumerate(units):
                v.wait_ge(half_copied, u + 1)
                if u == 0:
                    v.wait_ge(third_q, NC)
                    v.wait_ge(third_k, NC)
                if u >= 2 * PAIRS:
                    v.wait_ge(mx_free, (u // PAIRS - 1) * PAIRS)
                v.tensor_tensor_scan(running[u % (2 * PAIRS)], bank_ap[pair[u % PAIRS][0]], ck(copied, u % PAIRS),
                                     -BIG, ALU.max, ALU.max).then_inc(scan_done, 1)
                if u % PAIRS == 0 and u >= PAIRS and u != 2 * NT:
                    keep_maxima(u - PAIRS, PAIRS)
                if u == 2 * NT - 1:
                    keep_maxima(u + 1 - PAIRS, PAIRS)
                    combine(0, 0)
                if u == 2 * NT + 2:
                    turn(0, 0, pvps)
            keep_maxima(2 * NT + PAIRS, 2 * AHEAD - PAIRS)
            for h in range(4):
                head(h, h)
            with v.Fori(1, LOOPED // 4) as it:
                for j in range(4):
                    head(it * 4 + j, 4 + j, it - 1)
            for h in range(LOOPED, H):
                head(h, h)

            v.wait_ge(attn_loaded, 16 * 2 * NC)
            early = 96
            v.tensor_tensor(numF[0:early, :], numF[0:early, :], rdenF[0:early, :], ALU.mult).then_inc(attn_ready, 1)
            v.wait_ge(pv_out, H)
            v.reciprocal(pv_sb[:, 1, (H - 1) % 2, :], pv_sb[:, 0, (H - 1) % 2, :]).then_inc(rcp_ready, RP)
            for c in range(NC):
                v.wait_ge(last_head_loaded[c], 32)
                v.tensor_tensor(ck(numF, c)[early:, :], ck(numF, c)[early:, :], ck(rdenF, c)[early:, :], ALU.mult).then_inc(attn_ready, 1)
            v.wait_ge(ld_c, 192)

            def add_x1(c, meanwhile=()):
                o = full(v, ("wo", c))
                v.tensor_tensor(ck(xnT, c), o, ck(x1T, c), ALU.add).then_inc(resid_ready, 1)
                v.wait_ge(resid_ready, NC + c + 1)
                stats(N_RMSX, xnT, c, meanwhile)

            def norm_x_tile(t):
                c, j = t // TC, t % TC
                r, x = rs[:, norms.index((N_RMSX, c)), :], tl(xnT, t)
                if j == 0:
                    root(N_RMSX, c)
                v.scalar_tensor_tensor(out=x, in0=x, scalar=r[:, j:j + 1], in1=bc["n1"][:, :],
                                       op0=ALU.mult, op1=ALU.mult).then_inc(xnT_ready, 1)

            def norm_x(c):
                for j in range(TC):
                    norm_x_tile(c * TC + j)

            add_x1(0)
            norm_x(0)
            add_x1(1)
            add_x1(2)
            norm_x(1)
            add_x1(3, tiles(norm_x_tile, 2))
            norm_x(3)

            def turned(o, n):
                return o.rearrange("p (j c n) -> p c j n", j=TC, c=NC)[:, :, :, 0:n]

            def wide(x, n=EPG):
                return x.unsqueeze(2).broadcast_to([P, NT, n])

            def first_best(score, rank, rev, n, top, hit, oh):
                link(v.tensor_reduce(top, score, AX.X, ALU.max))
                link(v.tensor_tensor(hit, score, wide(top, n), ALU.is_equal))
                link(v.tensor_tensor(hit, hit, rev[:, :].unsqueeze(1).broadcast_to([P, NT, n]), ALU.mult))
                link(v.tensor_reduce(rank, hit, AX.X, ALU.max))
                link(v.tensor_tensor(oh, hit, wide(rank, n), ALU.is_equal))

            def hidden(c, between=()):
                for w in range(2):
                    for k in range(2):
                        i = 2 * w + k
                        o = full(v, ("ffn", c, 4 * w + 2 + k))
                        v.wait_ge(silu0_ready, 4 * c + i + 1)
                        v.tensor_tensor(ck(hid[w][k], c), o, act_ff[:, i * CH:(i + 1) * CH], ALU.mult).then_inc(hid_ready, 1)
                        if between and between[i]:
                            between[i]()

            hidden(0)
            hidden(1)
            g0, g1 = gl[:, :, 0], gl[:, :, 1]
            second, diff, ediff, first_, top, summ, rank, top2, rank2 = (g_s[:, i, :] for i in range(9))
            e4, tmp4, z4, x4, hit4, oh4, e4b, hit4b, oh4b = (g4[:, i, :, :] for i in range(9))

            def choose_group():
                o = full(v, ("gate",))
                v.tensor_copy(gl[:, :, :].rearrange("p (c j) n -> p c j n", j=TC), turned(o, 2 + E0)).then_inc(gate_ready, 1)
                v.wait_ge(gate_ready, 1)
                link(v.tensor_tensor(gl[:, :, :], gl[:, :, :], b_gate[:, :].unsqueeze(1).broadcast_to([P, NT, 2 + E0]), ALU.add))
                link(v.tensor_tensor(second, g1, g0, ALU.is_gt))
                link(v.tensor_scalar(first_, second, -1.0, 1.0, ALU.mult, ALU.add))
                link(v.tensor_tensor(diff, g1, g0, ALU.subtract))
                link(v.tensor_scalar(summ, diff, -1.0, None, ALU.mult))
                link(v.tensor_tensor(diff, diff, summ, ALU.min))

            def choose_first():
                link(v.tensor_tensor(e4, gl[:, :, 2:6], wide(first_), ALU.mult))
                link(v.tensor_tensor(tmp4, gl[:, :, 6:10], wide(second), ALU.mult))
                link(v.tensor_tensor(e4, e4, tmp4, ALU.add))
                first_best(e4, rank, rev4, EPG, top, hit4, oh4)

            def choose_second():
                v.tensor_tensor(z4, e4, wide(top), ALU.subtract).then_inc(gexp_in, 1)
                link(v.scalar_tensor_tensor(out=e4b, in0=oh4, scalar=-BIG, in1=e4, op0=ALU.mult, op1=ALU.add))
                first_best(e4b, rank2, rev4, EPG, top2, hit4b, oh4b)

            def both():
                link(v.tensor_tensor(oh4, oh4, oh4b, ALU.add))

            hidden(2)
            hidden(3, (None, choose_group, choose_first, choose_second))
            both()
            v.wait_ge(gexp_ready, 2)
            link(v.tensor_reduce(summ, x4, AX.X, ALU.add))
            link(v.scalar_tensor_tensor(out=summ, in0=ediff, scalar=1.0, in1=summ, op0=ALU.add, op1=ALU.mult))
            link(v.reciprocal(summ, summ))
            link(v.tensor_tensor(x4, x4, oh4, ALU.mult))
            link(v.tensor_tensor(x4, x4, wide(summ), ALU.mult))
            link(v.tensor_tensor(wtop[:, :, 0:EPG], x4, wide(first_), ALU.mult))
            link(v.tensor_tensor(wtop[:, :, EPG:], x4, wide(second), ALU.mult))

            def sum_experts(i, meanwhile=()):
                o = full(v, ("sh", i))
                v.tensor_tensor(ck(oT, i), o, ck(xnT, i), ALU.add).then_inc(acc_ready, 1)
                n = ACC * i + 1
                v.wait_ge(acc_ready, n)
                for t in range(i * TC, (i + 1) * TC, 2):
                    for e in range(E0):
                        for j in range(2):
                            o = full(v, ("rt", t + j, e // 4))
                            v.wait_ge(acc_ready, n - 1)
                            v.scalar_tensor_tensor(out=tl(oT, t + j), in0=tl(o, e % 4), scalar=wtop[:, t + j, e:e + 1],
                                                   in1=tl(oT, t + j), op0=ALU.mult, op1=ALU.add).then_inc(acc_ready, 1)
                            n += 1
                    if t % TC == 0 and i >= 2:
                        norm_x2(i - 2)
                v.wait_ge(acc_ready, n)
                stats(N_RMSO, oT, i, meanwhile)

            def add_input(c, meanwhile=()):
                _, r = root(N_RMSO, c)
                for j in range(TC):
                    x = tl(oT, c * TC + j)
                    steps[0] += 1
                    v.scalar_tensor_tensor(out=x, in0=x, scalar=r[:, j:j + 1], in1=bc["n2"][:, :],
                                           op0=ALU.mult, op1=ALU.mult).then_inc(dve_step, 1)
                v.wait_ge(dve_step, steps[0])
                link(v.tensor_tensor(ck(oT, c), ck(oT, c), ck(x1T, c), ALU.add))
                stats(N_LN2, oT, c, meanwhile)

            x2_norm = (N_LN2, x2T, oT, x2T_ready)
            x3_norm = (N_LN3, x3T, x3T, x3T_ready)

            def mean_square_x2(c, meanwhile=()):
                v.wait_ge(x2T_ready, TC * (c + 1))
                stats(N_RMS1, x2T, c, meanwhile)

            def norm_x2(c, meanwhile=()):
                normalize(N_LN2, c, x2T, oT, x2T_ready)
                mean_square_x2(c, meanwhile)

            def scale_tile(t):
                c, j = t // TC, t % TC
                r = rs[:, norms.index((N_RMS1, c)), :]
                if j == 0:
                    root(N_RMS1, c)
                v.tensor_scalar(tl(xrT, t), tl(x2T, t), r[:, j:j + 1], None, ALU.mult).then_inc(xrT_ready, 1)

            def scale_x2(c):
                for j in range(TC):
                    scale_tile(c * TC + j)

            def gated_scan(c):
                o = full(v, ("pv", c))
                v.wait_ge(l1_act, 4 * c + 1)
                v.tensor_tensor(ck(kvF, c), o, ck(kF, c), ALU.mult).then_inc(kv_ready, 1)
                v.wait_ge(kv_ready, c + 1)
                v.wait_ge(l1_act, 4 * c + 4)
                before = 0.0 if c == 0 else hsF[:, c * CH - 1:c * CH]
                v.tensor_tensor_scan(ck(hsF, c), ck(decF, c), ck(kvF, c), before, ALU.mult, ALU.add).then_inc(hs_ready, 1)
                v.wait_ge(hs_ready, c + 1)
                link(v.tensor_tensor(ck(yF, c), ck(hsF, c), ck(qF, c), ALU.mult))
                v.tensor_tensor(ck(yF, c), ck(yF, c), ck(gsF, c), ALU.mult).then_inc(y1_ready, 1)

            def add_x2(c, meanwhile=()):
                o = full(v, ("wo1", c))
                v.tensor_tensor(ck(x3T, c), o, ck(x2T, c), ALU.add).then_inc(resid_ready, 1)
                v.wait_ge(resid_ready, 2 * NC + c + 1)
                stats(N_LN3, x3T, c, meanwhile)

            def norm_x3(c):
                normalize(N_LN3, c, x3T, x3T, x3T_ready)

            for i in range(NC - 1):
                sum_experts(i)
                if i >= 1:
                    add_input(i - 1)
            scale_x2(0)
            sum_experts(3, tiles(scale_tile, 1))
            add_input(2)
            add_input(3, tiles(normalize_tile, 2, *x2_norm))
            mean_square_x2(2)
            gated_scan(0)
            norm_x2(3, tiles(scale_tile, 2))
            scale_x2(3)
            gated_scan(1)
            add_x2(0)
            gated_scan(2)
            add_x2(1)
            norm_x3(0)
            gated_scan(3)
            add_x2(2)
            norm_x3(1)
            add_x2(3, tiles(normalize_tile, 2, *x3_norm))
            norm_x3(3)

            z8, x8, hit8, oh8 = (r8[:, i, :, :] for i in range(1, 5))
            top, rank, ssum, pmax, place, base, kept, at, factor, tmp = (r_s[:, i, :] for i in range(10))
            lg = r8[:, 5, :, :]
            o = full(v, ("route",))
            v.tensor_copy(lg.rearrange("p (c j) e -> p c j e", j=TC), turned(o, E1)).then_inc(gate_ready, 1)
            v.wait_ge(gate_ready, 2)
            v.wait_ge(const_pool, 7)
            first_best(lg, rank, rev8, E1, top, hit8, oh8)
            oh_et = oh8.rearrange("p t e -> p e t")
            v.tensor_copy(onehot[:, :, :], oh_et).then_inc(onehot_ready, 1)
            v.tensor_tensor(z8, lg, wide(top, E1), ALU.subtract).then_inc(rexp_in, 1)
            link(v.tensor_tensor(hit8, oh8, base8[:, :].unsqueeze(1).broadcast_to([P, NT, E1]), ALU.mult))
            link(v.tensor_reduce(base, hit8, AX.X, ALU.add))
            link(v.scalar_tensor_tensor(out=base, in0=base, scalar=-1.0, in1=spare[:, :], op0=ALU.add, op1=ALU.subtract))
            tot, inc, cum, sel = (et[:, i, :, :] for i in range(4))
            fl = lambda x: x.rearrange("p e t -> p (e t)")
            o = full(v, ("cum",))
            link(v.tensor_copy(fl(tot), tl(o, 1)))
            link(v.tensor_tensor_scan(fl(inc), keep_scan[:, :], fl(tot), 0.0, ALU.mult, ALU.add))
            link(v.tensor_tensor(inc, inc, tot, ALU.subtract))
            v.tensor_tensor(fl(cum), tl(o, 0), fl(inc), ALU.add).then_inc(comb_ready, 1)
            v.wait_ge(comb_ready, 1)
            link(v.tensor_tensor(sel, cum, oh_et, ALU.mult))
            link(v.tensor_reduce(place, sel.rearrange("p e t -> p t e"), AX.X, ALU.add))
            link(v.tensor_tensor(at, place, base, ALU.add))
            link(v.scalar_tensor_tensor(out=at, in0=place, scalar=float(CAP) + 0.5, in1=at, op0=ALU.is_lt, op1=ALU.mult))
            v.tensor_tensor(dest[:, :], at, spare[:, :], ALU.add).then_inc(dest_ready, 1)
            v.wait_ge(rexp_ready, 1)
            link(v.tensor_reduce(ssum, x8, AX.X, ALU.add))
            link(v.reciprocal(pmax, ssum))
            link(v.tensor_scalar(kept, place, float(CAP) + 0.5, None, ALU.is_lt))
            link(v.scalar_tensor_tensor(out=tmp, in0=pmax, scalar=-1.0, in1=kept, op0=ALU.add, op1=ALU.mult))
            link(v.tensor_scalar(factor, tmp, 1.0, None, ALU.add))
            for e in range(E1):
                for m in (1, 3):
                    o = full(v, ("h1", e, m))
                    if e >= 2 and m == 1:
                        full(v, ("eo", e - 2))
                    v.tensor_scalar(hE[e % 2][:, m * CAP:(m + 1) * CAP], o[:, 0:CAP], 0.0, None, ALU.max).then_inc(relu_dve, 1)
            def weigh(t):
                if t % TC == 0:
                    v.wait_ge(gathered[t // TC], 16 * TC)
                steps[0] += 1
                v.scalar_tensor_tensor(out=tl(finT, t), in0=tl(combT, t), scalar=factor[:, t:t + 1], in1=tl(x3T, t),
                                       op0=ALU.mult, op1=ALU.add).then_inc(dve_step, 1)

            for j in range(TC):
                weigh(j)
            x4_norm = (N_LN4, yT, finT, out_ready)
            for c in range(NC):
                v.wait_ge(dve_step, steps[0])
                if c < NC - 2:
                    stats(N_LN4, finT, c, tiles(weigh, c + 1))
                    normalize(N_LN4, c, *x4_norm[1:])
                elif c == NC - 2:
                    stats(N_LN4, finT, c)
                    for j in range(TC):
                        weigh((c + 1) * TC + j)
                else:
                    stats(N_LN4, finT, c, tiles(normalize_tile, c - 1, *x4_norm))
                    normalize(N_LN4, c, *x4_norm[1:])

        @block.gpsimd
        def _(g):
            steps = [0]

            def link(ins):
                steps[0] += 1
                ins.then_inc(pool_step, 1)
                g.wait_ge(pool_step, steps[0])

            def refine(k, c):
                n, done = norms.index((k, c)), pool_norms.index((k, c)) + 1
                g.wait_ge(guess_ready, done)
                y, x, w = rs[:, n, :], var[:, n, :], nw[:, 0, :]
                for i in range(3):
                    link(g.tensor_tensor(w, y, y, ALU.mult))
                    link(g.tensor_tensor(w, w, x, ALU.mult))
                    link(g.tensor_scalar(w, w, -0.5, 1.5, ALU.mult, ALU.add))
                    ins = g.tensor_tensor(y, y, w, ALU.mult)
                    if i < 2:
                        link(ins)
                ins.then_inc(rstd_ready, 1)
                g.wait_ge(rstd_ready, done)

            link(g.memset(ident[:, :], 0.0))
            g.affine_select(out=ident[:, :], in_=ident[:, :], compare_op=ALU.not_equal, fill=1.0, base=0,
                            pattern=[[-1, P]], channel_multiplier=1).then_inc(const_pool, 1)
            g.wait_ge(const_pool, 1)
            g.tensor_copy(identb[:, :], ident[:, :]).then_inc(const_pool, 1)
            link(g.memset(triu[:, :], 1.0))
            g.affine_select(out=triu[:, :], in_=triu[:, :], compare_op=ALU.is_ge, fill=0.0, base=0,
                            pattern=[[1, P]], channel_multiplier=-1).then_inc(const_pool, 1)
            for t, n, lo, step in ((rev4, EPG, EPG, -1), (rev8, E1, E1, -1), (base8, E1, 0, CAP)):
                for e in range(n):
                    ins = g.memset(t[:, e:e + 1], float(lo + e * step))
                    if e < n - 1:
                        link(ins)
                ins.then_inc(const_pool, 1)
            link(g.iota(token_i[:, :], pattern=[[P, NT]], base=SLOTS, channel_multiplier=1))
            g.tensor_copy(spare[:, :], token_i[:, :]).then_inc(const_pool, 1)
            g.memset(vh[:, :, :, :], 1.0).then_inc(const_pool, 1)
            g.memset(w_r[:, E1:], 0.0).then_inc(const_pool, 1)
            g.memset(w_gate[:, 2 + E0:], 0.0).then_inc(const_pool, 1)

            def rows(x):
                return x[:, :].unsqueeze(1).broadcast_to([P, NT, D])

            for c in range(NC):
                g.wait_ge(ld_x[c], 16)
            g.wait_ge(ld_a2, 16 * 7)
            x3 = x0T[:, :].rearrange("p (t d) -> p t d", d=D)
            p3 = pre[:, :].rearrange("p (t d) -> p t d", d=D)
            g.tensor_tensor(p3, x3, rows(bc["d"]), ALU.mult).then_inc(pre_step, 1)
            g.wait_ge(pre_step, 1)
            g.tensor_tensor(p3, p3, rows(bc["bo"]), ALU.add).then_inc(pre_step, 1)
            g.wait_ge(pre_step, 2)
            g.tensor_tensor(pre[:, :], pre[:, :], x0T[:, :], ALU.add).then_inc(pre_step, 1)
            for c in range(NC):
                g.wait_ge(res_ready, 2 * c + 1)
                g.tensor_tensor(ck(gated[0], c), ck(gated[0], c), ck(xin[0], c), ALU.mult).then_inc(gated_ready, 1)

            def rotate(w, wr):
                src = w.rearrange("p (n two) -> p n two", two=2)
                dst = wr[:, :].rearrange("p (n two) -> p n two", two=2)
                g.tensor_scalar(dst[:, :, 0], src[:, :, 1], -1.0, None, ALU.mult).then_inc(rot_ready, 1)
                g.tensor_copy(dst[:, :, 1], src[:, :, 0]).then_inc(rot_ready, 1)

            g.wait_ge(ld_b, 112)
            rotate(wq[:, :], wqr)
            g.wait_ge(wkv_ready, 1)
            rotate(wkv[:, 0, :], wkr)
            for c in range(NC - 1):
                refine(N_LN1, c)

            g.wait_ge(x1T_ready, NT)
            for c in range(NC):
                for n in range(2) if c < NC - 1 else (0,):
                    i = 2 * c + n
                    g.wait_ge(part_ready, 4 * c + n + 1)
                    g.tensor_tensor(ck(rope_b(n), c), ck(rope_a(n), c), parts(i)[:, 0, :], ALU.subtract).then_inc(rest_ready, 1)
                if c >= 1:
                    i = 2 * (c - 1)
                    g.wait_ge(rest_ready, i + 1)
                    g.wait_ge(part_ready, 4 * (c - 1) + 3)
                    g.tensor_tensor(parts(i)[:, 2, :], ck(rope_b(0), c - 1), parts(i)[:, 1, :], ALU.subtract).then_inc(third_q, 1)
                for b in (2 * c, 2 * c + 1) if c < 2 else ():
                    if c == 0:
                        g.wait_ge(rest_ready, 2)
                    else:
                        g.wait_ge(third_q, 1)
                    g.memset(slot[4 + b // 2][64:96, (b % 2) * 1024:(b % 2) * 1024 + 1024], ONE_PAIR).then_inc(ones_ready, 1)
                    g.wait_ge(ones_ready, b + 1)

            g.wait_ge(vT_ready, NC)
            g.wait_ge(const_pool, 8)

            def head(hv, h, lap=0):
                if h >= 2:
                    g.wait_ge(pv_done, (hv - 1) * NT)
                g.tensor_copy(vh[:, h % 2, :, 0:DH],
                              vT[:, :].rearrange("p (t d) -> p t d", d=D)[:, :, bass.ds(hv * DH, DH)]).then_inc(vh_ready, 1)

            head(0, 0)
            head(1, 1)
            with g.Fori(1, H // 2) as it:
                for j in range(2):
                    head(it * 2 + j, 2 + j)

            for k, c in pool_norms[NC - 1:-1]:
                refine(k, c)

            g.wait_ge(zeroed, 17)
            g.wait_ge(x3T_ready, NT)
            g.wait_ge(dest_ready, 1)
            for t in range(NT):
                g.indirect_dma_start(out=disp[:, :], out_offset=bass.IndirectOffsetOnAxis(ap=dest[:, t:t + 1], axis=0),
                                     in_=tl(x3T, t), in_offset=None).then_inc(scattered, 16)
            g.wait_ge(spare_stored, 16)
            for b in range(4):
                g.wait_ge(eo_stored[b], 32 * (E1 // 4))
            for t in range(NT):
                g.indirect_dma_start(out=tl(combT, t), out_offset=None, in_=eout[:, :],
                                     in_offset=bass.IndirectOffsetOnAxis(ap=dest[:, t:t + 1], axis=0)).then_inc(gathered[t // TC], 16)
            refine(N_LN4, NC - 2)


_INS = [
    "L0_attn_x", "L0_attn_W_in", "L0_attn_b_in", "L0_attn_W_xp", "L0_attn_b_xp", "L0_attn_W_dt", "L0_attn_b_dt",
    "L0_attn_W_out", "L0_attn_b_out", "L0_attn_A_log", "L0_attn_D", "L0_ffn_Wq", "L0_ffn_Wk_c", "L0_ffn_Wv_c",
    "L0_ffn_Wk", "L0_ffn_Wv", "L0_ffn_Wo", "L0_ffn_W_shared_in", "L0_ffn_W_shared_out", "L0_ffn_W1_shared",
    "L0_ffn_W2_experts", "L0_ffn_Wg_gate", "L0_ffn_We_gate", "L0_ffn_group_bias", "L0_ffn_expert_bias",
    "L0_ffn_norm1_w", "L0_ffn_norm2_w", "L1_attn_gamma", "L1_attn_wq", "L1_attn_wk", "L1_attn_wv", "L1_attn_wa",
    "L1_attn_wg", "L1_attn_wo", "L1_ffn_Wr", "L1_ffn_W1", "L1_ffn_W2",
]


def kernel(**inputs):
    import numpy as np
    import concourse.bacc as bacc
    from concourse.bass_utils import run_bass_kernel_spmd as run

    nc = bacc.Bacc("TRN2", target_bir_lowering=False, num_devices=1)
    arrays, args = {}, {}
    for name in _INS:
        arrays[f"in_{name}"] = np.ascontiguousarray(inputs[name])
    inv_freq = np.float32(1.0) / np.float32(10000.0) ** (np.arange(0, DH, 2, dtype=np.float32) / np.float32(DH))
    angle = np.repeat(inv_freq.astype(np.float32), 2)[:, None] * np.arange(S, dtype=np.float32)[None, :]
    angle = np.tile(angle.astype(np.float32), (H, 1))
    arrays["in_cos"], arrays["in_sin"] = np.cos(angle), np.sin(angle)
    for name, array in arrays.items():
        args[name[3:]] = nc.dram_tensor(name, array.shape, mybir.dt.from_np(array.dtype), kind="ExternalInput").ap()
    out = nc.dram_tensor("out_0", (1, S, D), F32, kind="ExternalOutput").ap()
    scratch = (
        nc.dram_tensor("q_split", (3, P, S), BF16).ap(),
        nc.dram_tensor("k_split", (H, 3, DH, S), BF16).ap(),
        nc.dram_tensor("attn_out", (H, 2, P, CH), F32).ap(),
        nc.dram_tensor("disp", (SLOTS + S, D), F32).ap(),
        nc.dram_tensor("eout", (SLOTS + S, D), F32).ap(),
    )
    build(nc, args, scratch, out)
    r = run(nc, [arrays], core_ids=[0])
    return r.results[0]["out_0"]
```
